# Optimizing a Trainium2 kernel written in Bass

```python
import numpy as np
import jax
import jax.numpy as jnp

def _softmax(x, axis=-1):
    return jax.nn.softmax(x, axis=axis)

def _gelu(x):
    return jax.nn.gelu(x, approximate=True)

def _silu(x):
    return jax.nn.silu(x)

def _sigmoid(x):
    return jax.nn.sigmoid(x)

def _layernorm(x, axis=-1, eps=1e-05):
    m = jnp.mean(x, axis=axis, keepdims=True)
    v = jnp.var(x, axis=axis, keepdims=True)
    return (x - m) / jnp.sqrt(v + eps)

def _scatter_add(tgt, idx, src, axis=0):
    return tgt.at[idx].add(src)

def _segment_sum(src, seg, n):
    return jax.ops.segment_sum(src, seg, n)
kernel_name = 'mk_adj_resnorm_d2_adj_r2_ea5839'

def setup_inputs(seed: int=0):
    np.random.seed(seed)
    _w = jnp.asarray

    def _rec_inputs():
        import jax
        import jax.numpy as jnp
        _gk = jax.random.key(seed)
        x = -0.0005207 + 1.001 * jax.random.normal(jax.random.fold_in(_gk, 1), (8192, 128), jnp.float32)
        _w = (1.0 + jnp.arange(8192, dtype=jnp.float32)) ** (-0.5)
        _w = _w / _w.mean()
        _pij = jnp.clip(0.000244141 * _w[:, None] * _w[None, :], 0.0, 1.0)
        _a = jax.random.uniform(jax.random.fold_in(_gk, 2), (8192, 8192)) < _pij
        _a = jnp.logical_or(_a, jnp.eye(8192, dtype=bool))
        _af = _a.astype(jnp.float32)
        _af = _af * jax.random.uniform(jax.random.fold_in(_gk, 3), (8192, 8192), jnp.float32, 0.05, 1)
        adj = _af
        return (x, adj)
    x, adj = _rec_inputs()

    def _L0_gnn_setup():
        import jax, jax.numpy as jnp
        import numpy as np
        N = 4096
        DIM = 128
        HEADS = 4
        HD = DIM // HEADS
        SCALE = HD ** (-0.5)
        key = jax.random.key(seed)
        ks = jax.random.split(key, 8)
        x = jax.random.normal(ks[0], (N, DIM), dtype=jnp.float32)
        adj_matrix = jax.random.uniform(ks[1], (N, N), dtype=jnp.float32)
        attn_mask = jax.random.randint(ks[2], (N, N), 0, 2, dtype=jnp.int32)
        Wqkv = jax.random.normal(ks[3], (DIM, 3 * DIM), dtype=jnp.float32) * DIM ** (-0.5)
        bqkv = jnp.zeros((3 * DIM,), dtype=jnp.float32)
        Wout = jax.random.normal(ks[4], (DIM, DIM), dtype=jnp.float32) * DIM ** (-0.5)
        bout = jnp.zeros((DIM,), dtype=jnp.float32)
        graph_bias = jax.random.normal(ks[5], (1, 1, 1), dtype=jnp.float32) * 0.1
        return {'x': x, 'adj_matrix': adj_matrix, 'attn_mask': attn_mask, 'Wqkv': Wqkv, 'bqkv': bqkv, 'Wout': Wout, 'bout': bout, 'graph_bias': graph_bias}
    _L0_gnn_all = _L0_gnn_setup()
    _L0_gnn_in = {k: v for k, v in _L0_gnn_all.items() if k in ('Wqkv', 'bqkv', 'Wout', 'bout', 'graph_bias')}
    del _L0_gnn_all

    def _L1_gnn_setup():
        import jax, jax.numpy as jnp
        import numpy as np
        N = 4096
        D = 128
        CUTOFF = 1.0
        MU = 1.0
        SIGMA = 0.5

        def sensitivity(r, mu, sigma):
            return jnp.exp(-(1.0 / r - 1.0 / mu) ** 2 / (2.0 * sigma * sigma))
        key = jax.random.key(seed)
        k_z, k_d, k_w = jax.random.split(key, 3)
        z = jax.random.normal(k_z, (N, D), dtype=jnp.float32)
        dist_matrix = jax.random.uniform(k_d, (N, N), dtype=jnp.float32) * 2.0 + 0.05
        W = jax.random.normal(k_w, (D, D), dtype=jnp.float32)
        B = jnp.zeros((D,), dtype=jnp.float32)
        return {'z': z, 'dist_matrix': dist_matrix, 'W': W, 'B': B}
    _L1_gnn_all = _L1_gnn_setup()
    _L1_gnn_in = {k: v for k, v in _L1_gnn_all.items() if k in ('W', 'B')}
    del _L1_gnn_all
    return {'x': x, 'adj': adj, 'L0_gnn_Wqkv': _L0_gnn_in['Wqkv'], 'L0_gnn_bqkv': _L0_gnn_in['bqkv'], 'L0_gnn_Wout': _L0_gnn_in['Wout'], 'L0_gnn_bout': _L0_gnn_in['bout'], 'L0_gnn_graph_bias': _L0_gnn_in['graph_bias'], 'L1_gnn_W': _L1_gnn_in['W'], 'L1_gnn_B': _L1_gnn_in['B']}

def reference(x, adj, L0_gnn_Wqkv, L0_gnn_bqkv, L0_gnn_Wout, L0_gnn_bout, L0_gnn_graph_bias, L1_gnn_W, L1_gnn_B):
    import jax
    import jax.numpy as jnp

    def _L0_gnn_ref(x, adj_matrix, attn_mask, Wqkv, bqkv, Wout, bout, graph_bias):
        import jax, jax.numpy as jnp
        import numpy as np
        N = 4096
        DIM = 128
        HEADS = 4
        HD = DIM // HEADS
        SCALE = HD ** (-0.5)
        n, d = x.shape
        qkv = x @ Wqkv + bqkv
        q, k, v = jnp.split(qkv, 3, axis=-1)

        def split_heads(t):
            return t.reshape(n, HEADS, HD).transpose(1, 0, 2)
        qh, kh, vh = (split_heads(q), split_heads(k), split_heads(v))
        scores = jnp.einsum('hnd,hmd->hnm', qh, kh) * SCALE
        scores = scores + graph_bias * adj_matrix[None, :, :]
        scores = jnp.where(attn_mask[None, :, :] == 0, jnp.float32(-1000000000.0), scores)
        attn = jax.nn.softmax(scores, axis=-1)
        out = jnp.einsum('hnm,hmd->hnd', attn, vh)
        out = out.transpose(1, 0, 2).reshape(n, d)
        return out @ Wout + bout

    def _L1_gnn_ref(z, dist_matrix, W, B):
        import jax, jax.numpy as jnp
        import numpy as np
        N = 4096
        D = 128
        CUTOFF = 1.0
        MU = 1.0
        SIGMA = 0.5

        def sensitivity(r, mu, sigma):
            return jnp.exp(-(1.0 / r - 1.0 / mu) ** 2 / (2.0 * sigma * sigma))
        msg = z @ W + B
        sens = sensitivity(dist_matrix, MU, SIGMA)
        weights = jnp.where(dist_matrix < CUTOFF, sens, 0.0)
        return weights @ msg
    x = _layernorm(x + _L0_gnn_ref(x, adj, adj, L0_gnn_Wqkv, L0_gnn_bqkv, L0_gnn_Wout, L0_gnn_bout, L0_gnn_graph_bias), axis=-1)
    x = _layernorm(x + _L1_gnn_ref(x, adj, L1_gnn_W, L1_gnn_B), axis=-1)
    return x

_drawn_inputs = setup_inputs


def setup_inputs(seed=0):
    import zlib

    import numpy as np

    out = dict(_drawn_inputs(seed))
    spreads = {'L0_gnn_bqkv': (0.0, 0.1), 'L0_gnn_bout': (0.0, 0.1), 'L1_gnn_B': (0.0, 0.738)}
    factors = {}
    for name, (base, spread) in spreads.items():
        noise = np.random.default_rng([zlib.crc32(name.encode()), seed]).standard_normal(out[name].shape)
        drawn = base * np.exp(spread * noise) if base else spread * noise
        out[name] = jnp.asarray(drawn.astype(out[name].dtype))
    for name, factor in factors.items():
        out[name] = (out[name] * factor).astype(out[name].dtype)
    return out
```

```python
from contextlib import ExitStack, contextmanager

import concourse.bass as bass
from concourse import mybir

ALU = mybir.AluOpType
ACT = mybir.ActivationFunctionType
BF16 = mybir.dt.bfloat16
F32 = mybir.dt.float32
U32 = mybir.dt.uint32
AX_X = mybir.AxisListType.X

P = 128
N = 8192
D = 128
HEADS = 4
HD = D // HEADS
SCALE = float(HD) ** -0.5
EPS = 1e-5
MASKED = -1e9
SIGMA = 0.5

TILES = (N - P) // P
BLOCKS = 16
FOLD = N // BLOCKS
QUARTERS = 4
QW = N // QUARTERS
SLOTS = 16
GROUPS = 3
EDGES = GROUPS * P
EXPONENT = 0x7F800000


BEGIN = ("max_first", "sum_first", "out_first", "clear_q", "turn_q", "copy_q0", "copy_q1", "copy_q2", "copy_q3")
BLOCK = ("turn_k", "copy_k", "scores", "bias", "scale", "present", "mask", "penalty", "penalize", "block_max", "new_max",
         "fall", "fall_exp", "shift", "exp", "sum", "scale_sum", "add_sum", "scale_out", "keep_max", "turn_p", "copy_p",
         "weigh", "add_out")
FINISH = ("rden", "att", "turn_att", "copy_att", "project", "add_x", "add_b", "stats", "aggr", "ln", "r0",
          "n1", "n2", "n3", "n4", "x1", "turn_x1", "copy_x1", "message", "add_bm", "keep")
BLOCK_2 = ("zero", "fill", "recip", "minus", "square", "exp", "below", "weight", "turn_w", "copy_w", "weigh", "add")
FINISH_2 = ("stats", "aggr", "ln", "r0", "n1", "n2", "n3", "n4", "out")
DENSE_1 = len(BEGIN) + (N // P) * len(BLOCK) + len(FINISH)
DENSE_2 = 1 + (N // P) * len(BLOCK_2) + len(FINISH_2)
LOADS_1 = 16 * (2 + 2 * (N // P))
LOADS_2 = 16 * 2 * (N // P)


class Dense:

    def __init__(self, adj_, x_, q_, msg_, out_, z_index, turns, loads, stores):
        self.adj, self.x, self.q, self.msg, self.out, self.z_index = adj_, x_, q_, msg_, out_, z_index
        self.turns, self.loads, self.stores = turns, loads, stores


class Tile:

    def __init__(self, pair, n):
        self.pair, self.n = pair, n
        self.parity = n % 2

    def affine(self, per_tile, plus):
        c = self.n * per_tile + plus
        return c if self.pair is None else self.pair * (2 * per_tile) + c

    def index(self):
        return self.affine(1, 0)

    def of_parity(self, per_tile, plus):
        c = (self.n // 2) * per_tile + plus
        return c if self.pair is None else self.pair * per_tile + c

    def at_least(self, n):
        return self.pair is not None or self.n >= n


def build(nc, x, adj, w_qkv, b_qkv, w_out, b_out, graph_bias, w_msg, b_msg, out):
    q_dram = nc.dram_tensor("q_table", (N, D), F32, kind="Internal").ap()
    kv_dram = nc.dram_tensor("kv_table", (N, 2 * D), F32, kind="Internal").ap()
    msg_dram = nc.dram_tensor("msg_table", (N, D), F32, kind="Internal").ap()
    adj_flat = adj.rearrange("a (b c) -> (a b) c", c=1)

    def rows(dram):
        return dram[P:N, :].rearrange("(p t) d -> t p d", t=TILES)

    adj_rows, x_rows, q_rows, kv_rows, msg_rows, out_rows = map(rows, (adj, x, q_dram, kv_dram, msg_dram, out))

    with ExitStack() as ctx:
        def sb(name, shape, dt=F32):
            return ctx.enter_context(nc.sbuf_tensor(name, shape, dt))

        def bank(name):
            return ctx.enter_context(nc.psum_tensor(name, [P, 512], F32))

        def sem(name):
            return ctx.enter_context(nc.semaphore(name))

        ident = sb("ident", [P, P])
        power = sb("power", [P, BLOCKS, P], BF16)
        before = sb("before", [P, P])
        edge_no = sb("edge_no", [P, EDGES])
        row_no = sb("row_no", [P, P])
        slot_no = sb("slot_no", [P, GROUPS, SLOTS])
        edge_col = sb("edge_col", [P, GROUPS])
        own_col = sb("own_col", [P, TILES])
        ones = sb("ones", [P, P])
        row_first = sb("row_first", [P, TILES])
        epsc = sb("epsc", [P, 1])
        w_qkv_sb = sb("w_qkv_sb", [P, 3 * D])
        b_qkv_sb = sb("b_qkv_sb", [P, 3 * D])
        w_out_sb = sb("w_out_sb", [P, D])
        b_out_sb = sb("b_out_sb", [P, D])
        w_msg_sb = sb("w_msg_sb", [P, D])
        b_msg_sb = sb("b_msg_sb", [P, D])
        gb = sb("gb", [P, 1])
        diag_adj = sb("diag_adj", [P, TILES])
        neg_gb_diag = sb("neg_gb_diag", [P, TILES])
        diag_w = sb("diag_w", [P, TILES])
        wtmp = sb("wtmp", [P, TILES * GROUPS])
        wtmp2 = sb("wtmp2", [P, TILES * GROUPS])
        row_of = sb("row_of", [P, TILES, GROUPS])
        edge_adj = sb("edge_adj", [P, TILES, GROUPS])
        edge_w = sb("edge_w", [P, TILES, GROUPS])
        cols_all = sb("cols_all", [P, TILES, GROUPS], U32)
        ends = sb("ends", [P, TILES])
        found = sb("found", [P, TILES])
        left = sb("left", [P, TILES])
        last_code = sb("last_code", [P, TILES])
        z = sb("z", [P, TILES + 1, D])
        a_ring = sb("a_ring", [P, 2, N])
        present = sb("present", [P, QUARTERS, QW], BF16)
        code_left = sb("code_left", [P, FOLD])
        c8 = sb("c8", [P, SLOTS])
        m8 = sb("m8", [P, SLOTS], U32)
        bits = sb("bits", [P, 2, SLOTS], U32)
        rest = sb("rest", [P, SLOTS])
        rest2 = sb("rest2", [P, SLOTS])
        expo = sb("expo", [P, 2, SLOTS], U32)
        key = sb("key", [P, 2, SLOTS])
        cand = sb("cand", [P, 2, SLOTS])
        cand_left = sb("cand_left", [P, 2, SLOTS])
        taken = sb("taken", [P, 2, SLOTS])
        count = sb("count", [P, 2, 1])
        rowinfo = sb("rowinfo", [P, 2, SLOTS + 2])
        starts = sb("starts", [P, EDGES])
        member = sb("member", [P, 2, EDGES])
        slot = sb("slot", [P, GROUPS])
        is_slot = sb("is_slot", [P, 2, GROUPS, SLOTS])
        picked = sb("picked", [P, GROUPS, SLOTS])
        keys = sb("keys", [P, GROUPS])
        row_u = sb("row_u", [P, GROUPS], U32)
        row_sh = sb("row_sh", [P, GROUPS], U32)
        cols = sb("cols", [P, 2, GROUPS], U32)
        flat = sb("flat", [P, 2, GROUPS], U32)
        empty = sb("empty", [P, 2, SLOTS])
        q_own = sb("q_own", [P, 2, D])
        k_own = sb("k_own", [P, 2, D])
        v_own = sb("v_own", [P, 2, D])
        x_own = sb("x_own", [P, 2, D])
        kv_edge = sb("kv_edge", [P, 2, GROUPS, 2 * D])
        adj_edge = sb("adj_edge", [P, 2, GROUPS])
        diag_prod = sb("diag_prod", [P, D])
        diag_sum = sb("diag_sum", [P, HEADS])
        neg_diag = sb("neg_diag", [P, 2, HEADS])
        prod = sb("prod", [P, GROUPS, D])
        psum_ = sb("psum_", [P, GROUPS, HEADS])
        pen = sb("pen", [P, GROUPS])
        bias = sb("bias", [P, GROUPS])
        score = sb("score", [P, GROUPS, HEADS])
        by_slot = sb("by_slot", [P, GROUPS, HEADS, SLOTS])
        member_t = sb("member_t", [P, GROUPS, P])
        slotted = sb("slotted", [P, HEADS, SLOTS])
        rowmax = sb("rowmax", [P, HEADS])
        neg_max = sb("neg_max", [P, HEADS])
        shifted = sb("shifted", [P, GROUPS, HEADS])
        shifted_d = sb("shifted_d", [P, HEADS])
        weighted = sb("weighted", [P, GROUPS, D + HEADS])
        prob_d = sb("prob_d", [P, 2, HEADS])
        pv_d = sb("pv_d", [P, D])
        resid = sb("resid", [P, D])
        num = sb("num", [P, D])
        den = sb("den", [P, HEADS])
        rden = sb("rden", [P, HEADS])
        att = sb("att", [P, D])
        att_t = sb("att_t", [P, D])
        y = sb("y", [P, D])
        stats = sb("stats", [P, 6])
        mv = sb("mv", [P, 2])
        lnv = sb("lnv", [P, 1])
        r0 = sb("r0", [P, 1])
        t1 = sb("t1", [P, 1])
        t2 = sb("t2", [P, 1])
        rstd = sb("rstd", [P, 1])
        x1 = sb("x1", [P, D])
        x1_t = sb("x1_t", [P, D])
        msg = sb("msg", [P, 2, D])
        qkv = sb("qkv", [P, 2, 4, 3 * D])
        x_t = sb("x_t", [P, 2, P])
        msg_edge = sb("msg_edge", [P, 2, GROUPS, D])
        cols2 = sb("cols2", [P, 2, GROUPS], U32)
        memw = sb("memw", [P, 2, GROUPS, P])
        y2 = sb("y2", [P, 2, D])

        d_adj = sb("d_adj", [P, P])
        d_kv = sb("d_kv", [P, 2 * D])
        d_q = sb("d_q", [P, D])
        d_x = sb("d_x", [P, D])
        d_qh = sb("d_qh", [P, HEADS, P])
        d_kt = sb("d_kt", [P, P])
        d_s = sb("d_s", [P, HEADS, P])
        d_pt = sb("d_pt", [P, HEADS, P])
        d_bias = sb("d_bias", [P, P])
        d_on = sb("d_on", [P, P])
        d_pen = sb("d_pen", [P, P])
        d_max = sb("d_max", [P, HEADS])
        d_new = sb("d_new", [P, HEADS])
        d_fall = sb("d_fall", [P, HEADS])
        d_sum = sb("d_sum", [P, HEADS])
        d_part = sb("d_part", [P, HEADS])
        d_out = sb("d_out", [P, D])
        d_msg = sb("d_msg", [P, D])
        row_flags = sb("row_flags", [P, TILES])
        flag_part = sb("flag_part", [P, TILES])
        flags = sb("flags", [P, TILES + 1], U32)

        code = [bank("code0"), bank("code1")]
        b_edge = bank("b_edge")
        q_edge = [bank("q_edge0"), bank("q_edge1")]
        b_max = bank("b_max")
        b_sum = bank("b_sum")
        b_fin = bank("b_fin")
        info_e = b_edge[:, 16:16 + GROUPS * (SLOTS + 2)].rearrange("p (g s) -> p g s", g=GROUPS)
        first_ps = b_edge[:, 0:1]
        slot_ps = b_max[:, 0:HEADS * SLOTS]
        max_ps = b_max[:, 128:128 + GROUPS * HEADS]
        att_ps, proj_ps, x1_ps, msg_ps = (b_fin[:, n * P:(n + 1) * P] for n in range(4))

        s_const = sem("s_const")
        s_cstep = sem("s_cstep")
        s_loaded = sem("s_loaded")
        s_xall = sem("s_xall")
        s_powers = sem("s_powers")
        s_diag = sem("s_diag")
        s_diag2 = sem("s_diag2")
        s_xt = sem("s_xt")
        s_xtc = sem("s_xtc")
        s_qkv = sem("s_qkv")
        s_qkvb = sem("s_qkvb")
        s_stored = [sem("s_stored0"), sem("s_stored1")]
        s_adj = [[sem(f"s_adj{i}{h}") for h in range(2)] for i in range(2)]
        s_qk = [sem("s_qk0"), sem("s_qk1")]
        s_vx = [sem("s_vx0"), sem("s_vx1")]
        signed = sem("signed")
        folded = sem("folded")
        step = sem("step")
        code_free = sem("code_free")
        passed_dve = sem("passed_dve")
        passed_pool = sem("passed_pool")
        passed_sp = sem("passed_sp")
        counted = sem("counted")
        first_ready = sem("first_ready")
        member_ready = sem("member_ready")
        info_sent = sem("info_sent")
        q_sent = sem("q_sent")
        idx_ready = sem("idx_ready")
        s_kv = [sem("s_kv0"), sem("s_kv1")]
        s_val = [sem("s_val0"), sem("s_val1")]
        prod_d = sem("prod_d")
        q_read = sem("q_read")
        by_slot_ready = sem("by_slot_ready")
        slots_sent = sem("slots_sent")
        max_ready = sem("max_ready")
        max_sent = sem("max_sent")
        shift_ready = sem("shift_ready")
        exped = sem("exped")
        weighted_ready = sem("weighted_ready")
        summed = sem("summed")
        pool_fin = sem("pool_fin")
        pool_copy = sem("pool_copy")
        att_ready = sem("att_ready")
        att_turned = sem("att_turned")
        att_copied = sem("att_copied")
        projected = sem("projected")
        stats_ready = sem("stats_ready")
        rstd_step = sem("rstd_step")
        x1_ready = sem("x1_ready")
        x1_turned = sem("x1_turned")
        x1_copied = sem("x1_copied")
        msg_made = sem("msg_made")
        msg_ready = sem("msg_ready")
        s_msg = [sem("s_msg0"), sem("s_msg1")]
        w_squared = sem("w_squared")
        w_exped = sem("w_exped")
        l2_cols = sem("l2_cols")
        l2_in = [sem("l2_in0"), sem("l2_in1")]
        l2_memw = sem("l2_memw")
        l2_sum = sem("l2_sum")
        l2_y = sem("l2_y")
        l2_rstd = sem("l2_rstd")
        l2_out = sem("l2_out")
        s_out = [sem("s_out0"), sem("s_out1")]
        turn = sem("turn")
        d_loaded = sem("d_loaded")
        d_stored = sem("d_stored")
        flags_summed = sem("flags_summed")
        flags_ready = sem("flags_ready")

        HELD = 5
        LOOP_FROM, PAIRS = HELD, (TILES - HELD) // 2 - 1
        LAST = TILES + HELD - 1

        def active(it):
            return [Tile(it.pair, it.n - k) if it.pair is not None or 0 <= it.n - k < TILES else None
                    for k in range(HELD)]

        def iterations(eng, body):
            for i in range(LOOP_FROM):
                body(*active(Tile(None, i)))
            with eng.Fori(0, PAIRS) as pair:
                for u in range(2):
                    body(*active(Tile(pair, LOOP_FROM + u)))
            for i in range(LOOP_FROM + 2 * PAIRS, LAST):
                body(*active(Tile(None, i)))

        def before_step(eng, base, names, name):
            at = base + names.index(name)
            if not isinstance(at, int) or at > 0:
                eng.wait_ge(turn, at)

        def heads(ap):
            return ap.rearrange("p (h d) -> p h d", h=HEADS)

        first_tile = Dense(adj[0:P, :], x[0:P, :], q_dram[0:P, :], msg_dram[0:P, :], out[0:P, :], TILES, 0, 0, 0)
        first_tile_2 = Dense(adj[0:P, :], None, None, None, out[0:P, :], TILES,
                             DENSE_1 * (TILES + 1), LOADS_1 * (TILES + 1), 16 * (TILES + 1))

        def tile_1(t):
            return Dense(adj_rows[t], x_rows[t], q_rows[t], msg_rows[t], None, t, DENSE_1 * t + DENSE_1, LOADS_1 * t + LOADS_1, 16 * t + 16)

        def tile_2(t):
            return Dense(adj_rows[t], None, None, None, out_rows[t], t, DENSE_2 * t + (DENSE_1 * (TILES + 1) + DENSE_2),
                         LOADS_2 * t + (LOADS_1 * (TILES + 1) + LOADS_2), 16 * t + 16 * (TILES + 2))

        def messages_stored(eng):
            eng.wait_ge(s_msg[0], 16 * ((TILES + 1) // 2))
            eng.wait_ge(s_msg[1], 16 * (TILES // 2))
            eng.wait_ge(d_stored, 16)
            eng.wait_ge(flags_ready, 1)
            eng.wait_ge(d_stored, 16 * (TILES + 1))

        def flagged(eng, work, skip=None, skip_all=None):
            with eng.If(eng.value_load(flags[0:1, TILES:TILES + 1], min_val=0, max_val=N) > 0):
                with eng.Fori(0, TILES) as t:
                    with eng.If(eng.value_load(flags[0:1, bass.ds(t, 1)], min_val=0, max_val=N) > 0):
                        work(t)
                    if skip:
                        with eng.Else():
                            skip(t)
            if skip_all:
                with eng.Else():
                    skip_all()

        block = ctx.enter_context(nc.Block())
        NBLK = N // P

        @block.sync
        def _(sp):
            for dst, src in ((w_qkv_sb, w_qkv), (w_out_sb, w_out), (w_msg_sb, w_msg)):
                sp.dma_start(dst[:], src).then_inc(s_loaded, 16)
            for dst, src in ((b_qkv_sb, b_qkv), (b_out_sb, b_out), (b_msg_sb, b_msg)):
                sp.dma_start(dst[:], src.rearrange("(a n) -> a n", a=1).to_broadcast([P, src.shape[0]])).then_inc(s_loaded, 16)
            sp.dma_start(gb[:], graph_bias.rearrange("a b c -> (a b) c").to_broadcast([P, 1])).then_inc(s_loaded, 16)
            sp.dma_start(z[:, 0:NBLK, :], x.rearrange("(p b) d -> p b d", b=NBLK)).then_inc(s_xall, 16)

            def load_adj(t, h):
                sp.dma_start(a_ring[:, t.parity, h * (N // 2):(h + 1) * (N // 2)],
                             adj_rows[t.index()][:, h * (N // 2):(h + 1) * (N // 2)]).then_inc(s_adj[t.parity][h], 16)

            for i in range(2):
                for h in range(2):
                    load_adj(Tile(None, i), h)
            diagonal = bass.AP(tensor=adj.tensor, offset=P * (N + 1), ap=[[TILES * (N + 1), P], [N + 1, TILES]])
            with nc.allow_non_contiguous_dma(reason="one number of every row"):
                sp.dma_start(diag_adj[:], diagonal).then_inc(s_diag, 16)

            q_t = q_dram.rearrange("(p b) d -> p b d", b=NBLK)
            kv_t = kv_dram.rearrange("(p b) d -> p b d", b=NBLK)
            for g in range(NBLK // 4):
                sp.wait_ge(s_qkvb, 4 * g + 4)
                sp.dma_start(q_t[:, 4 * g:4 * g + 4, :], qkv[:, g % 2, :, 0:D]).then_inc(s_stored[g % 2], 16)
                sp.dma_start(kv_t[:, 4 * g:4 * g + 4, :], qkv[:, g % 2, :, D:3 * D]).then_inc(s_stored[g % 2], 16)
            sp.wait_ge(s_stored[0], 16 * NBLK // 4)
            sp.wait_ge(s_stored[1], 16 * NBLK // 4)

            def body(fold, scan, gather, attend, finish):
                if scan:
                    t = scan
                    if t.at_least(2):
                        sp.wait_ge(q_sent, t.affine(1, -1))
                        sp.wait_ge(prod_d, t.affine(1, -1))
                    sp.dma_start(q_own[:, t.parity, :], q_rows[t.index()]).then_inc(s_qk[t.parity], 16)
                    sp.dma_start(k_own[:, t.parity, :], kv_rows[t.index()][:, 0:D]).then_inc(s_qk[t.parity], 16)
                if attend:
                    t = attend
                    if t.at_least(2):
                        sp.wait_ge(pool_fin, t.affine(2, -2))
                    sp.dma_start(v_own[:, t.parity, :], kv_rows[t.index()][:, D:2 * D]).then_inc(s_vx[t.parity], 16)
                    sp.dma_start(x_own[:, t.parity, :], x_rows[t.index()]).then_inc(s_vx[t.parity], 16)
                if fold and fold.at_least(0) and not (fold.pair is None and fold.n + 2 >= TILES):
                    for h in range(2):
                        sp.wait_ge(signed, fold.affine(QUARTERS, 2 * h + 2))
                        load_adj(Tile(fold.pair, fold.n + 2), h)
                if finish and finish.at_least(1):
                    store_msg(Tile(finish.pair, finish.n - 1))

            def store_msg(t):
                sp.wait_ge(msg_ready, t.affine(1, 1))
                sp.dma_start(msg_rows[t.index()], msg[:, t.parity, :]).then_inc(s_msg[t.parity], 16)

            iterations(sp, body)
            store_msg(Tile(None, TILES - 1))

            def dense(d):
                sp.dma_start(d_q[:], d.q).then_inc(d_loaded, 16)
                sp.dma_start(d_x[:], d.x).then_inc(d_loaded, 16)
                with sp.Fori(0, NBLK) as b:
                    before_step(sp, d.turns + len(BEGIN) + b * len(BLOCK), BLOCK, "turn_k")
                    sp.dma_start(d_adj[:], d.adj[:, bass.ds(b * P, P)]).then_inc(d_loaded, 16)
                    sp.dma_start(d_kv[:], kv_dram[bass.ds(b * P, P), :]).then_inc(d_loaded, 16)
                sp.wait_ge(turn, d.turns + DENSE_1)
                sp.dma_start(d.msg, d_msg[:]).then_inc(d_stored, 16)
                sp.wait_ge(d_stored, d.stores + 16)
                sp.sem_inc(passed_sp, 1)

            def skip(t):
                d = tile_1(t)
                sp.wait_ge(turn, d.turns)
                sp.sem_inc(turn, DENSE_1)
                sp.sem_inc(d_loaded, LOADS_1)
                sp.sem_inc(d_stored, 16)

            def skip_all():
                sp.wait_ge(turn, DENSE_1)
                sp.sem_inc(turn, DENSE_1 * TILES)
                sp.sem_inc(d_loaded, LOADS_1 * TILES)
                sp.sem_inc(d_stored, 16 * TILES)

            dense(first_tile)
            sp.wait_ge(flags_ready, 1)
            sp.wait_ge(s_msg[0], 16 * ((TILES + 1) // 2))
            sp.wait_ge(s_msg[1], 16 * (TILES // 2))
            flagged(sp, lambda t: dense(tile_1(t)), skip, skip_all)

            def store_out(t):
                sp.wait_ge(l2_out, t.affine(1, 1))
                sp.dma_start(out_rows[t.index()], y2[:, t.parity, :]).then_inc(s_out[t.parity], 16)
            with sp.Fori(0, TILES // 2) as pair:
                for u in range(2):
                    store_out(Tile(pair, u))
            store_out(Tile(None, TILES - 1))
            sp.wait_ge(s_out[0], 16 * ((TILES + 1) // 2))
            sp.wait_ge(s_out[1], 16 * (TILES // 2))

            def dense2(d):
                with sp.Fori(0, NBLK) as b:
                    before_step(sp, d.turns + 1 + b * len(BLOCK_2), BLOCK_2, "zero")
                    sp.dma_start(d_adj[:], d.adj[:, bass.ds(b * P, P)]).then_inc(d_loaded, 16)
                    sp.dma_start(d_kv[:, 0:D], msg_dram[bass.ds(b * P, P), :]).then_inc(d_loaded, 16)
                sp.wait_ge(turn, d.turns + DENSE_2)
                sp.dma_start(d.out, d_msg[:]).then_inc(d_stored, 16)
                sp.wait_ge(d_stored, d.stores + 16)
                sp.sem_inc(passed_sp, 1)

            def skip2(t):
                d = tile_2(t)
                sp.wait_ge(turn, d.turns)
                sp.sem_inc(turn, DENSE_2)
                sp.sem_inc(d_loaded, LOADS_2)
                sp.sem_inc(d_stored, 16)

            messages_stored(sp)
            dense2(first_tile_2)
            flagged(sp, lambda t: dense2(tile_2(t)), skip2)

        @block.gpsimd
        def _(pool):
            done = [0]

            def const(ins):
                done[0] += 1
                ins.then_inc(s_cstep, 1)
                pool.wait_ge(s_cstep, done[0])

            const(nc.gpsimd.memset(ident[:], 0.0))
            const(nc.gpsimd.affine_select(out=ident[:], in_=ident[:], compare_op=ALU.not_equal, fill=1.0, base=0,
                                          pattern=[[-1, P]], channel_multiplier=1))
            const(nc.gpsimd.memset(before[:], 1.0))
            const(nc.gpsimd.affine_select(out=before[:], in_=before[:], compare_op=ALU.is_gt, fill=0.0, base=0,
                                          pattern=[[1, P]], channel_multiplier=-1))
            for dst, pattern, base, ch in ((edge_no[:], [[1, EDGES]], 1, 0), (row_no[:], [[1, P]], 1, 0),
                                           (slot_no[:], [[0, GROUPS], [1, SLOTS]], 0, 0), (edge_col[:], [[P, GROUPS]], 0, 1),
                                           (row_first[:], [[1, TILES]], P - TILES, 0),
                                           (own_col[:], [[1, TILES]], P + 1, TILES),
                                           (rowinfo[:, 0, SLOTS + 1:SLOTS + 2], [[1, 1]], 1, 1),
                                           (rowinfo[:, 1, SLOTS + 1:SLOTS + 2], [[1, 1]], 1, 1)):
                const(nc.gpsimd.iota(dst, pattern=pattern, base=base, channel_multiplier=ch, allow_small_or_imprecise_dtypes=True))
            const(nc.gpsimd.memset(ones[:], 1.0))
            nc.gpsimd.memset(epsc[:], EPS).then_inc(s_const, 1)
            pool.wait_ge(s_loaded, 16 * 7)

            def body(fold, scan, gather, attend, finish):
                if finish:
                    t = finish
                    pool.wait_ge(s_vx[t.parity], t.of_parity(32, 32))
                    if t.at_least(1):
                        pool.wait_ge(att_ready, t.affine(1, 0))
                        pool.wait_ge(stats_ready, t.affine(1, 0))
                    pool.wait_ge(exped, t.affine(2, 2))
                    nc.gpsimd.tensor_tensor(pv_d[:].rearrange("p (h d) -> p h d", h=HEADS),
                                            v_own[:, t.parity, :].rearrange("p (h d) -> p h d", h=HEADS),
                                            prob_d[:, t.parity, :].unsqueeze(2).to_broadcast([P, HEADS, HD]),
                                            ALU.mult).then_inc(pool_fin, 1)
                    nc.gpsimd.tensor_tensor(resid[:], x_own[:, t.parity, :], b_out_sb[:], ALU.add).then_inc(pool_fin, 1)
                if gather:
                    t = gather
                    pool.wait_ge(s_qk[t.parity], t.of_parity(32, 32))
                    if t.at_least(1):
                        pool.wait_ge(member_ready, t.affine(1, 0))
                    nc.gpsimd.tensor_tensor(diag_prod[:], q_own[:, t.parity, :], k_own[:, t.parity, :],
                                            ALU.mult).then_inc(prod_d, 1)
                    pool.wait_ge(idx_ready, t.affine(1, 1))
                    if t.at_least(2):
                        pool.wait_ge(weighted_ready, t.affine(1, -1))
                    pool.sem_inc(passed_pool, 1)
                    for g in range(GROUPS):
                        nc.gpsimd.indirect_dma_start(kv_edge[:, t.parity, g, :], None, kv_dram,
                                                     bass.IndirectOffsetOnAxis(ap=cols[:, t.parity, g:g + 1], axis=0)
                                                     ).then_inc(s_kv[t.parity], 16)
                        nc.gpsimd.indirect_dma_start(adj_edge[:, t.parity, g:g + 1], None, adj_flat,
                                                     bass.IndirectOffsetOnAxis(ap=flat[:, t.parity, g:g + 1], axis=0)
                                                     ).then_inc(s_val[t.parity], 16)
                    nc.gpsimd.tensor_copy(cols_all[:, t.index(), :], cols[:, t.parity, :]).then_inc(pool_copy, 1)

            iterations(pool, body)

            messages_stored(pool)

            def gather2(t):
                pool.wait_ge(l2_cols, t.affine(1, 1))
                if t.at_least(2):
                    pool.wait_ge(l2_sum, t.affine(1, -1))
                pool.sem_inc(passed_pool, 1)
                for g in range(GROUPS):
                    nc.gpsimd.indirect_dma_start(msg_edge[:, t.parity, g, :], None, msg_dram,
                                                 bass.IndirectOffsetOnAxis(ap=cols2[:, t.parity, g:g + 1], axis=0)
                                                 ).then_inc(l2_in[t.parity], 16)
            for i in range(2):
                gather2(Tile(None, i))
            with pool.Fori(0, (TILES - 3) // 2) as pair:
                for u in range(2):
                    gather2(Tile(pair, 2 + u))
            gather2(Tile(None, TILES - 1))

        @block.scalar
        def _(act):
            for b in range(NBLK):
                act.wait_ge(s_xt, b + 1)
                if b >= 2:
                    act.wait_ge(s_qkv, b - 1)
                nc.scalar.copy(x_t[:, b % 2, :], code[b % 2][:, 0:P]).then_inc(s_xtc, 1)

            def body(fold, scan, gather, attend, finish):
                def sign(q):
                    if not fold:
                        return
                    t = fold
                    if q % 2 == 0:
                        act.wait_ge(s_adj[t.parity][q // 2], t.of_parity(16, 16))
                    if t.at_least(1):
                        act.wait_ge(folded, t.affine(QUARTERS, q + 1 - QUARTERS))
                    nc.scalar.activation(present[:, q, :], a_ring[:, t.parity, q * QW:(q + 1) * QW].bitcast(U32),
                                         ACT.Sign).then_inc(signed, 1)

                sign(0)
                if finish:
                    t = finish
                    act.wait_ge(att_turned, t.affine(1, 1))
                    nc.scalar.copy(att_t[:], att_ps).then_inc(att_copied, 1)
                sign(1)
                if attend:
                    t = attend
                    act.wait_ge(shift_ready, t.affine(1, 1))
                    nc.scalar.activation(weighted[:, :, D:D + HEADS], shifted[:], ACT.Exp).then_inc(exped, 1)
                    nc.scalar.activation(prob_d[:, t.parity, :], shifted_d[:], ACT.Exp).then_inc(exped, 1)
                sign(2)
                if finish:
                    t = finish
                    rsqrt(stats_ready, t.affine(1, 1), rstd_step, t)
                sign(3)
                if finish:
                    t = finish
                    act.wait_ge(x1_turned, t.affine(1, 1))
                    nc.scalar.copy(x1_t[:], x1_ps).then_inc(x1_copied, 1)

            def rsqrt(ready, value, done, t):
                act.wait_ge(ready, value)
                nc.scalar.activation(lnv[:], mv[:, 1:2], ACT.Ln, bias=epsc[:]).then_inc(done, 1)
                act.wait_ge(done, t.affine(2, 1))
                nc.scalar.activation(r0[:], lnv[:], ACT.Exp, scale=-0.5).then_inc(done, 1)

            def weights_exp(dst, n):
                act.wait_ge(w_squared, n)
                nc.scalar.activation(dst, wtmp[:, 0:dst.shape[1]], ACT.Exp,
                                     scale=-1.0 / (2.0 * SIGMA * SIGMA)).then_inc(w_exped, 1)

            weights_exp(diag_w[:], 1)
            act.wait_ge(s_const, 1)
            iterations(act, body)

            def do(d_base, names, name, ins):
                before_step(act, d_base, names, name)
                ins().then_inc(turn, 1)

            def dense(d):
                for h in range(HEADS):
                    do(d.turns, BEGIN, f"copy_q{h}", lambda: nc.scalar.copy(d_qh[h * HD:(h + 1) * HD, h, :], code[0][h * HD:(h + 1) * HD, 0:P]))
                with act.Fori(0, NBLK) as b:
                    base = d.turns + len(BEGIN) + b * len(BLOCK)
                    do(base, BLOCK, "copy_k", lambda: nc.scalar.copy(d_kt[:], code[0][:, 0:P]))
                    do(base, BLOCK, "fall_exp", lambda: nc.scalar.activation(d_fall[:], d_fall[:], ACT.Exp))
                    do(base, BLOCK, "exp", lambda: nc.scalar.activation(d_s[:], d_s[:], ACT.Exp))
                    do(base, BLOCK, "copy_p", lambda: nc.scalar.copy(d_pt[:].rearrange("p h r -> p (h r)"), code[0][:]))
                base = d.turns + DENSE_1 - len(FINISH)
                do(base, FINISH, "copy_att", lambda: nc.scalar.copy(att_t[:], att_ps))
                do(base, FINISH, "ln", lambda: nc.scalar.activation(lnv[:], mv[:, 1:2], ACT.Ln, bias=epsc[:]))
                do(base, FINISH, "r0", lambda: nc.scalar.activation(r0[:], lnv[:], ACT.Exp, scale=-0.5))
                do(base, FINISH, "copy_x1", lambda: nc.scalar.copy(x1_t[:], x1_ps))

            dense(first_tile)
            act.wait_ge(flags_ready, 1)
            flagged(act, lambda t: dense(tile_1(t)))
            weights_exp(edge_w[:].rearrange("p t g -> p (t g)"), 2)

            def tile2(t):
                if t.at_least(2):
                    act.wait_ge(l2_in[t.parity], t.of_parity(16 * GROUPS, 0))
                nc.scalar.copy(cols2[:, t.parity, :], cols_all[:, t.index(), :]).then_inc(l2_cols, 1)
                if t.at_least(1):
                    prev(Tile(t.pair, t.n - 1))

            def prev(t):
                rsqrt(l2_y, t.affine(1, 1), l2_rstd, t)
            act.wait_ge(pool_copy, TILES)
            for i in range(2):
                tile2(Tile(None, i))
            with act.Fori(0, (TILES - 3) // 2) as pair:
                for u in range(2):
                    tile2(Tile(pair, 2 + u))
            tile2(Tile(None, TILES - 1))
            prev(Tile(None, TILES - 1))

            def dense2(d):
                with act.Fori(0, NBLK) as b:
                    base = d.turns + 1 + b * len(BLOCK_2)
                    do(base, BLOCK_2, "exp", lambda: nc.scalar.activation(d_on[:], d_on[:], ACT.Exp, scale=-1.0 / (2.0 * SIGMA * SIGMA)))
                    do(base, BLOCK_2, "copy_w", lambda: nc.scalar.copy(d_kt[:], b_max[:, 0:P]))
                base = d.turns + DENSE_2 - len(FINISH_2)
                do(base, FINISH_2, "ln", lambda: nc.scalar.activation(lnv[:], mv[:, 1:2], ACT.Ln, bias=epsc[:]))
                do(base, FINISH_2, "r0", lambda: nc.scalar.activation(r0[:], lnv[:], ACT.Exp, scale=-0.5))

            dense2(first_tile_2)
            flagged(act, lambda t: dense2(tile_2(t)))

        @block.tensor
        def _(pe):
            pe.wait_ge(s_const, 1)
            pe.wait_ge(s_loaded, 16 * 7)
            pe.wait_ge(s_xall, 16)

            def turn_x(b):
                if b >= 2:
                    pe.wait_ge(s_xtc, b - 1)
                nc.tensor.transpose(code[b % 2][:, 0:P], z[:, b, :], ident[:]).then_inc(s_xt, 1)

            turn_x(0)
            for b in range(NBLK):
                if b + 1 < NBLK:
                    turn_x(b + 1)
                pe.wait_ge(s_xtc, b + 1)
                if b >= 2:
                    pe.wait_ge(s_qkvb, b - 1)
                nc.tensor.matmul(q_edge[b % 2][:, 0:3 * D], x_t[:, b % 2, :], w_qkv_sb[:], start=True, stop=True).then_inc(s_qkv, 1)
            pe.wait_ge(s_qkvb, NBLK)
            pe.wait_ge(s_powers, 1)

            def body(fold, scan, gather, attend, finish):
                def fold_quarter(q):
                    if not fold:
                        return
                    t = fold
                    pe.wait_ge(signed, t.affine(QUARTERS, q + 1))
                    if q == 0 and t.at_least(2):
                        pe.wait_ge(code_free, t.affine(1, -1))
                    per = BLOCKS // QUARTERS
                    for b in range(q * per, (q + 1) * per):
                        last = nc.tensor.matmul(code[t.parity][:], power[:, b, :],
                                                present[:, q, (b % per) * FOLD:(b % per + 1) * FOLD],
                                                start=(b == 0), stop=(b == BLOCKS - 1))
                    last.then_inc(folded, 1)

                if finish:
                    t = finish
                    pe.wait_ge(att_ready, t.affine(1, 1))
                    if t.at_least(1):
                        pe.wait_ge(msg_ready, t.affine(1, 0))
                    nc.tensor.transpose(att_ps, att[:], ident[:]).then_inc(att_turned, 1)
                if gather:
                    t = gather
                    pe.wait_ge(counted, t.affine(1, 1))
                    if t.at_least(1):
                        pe.wait_ge(idx_ready, t.affine(1, 0))
                    nc.tensor.matmul(first_ps, before[:], count[:, t.parity, :], start=True, stop=True).then_inc(first_ready, 1)
                fold_quarter(0)
                if attend:
                    t = attend
                    pe.wait_ge(by_slot_ready, t.affine(1, 1))
                    for g in range(GROUPS):
                        last = nc.tensor.matmul(slot_ps, member_t[:, g, :], by_slot[:, g].rearrange("p h s -> p (h s)"),
                                                start=(g == 0), stop=(g == GROUPS - 1))
                    last.then_inc(slots_sent, 1)
                if finish:
                    t = finish
                    pe.wait_ge(att_copied, t.affine(1, 1))
                    nc.tensor.matmul(proj_ps, att_t[:], w_out_sb[:], start=True, stop=True).then_inc(projected, 1)
                if gather:
                    t = gather
                    pe.wait_ge(member_ready, t.affine(1, 1))
                    for g in range(GROUPS):
                        last = nc.tensor.matmul(info_e[:, g, :], member[:, t.parity, g * P:(g + 1) * P],
                                                rowinfo[:, t.parity, :], start=True, stop=True)
                    last.then_inc(info_sent, 1)
                    pe.wait_ge(s_qk[t.parity], t.of_parity(32, 32))
                    if t.at_least(2):
                        pe.wait_ge(q_read, t.affine(1, -1))
                    for g in range(GROUPS):
                        last = nc.tensor.matmul(q_edge[t.parity][:, g * D:(g + 1) * D], member[:, t.parity, g * P:(g + 1) * P],
                                                q_own[:, t.parity, :], start=True, stop=True)
                    last.then_inc(q_sent, 1)
                fold_quarter(1)
                if attend:
                    t = attend
                    pe.wait_ge(max_ready, t.affine(1, 1))
                    for g in range(GROUPS):
                        last = nc.tensor.matmul(max_ps[:, g * HEADS:(g + 1) * HEADS], member[:, t.parity, g * P:(g + 1) * P],
                                                neg_max[:], start=True, stop=True)
                    last.then_inc(max_sent, 1)
                fold_quarter(2)
                if finish:
                    t = finish
                    pe.wait_ge(x1_ready, t.affine(1, 1))
                    nc.tensor.transpose(x1_ps, x1[:], ident[:]).then_inc(x1_turned, 1)
                if attend:
                    t = attend
                    pe.wait_ge(weighted_ready, t.affine(1, 1))
                    if t.at_least(1):
                        pe.wait_ge(att_ready, t.affine(1, 0))
                    for g in range(GROUPS):
                        last = nc.tensor.matmul(b_sum[:, 0:D + HEADS], member_t[:, g, :], weighted[:, g, :],
                                                start=(g == 0), stop=(g == GROUPS - 1))
                    last.then_inc(summed, 1)
                fold_quarter(3)
                if finish:
                    t = finish
                    pe.wait_ge(x1_copied, t.affine(1, 1))
                    nc.tensor.matmul(msg_ps, x1_t[:], w_msg_sb[:], start=True, stop=True).then_inc(msg_made, 1)

            iterations(pe, body)

            def do(d_base, names, name, work):
                before_step(pe, d_base, names, name)
                work().then_inc(turn, 1)

            def turn_p():
                for h in range(HEADS):
                    last = nc.tensor.transpose(code[0][:, h * P:(h + 1) * P], d_s[:, h, :], ident[:])
                return last

            def scores():
                for h in range(HEADS):
                    last = nc.tensor.matmul(code[1][:, h * P:(h + 1) * P], d_qh[:, h, :], d_kt[:], start=True, stop=True)
                return last

            def weigh():
                for h in range(HEADS):
                    last = nc.tensor.matmul(b_sum[:, h * HD:(h + 1) * HD], d_pt[:, h, :], d_kv[:, D + h * HD:D + (h + 1) * HD],
                                            start=True, stop=True)
                return last

            def dense(d):
                pe.wait_ge(d_loaded, d.loads + 32)
                do(d.turns, BEGIN, "turn_q", lambda: nc.tensor.transpose(code[0][:, 0:P], d_q[:], ident[:]))
                with pe.Fori(0, NBLK) as b:
                    base = d.turns + len(BEGIN) + b * len(BLOCK)
                    pe.wait_ge(d_loaded, d.loads + 64 + b * 32)
                    do(base, BLOCK, "turn_k", lambda: nc.tensor.transpose(code[0][:, 0:P], d_kv[:, 0:D], ident[:]))
                    do(base, BLOCK, "scores", scores)
                    do(base, BLOCK, "turn_p", turn_p)
                    do(base, BLOCK, "weigh", weigh)
                base = d.turns + DENSE_1 - len(FINISH)
                do(base, FINISH, "turn_att", lambda: nc.tensor.transpose(att_ps, att[:], ident[:]))
                do(base, FINISH, "project", lambda: nc.tensor.matmul(proj_ps, att_t[:], w_out_sb[:], start=True, stop=True))
                do(base, FINISH, "turn_x1", lambda: nc.tensor.transpose(x1_ps, x1[:], ident[:]))
                do(base, FINISH, "message", lambda: nc.tensor.matmul(msg_ps, x1_t[:], w_msg_sb[:], start=True, stop=True))

            pe.wait_ge(msg_ready, TILES)
            dense(first_tile)
            pe.wait_ge(flags_summed, 1)
            nc.tensor.matmul(b_edge[:, 0:TILES], ones[:], row_flags[:], start=True, stop=True).then_inc(flags_summed, 1)
            pe.wait_ge(flags_ready, 1)
            flagged(pe, lambda t: dense(tile_1(t)))

            def sum2(t):
                pe.wait_ge(l2_in[t.parity], t.of_parity(16 * GROUPS, 16 * GROUPS))
                pe.wait_ge(l2_memw, t.affine(1, 1))
                if t.at_least(2):
                    pe.wait_ge(l2_y, t.affine(1, -1))
                for g in range(GROUPS):
                    last = nc.tensor.matmul(code[t.parity][:, 0:D], memw[:, t.parity, g, :], msg_edge[:, t.parity, g, :],
                                            start=(g == 0), stop=(g == GROUPS - 1))
                last.then_inc(l2_sum, 1)
            for i in range(2):
                sum2(Tile(None, i))
            with pe.Fori(0, (TILES - 3) // 2) as pair:
                for u in range(2):
                    sum2(Tile(pair, 2 + u))
            sum2(Tile(None, TILES - 1))

            def dense2(d):
                with pe.Fori(0, NBLK) as b:
                    base = d.turns + 1 + b * len(BLOCK_2)
                    do(base, BLOCK_2, "turn_w", lambda: nc.tensor.transpose(b_max[:, 0:P], d_on[:], ident[:]))
                    do(base, BLOCK_2, "weigh", lambda: nc.tensor.matmul(b_sum[:, 0:D], d_kt[:], d_kv[:, 0:D], start=True, stop=True))

            dense2(first_tile_2)
            flagged(pe, lambda t: dense2(tile_2(t)))

        @block.vector
        def _(dve):
            V = nc.vector
            STEPS = 52
            made = [0]
            pairing = [None]
            STEPS2 = 9
            history = []

            def run(ins, ready=None, value=None):
                if ready is None:
                    made[0] += 1
                    v = made[0] if pairing[0] is None else pairing[0][0] * pairing[0][1] + made[0]
                    ins.then_inc(step, 1)
                    history.append((step, v))
                else:
                    ins.then_inc(ready, 1)
                    history.append((ready, value))

            @contextmanager
            def counted_loop(count, steps):
                begun = made[0]
                with dve.Fori(0, count) as pair:
                    pairing[0] = (pair, steps)
                    history[:] = [(step, pair * steps + begun)] * 3
                    yield pair
                assert made[0] == begun + steps and history[-1][0] is step, (made[0] - begun, steps)
                pairing[0] = None
                made[0] = begun + count * steps
                history[:] = [(step, made[0])] * 3

            def unfused():
                dve.sem_inc(passed_dve, 1)

            def after(n=1):
                if len(history) >= n:
                    dve.wait_ge(*history[-n])

            dve.wait_ge(s_const, 1)
            for b in range(BLOCKS):
                run(V.tensor_scalar(power[:, b, :], ident[:], float(2 ** b), None, ALU.mult))
            after()
            run(V.memset(rest2[:], 0.0), s_powers, 1)
            dve.wait_ge(s_loaded, 16 * 7)
            for b in range(NBLK):
                g = b // 4
                dve.wait_ge(s_qkv, b + 1)
                if g >= 2 and b % 4 == 0:
                    dve.wait_ge(s_stored[g % 2], 32 * (g // 2))
                run(V.tensor_tensor(qkv[:, g % 2, b % 4, :], q_edge[b % 2][:, 0:3 * D], b_qkv_sb[:], ALU.add), s_qkvb, b + 1)

            def weights(dst, src, n):
                w, zero = wtmp[:, 0:src.shape[1]], wtmp2[:, 0:src.shape[1]]
                after()
                run(V.tensor_scalar(zero, src, 0.0, None, ALU.is_equal))
                after()
                run(V.tensor_tensor(w, src, zero, ALU.add))
                after()
                run(V.reciprocal(w, w))
                after()
                run(V.tensor_scalar(w, w, -1.0, None, ALU.add))
                after()
                run(V.tensor_tensor(w, w, w, ALU.mult), w_squared, n)
                after()
                run(V.scalar_tensor_tensor(zero, src, 1.0, zero, ALU.is_lt, ALU.subtract))
                dve.wait_ge(w_exped, n)
                after()
                run(V.tensor_tensor(dst, dst, zero, ALU.mult))

            def newton():
                run(V.tensor_tensor(t1[:], r0[:], r0[:], ALU.mult))
                after()
                run(V.scalar_tensor_tensor(t2[:], mv[:, 1:2], EPS, t1[:], ALU.add, ALU.mult))
                after()
                run(V.tensor_scalar(t1[:], t2[:], -0.5, 1.5, ALU.mult, ALU.add))
                after()
                run(V.tensor_tensor(rstd[:], t1[:], r0[:], ALU.mult))

            dve.wait_ge(s_diag, 16)
            run(V.tensor_scalar(neg_gb_diag[:], diag_adj[:], gb[:], -1.0, ALU.mult, ALU.mult))
            weights(diag_w[:], diag_adj[:], 1)

            def scan(t, part):
                ps = code[t.parity]
                if part == 0:
                    dve.wait_ge(folded, t.affine(QUARTERS, QUARTERS))
                    after()
                    unfused()
                    run(V.max(c8[:, 0:8], ps[:]))
                elif part == 1:
                    unfused()
                    run(V.max_index(m8[:, 0:8], c8[:, 0:8], ps[:]))
                elif part == 2:
                    unfused()
                    run(V.match_replace(code_left[:], c8[:, 0:8], ps[:], 0.0), code_free, t.affine(1, 1))
                elif part == 3:
                    unfused()
                    run(V.max(c8[:, 8:16], code_left[:]))
                elif part == 4:
                    unfused()
                    run(V.max_index(m8[:, 8:16], c8[:, 8:16], code_left[:]))
                elif part == 5:
                    run(V.tensor_scalar(bits[:, 0, :], c8[:].bitcast(U32), EXPONENT, None, ALU.bitwise_and))
                elif part == 6:
                    run(V.tensor_tensor(rest[:], c8[:], bits[:, 0, :].bitcast(F32), ALU.subtract))
                elif part == 7:
                    run(V.tensor_scalar(bits[:, 1, :], rest[:].bitcast(U32), EXPONENT, None, ALU.bitwise_and))
                elif part == 8:
                    run(V.tensor_scalar(expo[:], bits[:], 23 - 9, None, ALU.logical_shift_right))
                elif part == 9:
                    run(V.scalar_tensor_tensor(rest2[:], rest[:], 1.0, bits[:, 1, :].bitcast(F32), ALU.mult, ALU.subtract,
                                               accum_out=left[:, bass.ds(t.index(), 1)]))
                elif part == 10:
                    run(V.scalar_tensor_tensor(key[:], expo[:], float(1 - 127 * FOLD),
                                               m8[:].unsqueeze(1).to_broadcast([P, 2, SLOTS]), ALU.add, ALU.add))
                elif part == 11:
                    run(V.scalar_tensor_tensor(cand[:], bits[:].bitcast(F32), 0.0, key[:], ALU.is_gt, ALU.mult))
                elif part == 18:
                    run(V.scalar_tensor_tensor(cand[:], key[:], own_col[:, bass.ds(t.index(), 1)], cand[:], ALU.not_equal, ALU.mult))
                elif part == 12:
                    unfused()
                    run(V.max(rowinfo[:, t.parity, 0:8], cand[:].rearrange("p a s -> p (a s)")))
                elif part == 13:
                    run(V.tensor_scalar(taken[:], cand[:], 0.0, 0.0, ALU.is_gt, ALU.add, accum_out=found[:, bass.ds(t.index(), 1)]))
                elif part == 14:
                    unfused()
                    run(V.match_replace(cand_left[:].rearrange("p a s -> p (a s)"), rowinfo[:, t.parity, 0:8],
                                        cand[:].rearrange("p a s -> p (a s)"), 0.0))
                elif part == 15:
                    run(V.tensor_copy(last_code[:, bass.ds(t.index(), 1)], c8[:, SLOTS - 1:SLOTS]))
                elif part == 16:
                    unfused()
                    run(V.max(rowinfo[:, t.parity, 8:16], cand_left[:].rearrange("p a s -> p (a s)")))
                elif part == 17:
                    run(V.tensor_scalar(count[:, t.parity, :], found[:, bass.ds(t.index(), 1)], float(SLOTS), None, ALU.min),
                        counted, t.affine(1, 1))

            def gather_(t, part):
                info = rowinfo[:, t.parity, :]
                if part == 0:
                    dve.wait_ge(first_ready, t.affine(1, 1))
                    after()
                    run(V.tensor_copy(info[:, SLOTS:SLOTS + 1], first_ps))
                    run(V.tensor_tensor(ends[:, bass.ds(t.index(), 1)], first_ps, count[:, t.parity, :], ALU.add))
                elif part == 1:
                    run(V.tensor_scalar(starts[:], edge_no[:], info[:, SLOTS:SLOTS + 1], None, ALU.is_gt))
                elif part == 2:
                    dve.wait_ge(prod_d, t.affine(1, 1))
                    run(V.tensor_reduce(diag_sum[:], diag_prod[:].rearrange("p (h d) -> p h d", h=HEADS), AX_X, ALU.add))
                elif part == 3:
                    run(V.scalar_tensor_tensor(member[:, t.parity, :], edge_no[:], ends[:, bass.ds(t.index(), 1)], starts[:],
                                               ALU.is_le, ALU.mult), member_ready, t.affine(1, 1))
                elif part == 4:
                    run(V.tensor_scalar(neg_diag[:, t.parity, :], diag_sum[:], -SCALE, neg_gb_diag[:, bass.ds(t.index(), 1)],
                                        ALU.mult, ALU.add))
                elif part == 5:
                    run(V.tensor_scalar(empty[:, t.parity, :], info[:, 0:SLOTS], 0.0, MASKED, ALU.is_equal, ALU.mult))
                elif part == 6:
                    dve.wait_ge(info_sent, t.affine(1, 1))
                    run(V.tensor_tensor(slot[:], edge_col[:], info_e[:, :, SLOTS], ALU.subtract))
                elif part == 7:
                    run(V.tensor_copy(row_of[:, t.index(), :], info_e[:, :, SLOTS + 1]))
                elif part == 8:
                    run(V.tensor_tensor(is_slot[:, t.parity], slot_no[:], slot[:].unsqueeze(2).to_broadcast([P, GROUPS, SLOTS]),
                                        ALU.is_equal))
                elif part == 9:
                    run(V.tensor_scalar(row_u[:], row_of[:, t.index(), :], float(TILES), row_first[:, bass.ds(t.index(), 1)],
                                        ALU.mult, ALU.add))
                elif part == 10:
                    run(V.tensor_tensor(picked[:], is_slot[:, t.parity], info_e[:, :, 0:SLOTS], ALU.mult))
                elif part == 11:
                    run(V.tensor_scalar(row_sh[:], row_u[:], 13, None, ALU.logical_shift_left))
                elif part == 12:
                    run(V.tensor_reduce(keys[:], picked[:], AX_X, ALU.add))
                elif part == 13:
                    if t.at_least(2):
                        dve.wait_ge(pool_copy, t.affine(1, -1))
                    run(V.tensor_scalar(cols[:, t.parity, :], keys[:], -1.0, 0.0, ALU.add, ALU.max))
                elif part == 14:
                    run(V.tensor_tensor(flat[:, t.parity, :], row_sh[:], cols[:, t.parity, :], ALU.bitwise_or),
                        idx_ready, t.affine(1, 1))

            def attend_(t, part):
                if part == 0:
                    dve.wait_ge(s_kv[t.parity], t.of_parity(16 * GROUPS, 16 * GROUPS))
                    dve.wait_ge(q_sent, t.affine(1, 1))
                    run(V.tensor_tensor(prod[:], kv_edge[:, t.parity, :, 0:D],
                                        q_edge[t.parity][:, 0:GROUPS * D].rearrange("p (g d) -> p g d", g=GROUPS), ALU.mult),
                        q_read, t.affine(1, 1))
                elif part == 1:
                    dve.wait_ge(s_val[t.parity], t.of_parity(16 * GROUPS, 16 * GROUPS))
                    run(V.tensor_scalar(pen[:], adj_edge[:, t.parity, :], 0.0, MASKED, ALU.is_equal, ALU.mult))
                elif part == 2:
                    run(V.tensor_reduce(psum_[:].rearrange("p g h -> p (g h)"),
                                        prod[:].rearrange("p g (h d) -> p (g h) d", h=HEADS), AX_X, ALU.add))
                elif part == 3:
                    run(V.scalar_tensor_tensor(bias[:], adj_edge[:, t.parity, :], gb[:], pen[:], ALU.mult, ALU.add))
                elif part == 4:
                    run(V.tensor_copy(edge_adj[:, t.index(), :], adj_edge[:, t.parity, :]))
                elif part == 5:
                    run(V.scalar_tensor_tensor(score[:], psum_[:], SCALE, bias[:].unsqueeze(2).to_broadcast([P, GROUPS, HEADS]),
                                               ALU.mult, ALU.add))
                elif part in (6, 7, 8):
                    g = part - 6
                    run(V.tensor_scalar(member_t[:, g, :], row_no[:], row_of[:, t.index(), g:g + 1], None, ALU.is_equal))
                elif part == 9:
                    run(V.tensor_tensor(by_slot[:], is_slot[:, t.parity].unsqueeze(2).to_broadcast([P, GROUPS, HEADS, SLOTS]),
                                        score[:].unsqueeze(3).to_broadcast([P, GROUPS, HEADS, SLOTS]), ALU.mult),
                        by_slot_ready, t.affine(1, 1))
                elif part == 10:
                    dve.wait_ge(slots_sent, t.affine(1, 1))
                    run(V.tensor_tensor(slotted[:], slot_ps.rearrange("p (h s) -> p h s", h=HEADS),
                                        empty[:, t.parity, :].unsqueeze(1).to_broadcast([P, HEADS, SLOTS]), ALU.add))
                elif part == 11:
                    run(V.tensor_reduce(rowmax[:], slotted[:], AX_X, ALU.max))
                elif part == 12:
                    run(V.scalar_tensor_tensor(neg_max[:], rowmax[:], -1.0, neg_diag[:, t.parity, :], ALU.mult, ALU.min),
                        max_ready, t.affine(1, 1))
                elif part == 13:
                    run(V.tensor_tensor(shifted_d[:], neg_max[:], neg_diag[:, t.parity, :], ALU.subtract))
                elif part == 14:
                    dve.wait_ge(max_sent, t.affine(1, 1))
                    run(V.tensor_tensor(shifted[:].rearrange("p g h -> p (g h)"), score[:].rearrange("p g h -> p (g h)"), max_ps,
                                        ALU.add), shift_ready, t.affine(1, 1))
                elif part == 15:
                    dve.wait_ge(exped, t.affine(2, 1))
                    run(V.tensor_tensor(weighted[:, :, 0:D].rearrange("p g (h d) -> p g h d", h=HEADS),
                                        kv_edge[:, t.parity, :, D:2 * D].rearrange("p g (h d) -> p g h d", h=HEADS),
                                        weighted[:, :, D:D + HEADS].unsqueeze(3).to_broadcast([P, GROUPS, HEADS, HD]), ALU.mult),
                        weighted_ready, t.affine(1, 1))

            def finish_(t, part):
                if part == 0:
                    dve.wait_ge(summed, t.affine(1, 1))
                    dve.wait_ge(pool_fin, t.affine(2, 1))
                    run(V.tensor_tensor(den[:], b_sum[:, D:D + HEADS], prob_d[:, t.parity, :], ALU.add))
                elif part == 1:
                    run(V.tensor_tensor(num[:], b_sum[:, 0:D], pv_d[:], ALU.add))
                elif part == 2:
                    run(V.reciprocal(rden[:], den[:]))
                elif part == 3:
                    run(V.tensor_tensor(att[:].rearrange("p (h d) -> p h d", h=HEADS), num[:].rearrange("p (h d) -> p h d", h=HEADS),
                                        rden[:].unsqueeze(2).to_broadcast([P, HEADS, HD]), ALU.mult), att_ready, t.affine(1, 1))
                elif part == 4:
                    dve.wait_ge(projected, t.affine(1, 1))
                    dve.wait_ge(pool_fin, t.affine(2, 2))
                    run(V.tensor_tensor(y[:], proj_ps, resid[:], ALU.add))
                elif part == 5:
                    run(V.bn_stats(stats[:], y[:]))
                elif part == 6:
                    unfused()
                    run(V.bn_aggr(mv[:], stats[:]), stats_ready, t.affine(1, 1))
                elif part == 7:
                    dve.wait_ge(rstd_step, t.affine(2, 2))
                    run(V.tensor_tensor(t1[:], r0[:], r0[:], ALU.mult))
                elif part == 8:
                    run(V.scalar_tensor_tensor(t2[:], mv[:, 1:2], EPS, t1[:], ALU.add, ALU.mult))
                elif part == 9:
                    run(V.tensor_scalar(t1[:], t2[:], -0.5, 1.5, ALU.mult, ALU.add))
                elif part == 10:
                    run(V.tensor_tensor(rstd[:], t1[:], r0[:], ALU.mult))
                elif part == 11:
                    run(V.tensor_scalar(x1[:], y[:], mv[:, 0:1], rstd[:], ALU.subtract, ALU.mult), x1_ready, t.affine(1, 1))
                elif part == 12:
                    dve.wait_ge(msg_made, t.affine(1, 1))
                    if t.at_least(2):
                        dve.wait_ge(s_msg[t.parity], t.of_parity(16, 0))
                    run(V.tensor_tensor(msg[:, t.parity, :], msg_ps, b_msg_sb[:], ALU.add), msg_ready, t.affine(1, 1))
                elif part == 13:
                    run(V.scalar_tensor_tensor(z[:, t.index(), :], msg[:, t.parity, :], diag_w[:, bass.ds(t.index(), 1)], x1[:],
                                               ALU.mult, ALU.add))

            F, A, G, S = finish_, attend_, gather_, scan
            ORDER = [
                (F, 0, 1), (A, 0, 2), (F, 1, 2), (A, 1, 2), (F, 2, 3), (A, 2, 2), (F, 3, 2), (A, 3, 2), (G, 0, 2), (A, 4, 2), (G, 1, 3),
                (A, 5, 2), (G, 2, 2), (G, 3, 2), (A, 6, 2), (A, 7, 2), (A, 8, 2), (A, 9, 2), (G, 4, 2), (G, 5, 2),
                (S, 0, 1), (A, 10, 2), (S, 1, 2), (A, 11, 2), (A, 12, 1), (F, 4, 2), (A, 13, 2), (G, 6, 2), (F, 5, 2), (G, 7, 2), (F, 6, 2),
                (G, 8, 3), (A, 14, 2), (S, 2, 3), (G, 9, 2), (G, 10, 2), (G, 11, 2), (G, 12, 2), (F, 7, 2), (G, 13, 2), (F, 8, 2), (G, 14, 2),
                (F, 9, 2), (S, 3, 2), (F, 10, 2), (A, 15, 1), (F, 11, 2), (S, 4, 2), (S, 5, 2), (S, 6, 1), (S, 7, 1), (F, 12, 2), (S, 8, 2), (F, 13, 2),
                (S, 9, 2), (S, 10, 2), (S, 11, 1), (S, 18, 1), (S, 12, 1), (S, 13, 2), (S, 14, 2), (S, 17, 2), (S, 16, 2), (S, 15, 2)]

            def body(fold, scan_t, gather_t, attend_t, finish_t):
                tile = {S: scan_t, G: gather_t, A: attend_t, F: finish_t}
                whole = all(tile.values())
                for stage, part, back in ORDER:
                    if tile[stage]:
                        after(back if whole else 1)
                        stage(tile[stage], part)

            for i in range(LOOP_FROM):
                body(*active(Tile(None, i)))
            with counted_loop(PAIRS, 2 * STEPS) as pair:
                for u in range(2):
                    body(*active(Tile(pair, LOOP_FROM + u)))
            for i in range(LOOP_FROM + 2 * PAIRS, LAST):
                body(*active(Tile(None, i)))

            def do(d_base, names, name, ins):
                before_step(dve, d_base, names, name)
                ins().then_inc(turn, 1)

            def wide(ap, n=P):
                return ap.unsqueeze(2).to_broadcast([P, HEADS, n])

            def each_head(ap):
                return ap.unsqueeze(1).to_broadcast([P, HEADS, P])

            def newton_steps(base, names):
                do(base, names, "n1", lambda: V.tensor_tensor(t1[:], r0[:], r0[:], ALU.mult))
                do(base, names, "n2", lambda: V.scalar_tensor_tensor(t2[:], mv[:, 1:2], EPS, t1[:], ALU.add, ALU.mult))
                do(base, names, "n3", lambda: V.tensor_scalar(t1[:], t2[:], -0.5, 1.5, ALU.mult, ALU.add))
                do(base, names, "n4", lambda: V.tensor_tensor(rstd[:], t1[:], r0[:], ALU.mult))

            def aggregate(base, names):
                before_step(dve, base, names, "aggr")
                unfused()
                V.bn_aggr(mv[:], stats[:]).then_inc(turn, 1)

            def dense(d):
                do(d.turns, BEGIN, "max_first", lambda: V.memset(d_max[:], -3e38))
                do(d.turns, BEGIN, "sum_first", lambda: V.memset(d_sum[:], 0.0))
                do(d.turns, BEGIN, "out_first", lambda: V.memset(d_out[:], 0.0))
                do(d.turns, BEGIN, "clear_q", lambda: V.memset(d_qh[:], 0.0))
                with dve.Fori(0, NBLK) as b:
                    base = d.turns + len(BEGIN) + b * len(BLOCK)
                    do(base, BLOCK, "bias", lambda: V.tensor_scalar(d_bias[:], d_adj[:], gb[:], None, ALU.mult))
                    do(base, BLOCK, "scale", lambda: V.scalar_tensor_tensor(
                        d_s[:], code[1][:].rearrange("p (h r) -> p h r", h=HEADS), SCALE, each_head(d_bias[:]), ALU.mult, ALU.add))
                    do(base, BLOCK, "present", lambda: V.tensor_scalar(d_on[:], d_adj[:], 0.0, None, ALU.not_equal))
                    do(base, BLOCK, "mask", lambda: V.tensor_tensor(d_s[:], d_s[:], each_head(d_on[:]), ALU.mult))
                    do(base, BLOCK, "penalty", lambda: V.tensor_scalar(d_pen[:], d_on[:], -1.0, -MASKED, ALU.add, ALU.mult))
                    do(base, BLOCK, "penalize", lambda: V.tensor_tensor(d_s[:], d_s[:], each_head(d_pen[:]), ALU.add))
                    do(base, BLOCK, "block_max", lambda: V.tensor_reduce(d_new[:], d_s[:], AX_X, ALU.max))
                    do(base, BLOCK, "new_max", lambda: V.tensor_tensor(d_new[:], d_new[:], d_max[:], ALU.max))
                    do(base, BLOCK, "fall", lambda: V.tensor_tensor(d_fall[:], d_max[:], d_new[:], ALU.subtract))
                    do(base, BLOCK, "shift", lambda: V.tensor_tensor(d_s[:], d_s[:], wide(d_new[:]), ALU.subtract))
                    do(base, BLOCK, "sum", lambda: V.tensor_reduce(d_part[:], d_s[:], AX_X, ALU.add))
                    do(base, BLOCK, "scale_sum", lambda: V.tensor_tensor(d_sum[:], d_sum[:], d_fall[:], ALU.mult))
                    do(base, BLOCK, "add_sum", lambda: V.tensor_tensor(d_sum[:], d_sum[:], d_part[:], ALU.add))
                    do(base, BLOCK, "scale_out", lambda: V.tensor_tensor(heads(d_out[:]), heads(d_out[:]), wide(d_fall[:], HD), ALU.mult))
                    do(base, BLOCK, "keep_max", lambda: V.tensor_copy(d_max[:], d_new[:]))
                    do(base, BLOCK, "add_out", lambda: V.tensor_tensor(d_out[:], d_out[:], b_sum[:, 0:D], ALU.add))
                base = d.turns + DENSE_1 - len(FINISH)
                do(base, FINISH, "rden", lambda: V.reciprocal(rden[:], d_sum[:]))
                do(base, FINISH, "att", lambda: V.tensor_tensor(heads(att[:]), heads(d_out[:]), wide(rden[:], HD), ALU.mult))
                do(base, FINISH, "add_x", lambda: V.tensor_tensor(y[:], proj_ps, d_x[:], ALU.add))
                do(base, FINISH, "add_b", lambda: V.tensor_tensor(y[:], y[:], b_out_sb[:], ALU.add))
                do(base, FINISH, "stats", lambda: V.bn_stats(stats[:], y[:]))
                aggregate(base, FINISH)
                newton_steps(base, FINISH)
                do(base, FINISH, "x1", lambda: V.tensor_scalar(x1[:], y[:], mv[:, 0:1], rstd[:], ALU.subtract, ALU.mult))
                do(base, FINISH, "add_bm", lambda: V.tensor_tensor(d_msg[:], msg_ps, b_msg_sb[:], ALU.add))
                do(base, FINISH, "keep", lambda: V.tensor_copy(z[:, d.z_index, :], x1[:]))

            after()
            dense(first_tile)
            for n, (src, limit) in enumerate(((ends, EDGES), (found, SLOTS), (left, 0), (last_code, 0))):
                after()
                if n == 0:
                    run(V.tensor_scalar(row_flags[:], src[:], float(limit), None, ALU.is_gt))
                else:
                    run(V.scalar_tensor_tensor(row_flags[:], src[:], float(limit), row_flags[:], ALU.is_gt, ALU.add))
            after()
            run(V.scalar_tensor_tensor(row_flags[:], diag_adj[:], 0.0, row_flags[:], ALU.is_equal, ALU.add), flags_summed, 1)
            dve.wait_ge(flags_summed, 2)
            run(V.tensor_copy(flags[:, 0:TILES], b_edge[:, 0:TILES]))
            run(V.tensor_reduce(flag_part[:, 0:1], b_edge[:, 0:TILES], AX_X, ALU.add))
            after()
            run(V.tensor_copy(flags[:, TILES:TILES + 1], flag_part[:, 0:1]), flags_ready, 1)
            after()
            flagged(dve, lambda t: dense(tile_1(t)))
            run(V.memset(flag_part[:], 0.0))

            weights(edge_w[:].rearrange("p t g -> p (t g)"), edge_adj[:].rearrange("p t g -> p (t g)"), 2)

            def members(t):
                if t.at_least(2):
                    dve.wait_ge(l2_sum, t.affine(1, -1))
                for g in range(GROUPS):
                    after(2)
                    ins = V.tensor_scalar(memw[:, t.parity, g, :], row_no[:], row_of[:, t.index(), g:g + 1],
                                          edge_w[:, t.index(), g:g + 1], ALU.is_equal, ALU.mult)
                    if g < GROUPS - 1:
                        run(ins)
                    else:
                        run(ins, l2_memw, t.affine(1, 1))

            def rows2(t):
                dve.wait_ge(l2_sum, t.affine(1, 1))
                if t.at_least(2):
                    dve.wait_ge(s_out[t.parity], t.of_parity(16, 0))
                after()
                run(V.tensor_tensor(y[:], code[t.parity][:, 0:D], z[:, t.index(), :], ALU.add))
                after()
                run(V.bn_stats(stats[:], y[:]))
                after()
                unfused()
                run(V.bn_aggr(mv[:], stats[:]), l2_y, t.affine(1, 1))

            def norm2(t):
                dve.wait_ge(l2_rstd, t.affine(2, 2))
                newton()
                after()
                run(V.tensor_scalar(y2[:, t.parity, :], y[:], mv[:, 0:1], rstd[:], ALU.subtract, ALU.mult), l2_out, t.affine(1, 1))

            def tile2(t):
                rows2(t)
                if t.pair is not None or t.n + 1 < TILES:
                    members(Tile(t.pair, t.n + 1))
                norm2(t)

            after()
            members(Tile(None, 0))
            tile2(Tile(None, 0))
            after()
            run(V.tensor_copy(t1[:], r0[:]))
            with counted_loop((TILES - 1) // 2 - 1, 2 * STEPS2) as pair:
                for u in range(2):
                    tile2(Tile(pair, 1 + u))
                    after()
                    run(V.tensor_copy(t1[:], r0[:]))
            for i in range(TILES - 2, TILES):
                tile2(Tile(None, i))

            def dense2(d):
                dve.wait_ge(turn, d.turns)
                V.tensor_copy(y[:], z[:, d.z_index, :]).then_inc(turn, 1)
                with dve.Fori(0, NBLK) as b:
                    base = d.turns + 1 + b * len(BLOCK_2)
                    dve.wait_ge(d_loaded, d.loads + 32 + b * 32)
                    do(base, BLOCK_2, "zero", lambda: V.tensor_scalar(d_pen[:], d_adj[:], 0.0, None, ALU.is_equal))
                    do(base, BLOCK_2, "fill", lambda: V.tensor_tensor(d_on[:], d_adj[:], d_pen[:], ALU.add))
                    do(base, BLOCK_2, "recip", lambda: V.reciprocal(d_on[:], d_on[:]))
                    do(base, BLOCK_2, "minus", lambda: V.tensor_scalar(d_on[:], d_on[:], -1.0, None, ALU.add))
                    do(base, BLOCK_2, "square", lambda: V.tensor_tensor(d_on[:], d_on[:], d_on[:], ALU.mult))
                    do(base, BLOCK_2, "below", lambda: V.scalar_tensor_tensor(d_pen[:], d_adj[:], 1.0, d_pen[:], ALU.is_lt, ALU.subtract))
                    do(base, BLOCK_2, "weight", lambda: V.tensor_tensor(d_on[:], d_on[:], d_pen[:], ALU.mult))
                    do(base, BLOCK_2, "add", lambda: V.tensor_tensor(y[:], y[:], b_sum[:, 0:D], ALU.add))
                base = d.turns + DENSE_2 - len(FINISH_2)
                do(base, FINISH_2, "stats", lambda: V.bn_stats(stats[:], y[:]))
                aggregate(base, FINISH_2)
                newton_steps(base, FINISH_2)
                do(base, FINISH_2, "out", lambda: V.tensor_scalar(d_msg[:], y[:], mv[:, 0:1], rstd[:], ALU.subtract, ALU.mult))

            after()
            dense2(first_tile_2)
            flagged(dve, lambda t: dense2(tile_2(t)))

        return


_INS = ["x", "adj", "L0_gnn_Wqkv", "L0_gnn_bqkv", "L0_gnn_Wout", "L0_gnn_bout", "L0_gnn_graph_bias", "L1_gnn_W", "L1_gnn_B"]
_OUTS = [((N, D), "float32")]


def kernel(**inputs):
    import numpy as _np
    import concourse.bacc as _bacc
    from concourse import mybir as _mybir
    from concourse.bass_utils import run_bass_kernel_spmd as _run

    nc = _bacc.Bacc("TRN2", target_bir_lowering=False, num_devices=1)
    arrays, args = {}, []
    for name in _INS:
        a = _np.ascontiguousarray(inputs[name])
        arrays[f"in_{name}_dram"] = a
        args.append(nc.dram_tensor(f"in_{name}_dram", a.shape, _mybir.dt.from_np(a.dtype), kind="ExternalInput").ap())
    for i, (shape, dtype) in enumerate(_OUTS):
        dt = _mybir.dt.from_np(_np.dtype(dtype))
        args.append(nc.dram_tensor(f"out_{i}_dram", shape, dt, kind="ExternalOutput").ap())
    build(nc, *args)
    r = _run(nc, [arrays], core_ids=[0])
    return r.results[0]["out_0_dram"]
```

```python
from contextlib import ExitStack, contextmanager

import concourse.bass as bass
from concourse import mybir

ALU = mybir.AluOpType
ACT = mybir.ActivationFunctionType
BF16 = mybir.dt.bfloat16
F32 = mybir.dt.float32
U32 = mybir.dt.uint32
AX_X = mybir.AxisListType.X

P = 128
N = 8192
D = 128
HEADS = 4
HD = D // HEADS
SCALE = float(HD) ** -0.5
EPS = 1e-5
MASKED = -1e9
SIGMA = 0.5

TILES = (N - P) // P
BLOCKS = 16
FOLD = N // BLOCKS
QUARTERS = 4
QW = N // QUARTERS
SLOTS = 16
GROUPS = 3
EDGES = GROUPS * P
EXPONENT = 0x7F800000


CHUNKS = 4
DENSE_COLS = CHUNKS * P
DENSE_BLOCKS = N // DENSE_COLS
FINISH = ("rden", "att", "turn_att", "copy_att", "project", "add_x", "add_b", "stats", "aggr", "ln", "r0",
          "n1", "n2", "n3", "n4", "x1", "turn_x1", "copy_x1", "message", "add_bm", "keep")
FINISH_2 = ("stats", "aggr", "ln", "r0", "n1", "n2", "n3", "n4", "out")


class Dense:

    def __init__(self, no, z_index, turns, adj_, x_=None, q_=None, msg_=None, out_=None):
        self.no, self.z_index, self.turns = no, z_index, turns
        self.adj, self.x, self.q, self.msg, self.out = adj_, x_, q_, msg_, out_

    def count(self, b, per_block, plus):
        return (self.no * DENSE_BLOCKS + b) * per_block + plus


class Tile:

    def __init__(self, pair, n):
        self.pair, self.n = pair, n
        self.parity = n % 2

    def affine(self, per_tile, plus):
        c = self.n * per_tile + plus
        return c if self.pair is None else self.pair * (2 * per_tile) + c

    def index(self):
        return self.affine(1, 0)

    def of_parity(self, per_tile, plus):
        c = (self.n // 2) * per_tile + plus
        return c if self.pair is None else self.pair * per_tile + c

    def at_least(self, n):
        return self.pair is not None or self.n >= n


def build(nc, x, adj, w_qkv, b_qkv, w_out, b_out, graph_bias, w_msg, b_msg, out):
    q_dram = nc.dram_tensor("q_table", (N, D), F32, kind="Internal").ap()
    kv_dram = nc.dram_tensor("kv_table", (N, 2 * D), F32, kind="Internal").ap()
    msg_dram = nc.dram_tensor("msg_table", (N, D), F32, kind="Internal").ap()
    adj_flat = adj.rearrange("a (b c) -> (a b) c", c=1)

    def rows(dram):
        return dram[P:N, :].rearrange("(p t) d -> t p d", t=TILES)

    adj_rows, x_rows, q_rows, kv_rows, msg_rows, out_rows = map(rows, (adj, x, q_dram, kv_dram, msg_dram, out))

    with ExitStack() as ctx:
        def sb(name, shape, dt=F32):
            return ctx.enter_context(nc.sbuf_tensor(name, shape, dt))

        def bank(name):
            return ctx.enter_context(nc.psum_tensor(name, [P, 512], F32))

        def sem(name):
            return ctx.enter_context(nc.semaphore(name))

        ident = sb("ident", [P, P])
        power = sb("power", [P, BLOCKS, P], BF16)
        before = sb("before", [P, P])
        edge_no = sb("edge_no", [P, EDGES])
        row_no = sb("row_no", [P, P])
        slot_no = sb("slot_no", [P, GROUPS, SLOTS])
        edge_col = sb("edge_col", [P, GROUPS])
        own_col = sb("own_col", [P, TILES])
        ones = sb("ones", [P, P])
        row_first = sb("row_first", [P, TILES])
        epsc = sb("epsc", [P, 1])
        w_qkv_sb = sb("w_qkv_sb", [P, 3 * D])
        b_qkv_sb = sb("b_qkv_sb", [P, 3 * D])
        w_out_sb = sb("w_out_sb", [P, D])
        b_out_sb = sb("b_out_sb", [P, D])
        w_msg_sb = sb("w_msg_sb", [P, D])
        b_msg_sb = sb("b_msg_sb", [P, D])
        gb = sb("gb", [P, 1])
        diag_adj = sb("diag_adj", [P, TILES])
        neg_gb_diag = sb("neg_gb_diag", [P, TILES])
        diag_w = sb("diag_w", [P, TILES])
        wtmp = sb("wtmp", [P, TILES * GROUPS])
        wtmp2 = sb("wtmp2", [P, TILES * GROUPS])
        row_of = sb("row_of", [P, TILES, GROUPS])
        edge_adj = sb("edge_adj", [P, TILES, GROUPS])
        edge_w = sb("edge_w", [P, TILES, GROUPS])
        cols_all = sb("cols_all", [P, TILES, GROUPS], U32)
        ends = sb("ends", [P, TILES])
        found = sb("found", [P, TILES])
        left = sb("left", [P, TILES])
        last_code = sb("last_code", [P, TILES])
        z = sb("z", [P, TILES + 1, D])
        a_ring = sb("a_ring", [P, 2, N])
        present = sb("present", [P, QUARTERS, QW], BF16)
        code_left = sb("code_left", [P, FOLD])
        c8 = sb("c8", [P, SLOTS])
        m8 = sb("m8", [P, SLOTS], U32)
        bits = sb("bits", [P, 2, SLOTS], U32)
        rest = sb("rest", [P, SLOTS])
        rest2 = sb("rest2", [P, SLOTS])
        expo = sb("expo", [P, 2, SLOTS], U32)
        key = sb("key", [P, 2, SLOTS])
        cand = sb("cand", [P, 2, SLOTS])
        cand_left = sb("cand_left", [P, 2, SLOTS])
        taken = sb("taken", [P, 2, SLOTS])
        count = sb("count", [P, 2, 1])
        rowinfo = sb("rowinfo", [P, 2, SLOTS + 2])
        starts = sb("starts", [P, EDGES])
        member = sb("member", [P, 2, EDGES])
        slot = sb("slot", [P, GROUPS])
        is_slot = sb("is_slot", [P, 2, GROUPS, SLOTS])
        picked = sb("picked", [P, GROUPS, SLOTS])
        keys = sb("keys", [P, GROUPS])
        row_u = sb("row_u", [P, GROUPS], U32)
        row_sh = sb("row_sh", [P, GROUPS], U32)
        cols = sb("cols", [P, 2, GROUPS], U32)
        flat = sb("flat", [P, 2, GROUPS], U32)
        empty = sb("empty", [P, 2, SLOTS])
        q_own = sb("q_own", [P, 2, D])
        k_own = sb("k_own", [P, 2, D])
        v_own = sb("v_own", [P, 2, D])
        x_own = sb("x_own", [P, 2, D])
        kv_edge = sb("kv_edge", [P, 2, GROUPS, 2 * D])
        adj_edge = sb("adj_edge", [P, 2, GROUPS])
        diag_prod = sb("diag_prod", [P, D])
        diag_sum = sb("diag_sum", [P, HEADS])
        neg_diag = sb("neg_diag", [P, 2, HEADS])
        prod = sb("prod", [P, GROUPS, D])
        psum_ = sb("psum_", [P, GROUPS, HEADS])
        pen = sb("pen", [P, GROUPS])
        bias = sb("bias", [P, GROUPS])
        score = sb("score", [P, GROUPS, HEADS])
        by_slot = sb("by_slot", [P, GROUPS, HEADS, SLOTS])
        member_t = sb("member_t", [P, GROUPS, P])
        slotted = sb("slotted", [P, HEADS, SLOTS])
        rowmax = sb("rowmax", [P, HEADS])
        neg_max = sb("neg_max", [P, HEADS])
        shifted = sb("shifted", [P, GROUPS, HEADS])
        shifted_d = sb("shifted_d", [P, HEADS])
        weighted = sb("weighted", [P, GROUPS, D + HEADS])
        prob_d = sb("prob_d", [P, 2, HEADS])
        pv_d = sb("pv_d", [P, D])
        resid = sb("resid", [P, D])
        num = sb("num", [P, D])
        den = sb("den", [P, HEADS])
        rden = sb("rden", [P, HEADS])
        att = sb("att", [P, D])
        att_t = sb("att_t", [P, D])
        y = sb("y", [P, D])
        stats = sb("stats", [P, 6])
        mv = sb("mv", [P, 2])
        lnv = sb("lnv", [P, 1])
        r0 = sb("r0", [P, 1])
        t1 = sb("t1", [P, 1])
        t2 = sb("t2", [P, 1])
        rstd = sb("rstd", [P, 1])
        x1 = sb("x1", [P, D])
        x1_t = sb("x1_t", [P, D])
        msg = sb("msg", [P, 2, D])
        qkv = sb("qkv", [P, 2, 4, 3 * D])
        x_t = sb("x_t", [P, 2, P])
        msg_edge = sb("msg_edge", [P, 2, GROUPS, D])
        cols2 = sb("cols2", [P, 2, GROUPS], U32)
        memw = sb("memw", [P, 2, GROUPS, P])
        y2 = sb("y2", [P, 2, D])

        room = a_ring[:].rearrange("p a n -> p (a n)")
        carved = [0]

        def carve(columns):
            carved[0] += columns
            return room[:, carved[0] - columns:carved[0]]

        d_s = carve(HEADS * DENSE_COLS).rearrange("p (h n) -> p h n", h=HEADS)
        d_p = carve(HEADS * DENSE_COLS).rearrange("p (h n) -> p h n", h=HEADS)
        d_pt = carve(HEADS * DENSE_COLS).rearrange("p (h c r) -> p h c r", h=HEADS, c=CHUNKS)
        d_adj = carve(DENSE_COLS)
        d_on = carve(DENSE_COLS)
        d_pen = carve(DENSE_COLS)
        d_bias = carve(DENSE_COLS)
        d_kt = carve(DENSE_COLS)
        d_k = carve(CHUNKS * D).rearrange("p (c d) -> p c d", c=CHUNKS)
        d_v = carve(CHUNKS * D).rearrange("p (c d) -> p c d", c=CHUNKS)
        d_e = carve(DENSE_COLS)
        d_w = carve(DENSE_COLS)
        d_q = sb("d_q", [P, D])
        d_x = sb("d_x", [P, D])
        d_qh = sb("d_qh", [P, HEADS, P])
        d_bmax = sb("d_bmax", [P, HEADS])
        d_new = sb("d_new", [P, HEADS])
        d_old = sb("d_old", [P, HEADS])
        d_fall = sb("d_fall", [P, HEADS])
        d_fell = sb("d_fell", [P, HEADS])
        d_sum = sb("d_sum", [P, HEADS])
        d_part = sb("d_part", [P, HEADS])
        d_out = sb("d_out", [P, D])
        d_msg = sb("d_msg", [P, D])
        row_flags = sb("row_flags", [P, TILES])
        flag_part = sb("flag_part", [P, TILES])
        flags = sb("flags", [P, TILES + 1], U32)

        code = [bank("code0"), bank("code1")]
        b_edge = bank("b_edge")
        q_edge = [bank("q_edge0"), bank("q_edge1")]
        b_max = bank("b_max")
        b_sum = bank("b_sum")
        b_fin = bank("b_fin")
        score_bank = code + q_edge
        p_bank = [b_max, b_fin]
        info_e = b_edge[:, 16:16 + GROUPS * (SLOTS + 2)].rearrange("p (g s) -> p g s", g=GROUPS)
        first_ps = b_edge[:, 0:1]
        slot_ps = b_max[:, 0:HEADS * SLOTS]
        max_ps = b_max[:, 128:128 + GROUPS * HEADS]
        att_ps, proj_ps, x1_ps, msg_ps = (b_fin[:, n * P:(n + 1) * P] for n in range(4))

        s_const = sem("s_const")
        s_cstep = sem("s_cstep")
        s_loaded = sem("s_loaded")
        s_xall = sem("s_xall")
        s_powers = sem("s_powers")
        s_diag = sem("s_diag")
        s_diag2 = sem("s_diag2")
        s_xt = sem("s_xt")
        s_xtc = sem("s_xtc")
        s_qkv = sem("s_qkv")
        s_qkvb = sem("s_qkvb")
        s_stored = [sem("s_stored0"), sem("s_stored1")]
        s_adj = [[sem(f"s_adj{i}{h}") for h in range(2)] for i in range(2)]
        s_qk = [sem("s_qk0"), sem("s_qk1")]
        s_vx = [sem("s_vx0"), sem("s_vx1")]
        signed = sem("signed")
        folded = sem("folded")
        step = sem("step")
        code_free = sem("code_free")
        passed_dve = sem("passed_dve")
        passed_pool = sem("passed_pool")
        passed_sp = sem("passed_sp")
        counted = sem("counted")
        first_ready = sem("first_ready")
        first_copied = sem("first_copied")
        starts_ready = sem("starts_ready")
        member_ready = sem("member_ready")
        info_sent = sem("info_sent")
        q_sent = sem("q_sent")
        idx_ready = sem("idx_ready")
        s_kv = [sem("s_kv0"), sem("s_kv1")]
        s_val = [sem("s_val0"), sem("s_val1")]
        prod_d = sem("prod_d")
        q_read = sem("q_read")
        by_slot_ready = sem("by_slot_ready")
        slots_sent = sem("slots_sent")
        max_ready = sem("max_ready")
        max_sent = sem("max_sent")
        shift_ready = sem("shift_ready")
        exped = sem("exped")
        weighted_ready = sem("weighted_ready")
        summed = sem("summed")
        pool_fin = sem("pool_fin")
        pool_copy = sem("pool_copy")
        att_ready = sem("att_ready")
        att_turned = sem("att_turned")
        att_copied = sem("att_copied")
        projected = sem("projected")
        stats_ready = sem("stats_ready")
        rstd_step = sem("rstd_step")
        x1_ready = sem("x1_ready")
        x1_turned = sem("x1_turned")
        x1_copied = sem("x1_copied")
        msg_made = sem("msg_made")
        msg_ready = sem("msg_ready")
        s_msg = [sem("s_msg0"), sem("s_msg1")]
        w_squared = sem("w_squared")
        w_exped = sem("w_exped")
        l2_cols = sem("l2_cols")
        l2_in = [sem("l2_in0"), sem("l2_in1")]
        l2_memw = sem("l2_memw")
        l2_sum = sem("l2_sum")
        l2_y = sem("l2_y")
        l2_rstd = sem("l2_rstd")
        l2_out = sem("l2_out")
        s_out = [sem("s_out0"), sem("s_out1")]
        turn = sem("turn")
        d_qx_in = sem("d_qx_in")
        d_a_in = sem("d_a_in")
        d_k_in = sem("d_k_in")
        d_v_in = sem("d_v_in")
        d_q_turned = sem("d_q_turned")
        d_q_copied = sem("d_q_copied")
        d_k_turned = sem("d_k_turned")
        d_k_copied = sem("d_k_copied")
        d_scored = sem("d_scored")
        d_a_read = sem("d_a_read")
        d_masked = sem("d_masked")
        d_max_ready = sem("d_max_ready")
        d_fell_ready = sem("d_fell_ready")
        d_exped = sem("d_exped")
        d_p_turned = sem("d_p_turned")
        d_p_copied = sem("d_p_copied")
        d_weighed = sem("d_weighed")
        d_added = sem("d_added")
        e_a_in = sem("e_a_in")
        e_m_in = sem("e_m_in")
        e_squared = sem("e_squared")
        e_a_read = sem("e_a_read")
        e_exped = sem("e_exped")
        e_weight = sem("e_weight")
        e_turned = sem("e_turned")
        e_copied = sem("e_copied")
        e_weighed = sem("e_weighed")
        e_added = sem("e_added")
        d_stored = sem("d_stored")
        flags_summed = sem("flags_summed")
        flags_ready = sem("flags_ready")

        HELD = 6
        LOOP_FROM, PAIRS = HELD, (TILES - HELD) // 2 - 1
        LAST = TILES + HELD - 1

        def active(it):
            return [Tile(it.pair, it.n - k) if it.pair is not None or 0 <= it.n - k < TILES else None
                    for k in range(HELD)]

        def iterations(eng, body):
            for i in range(LOOP_FROM):
                body(active(Tile(None, i)))
            with eng.Fori(0, PAIRS) as pair:
                for u in range(2):
                    body(active(Tile(pair, LOOP_FROM + u)))
            for i in range(LOOP_FROM + 2 * PAIRS, LAST):
                body(active(Tile(None, i)))

        def before_step(eng, base, names, name):
            at = base + names.index(name)
            if not isinstance(at, int) or at > 0:
                eng.wait_ge(turn, at)

        def reached(eng, s, at_least):
            if not isinstance(at_least, int) or at_least > 0:
                eng.wait_ge(s, at_least)

        def heads(ap):
            return ap.rearrange("p (h d) -> p h d", h=HEADS)

        first_tile = Dense(0, TILES, 0, adj[0:P, :], x[0:P, :], q_dram[0:P, :], msg_dram[0:P, :])
        first_tile_2 = Dense(0, TILES, len(FINISH) * (TILES + 1), adj[0:P, :], out_=out[0:P, :])

        def tile_1(t):
            return Dense(t + 1, t, len(FINISH) * t + len(FINISH), adj_rows[t], x_rows[t], q_rows[t], msg_rows[t])

        def tile_2(t):
            return Dense(t + 1, t, len(FINISH_2) * t + (len(FINISH) * (TILES + 1) + len(FINISH_2)), adj_rows[t], out_=out_rows[t])

        def messages_stored(eng):
            eng.wait_ge(s_msg[0], 16 * ((TILES + 1) // 2))
            eng.wait_ge(s_msg[1], 16 * (TILES // 2))
            eng.wait_ge(d_stored, 16)
            eng.wait_ge(flags_ready, 1)
            eng.wait_ge(d_stored, 16 * (TILES + 1))

        def flagged(eng, work, own, first=True):
            def skip(done, tiles):
                for s, amount, *begun in own:
                    eng.wait_ge(s, amount * done + sum(begun))
                    eng.sem_inc(s, amount * tiles)

            with eng.If(eng.value_load(flags[0:1, TILES:TILES + 1], min_val=0, max_val=N) > 0):
                with eng.Fori(0, TILES) as t:
                    with eng.If(eng.value_load(flags[0:1, bass.ds(t, 1)], min_val=0, max_val=N) > 0):
                        work(t)
                    with eng.Else():
                        skip(t + 1, 1)
            with eng.Else():
                skip(1, TILES)

        block = ctx.enter_context(nc.Block())
        NBLK = N // P

        @block.sync
        def _(sp):
            for dst, src in ((w_qkv_sb, w_qkv), (w_out_sb, w_out), (w_msg_sb, w_msg)):
                sp.dma_start(dst[:], src).then_inc(s_loaded, 16)
            for dst, src in ((b_qkv_sb, b_qkv), (b_out_sb, b_out), (b_msg_sb, b_msg)):
                sp.dma_start(dst[:], src.rearrange("(a n) -> a n", a=1).to_broadcast([P, src.shape[0]])).then_inc(s_loaded, 16)
            sp.dma_start(gb[:], graph_bias.rearrange("a b c -> (a b) c").to_broadcast([P, 1])).then_inc(s_loaded, 16)
            sp.dma_start(z[:, 0:NBLK, :], x.rearrange("(p b) d -> p b d", b=NBLK)).then_inc(s_xall, 16)

            def load_adj(t, h):
                sp.dma_start(a_ring[:, t.parity, h * (N // 2):(h + 1) * (N // 2)],
                             adj_rows[t.index()][:, h * (N // 2):(h + 1) * (N // 2)]).then_inc(s_adj[t.parity][h], 16)

            for i in range(2):
                for h in range(2):
                    load_adj(Tile(None, i), h)
            diagonal = bass.AP(tensor=adj.tensor, offset=P * (N + 1), ap=[[TILES * (N + 1), P], [N + 1, TILES]])
            with nc.allow_non_contiguous_dma(reason="one number of every row"):
                sp.dma_start(diag_adj[:], diagonal).then_inc(s_diag, 16)

            q_t = q_dram.rearrange("(p b) d -> p b d", b=NBLK)
            kv_t = kv_dram.rearrange("(p b) d -> p b d", b=NBLK)
            for g in range(NBLK // 4):
                sp.wait_ge(s_qkvb, 4 * g + 4)
                sp.dma_start(q_t[:, 4 * g:4 * g + 4, :], qkv[:, g % 2, :, 0:D]).then_inc(s_stored[g % 2], 16)
                sp.dma_start(kv_t[:, 4 * g:4 * g + 4, :], qkv[:, g % 2, :, D:3 * D]).then_inc(s_stored[g % 2], 16)
            sp.wait_ge(s_stored[0], 16 * NBLK // 4)
            sp.wait_ge(s_stored[1], 16 * NBLK // 4)

            def body(at):
                t = at[0]
                if t:
                    if t.at_least(2):
                        sp.wait_ge(q_sent, t.affine(1, -1))
                        sp.wait_ge(prod_d, t.affine(1, -1))
                    sp.dma_start(q_own[:, t.parity, :], q_rows[t.index()]).then_inc(s_qk[t.parity], 16)
                    sp.dma_start(k_own[:, t.parity, :], kv_rows[t.index()][:, 0:D]).then_inc(s_qk[t.parity], 16)
                    load_ahead(t, 0)
                t = at[3]
                if t:
                    if t.at_least(2):
                        sp.wait_ge(pool_fin, t.affine(2, -2))
                    sp.dma_start(v_own[:, t.parity, :], kv_rows[t.index()][:, D:2 * D]).then_inc(s_vx[t.parity], 16)
                    sp.dma_start(x_own[:, t.parity, :], x_rows[t.index()]).then_inc(s_vx[t.parity], 16)
                if at[5]:
                    store_msg(at[5])
                if at[0]:
                    load_ahead(at[0], 1)

            def load_ahead(t, h):
                if not (t.pair is None and t.n + 2 >= TILES):
                    sp.wait_ge(signed, t.affine(QUARTERS, 2 * h + 2))
                    load_adj(Tile(t.pair, t.n + 2), h)

            def store_msg(t):
                sp.wait_ge(msg_ready, t.affine(1, 1))
                sp.dma_start(msg_rows[t.index()], msg[:, t.parity, :]).then_inc(s_msg[t.parity], 16)

            iterations(sp, body)

            def dense(d):
                def load_a_k(b):
                    reached(sp, d_a_read, d.count(b, 1, 0))
                    sp.dma_start(d_adj, d.adj[:, bass.ds(b * DENSE_COLS, DENSE_COLS)]).then_inc(d_a_in, 16)
                    reached(sp, d_k_turned, d.count(b, 1, 0))
                    sp.dma_start(d_k, kv_dram[bass.ds(b * DENSE_COLS, DENSE_COLS), 0:D].rearrange("(c p) d -> p c d", p=P)
                                 ).then_inc(d_k_in, 16)

                def load_v(b):
                    reached(sp, d_weighed, d.count(b, 1, 0))
                    sp.dma_start(d_v, kv_dram[bass.ds(b * DENSE_COLS, DENSE_COLS), D:2 * D].rearrange("(c p) d -> p c d", p=P)
                                 ).then_inc(d_v_in, 16)

                sp.dma_start(d_q[:], d.q).then_inc(d_qx_in, 16)
                sp.dma_start(d_x[:], d.x).then_inc(d_qx_in, 16)
                load_a_k(0)
                load_a_k(1)
                load_v(0)
                with sp.Fori(0, DENSE_BLOCKS - 2) as b:
                    load_a_k(b + 2)
                    load_v(b + 1)
                load_v(DENSE_BLOCKS - 1)
                sp.wait_ge(turn, d.turns + len(FINISH))
                sp.dma_start(d.msg, d_msg[:]).then_inc(d_stored, 16)
                sp.wait_ge(d_stored, 16 * d.no + 16)
                sp.sem_inc(passed_sp, 1)

            sp.wait_ge(signed, TILES * QUARTERS)
            dense(first_tile)
            sp.wait_ge(flags_ready, 1)
            sp.wait_ge(s_msg[0], 16 * ((TILES + 1) // 2))
            sp.wait_ge(s_msg[1], 16 * (TILES // 2))
            flagged(sp, lambda t: dense(tile_1(t)),
                    [(d_qx_in, 32), (d_a_in, 16 * DENSE_BLOCKS), (d_k_in, 16 * DENSE_BLOCKS), (d_v_in, 16 * DENSE_BLOCKS),
                     (d_stored, 16), (turn, len(FINISH))])

            def store_out(t):
                sp.wait_ge(l2_out, t.affine(1, 1))
                sp.dma_start(out_rows[t.index()], y2[:, t.parity, :]).then_inc(s_out[t.parity], 16)
            with sp.Fori(0, TILES // 2) as pair:
                for u in range(2):
                    store_out(Tile(pair, u))
            store_out(Tile(None, TILES - 1))
            sp.wait_ge(s_out[0], 16 * ((TILES + 1) // 2))
            sp.wait_ge(s_out[1], 16 * (TILES // 2))

            def dense2(d):
                def load_a(b):
                    reached(sp, e_a_read, d.count(b, 1, 0))
                    sp.dma_start(d_adj, d.adj[:, bass.ds(b * DENSE_COLS, DENSE_COLS)]).then_inc(e_a_in, 16)

                def load_m(b):
                    reached(sp, e_weighed, d.count(b, 1, 0))
                    sp.dma_start(d_v, msg_dram[bass.ds(b * DENSE_COLS, DENSE_COLS), :].rearrange("(c p) d -> p c d", p=P)
                                 ).then_inc(e_m_in, 16)

                load_a(0)
                load_a(1)
                load_m(0)
                with sp.Fori(0, DENSE_BLOCKS - 2) as b:
                    load_a(b + 2)
                    load_m(b + 1)
                load_m(DENSE_BLOCKS - 1)
                sp.wait_ge(turn, d.turns + len(FINISH_2))
                sp.dma_start(d.out, d_msg[:]).then_inc(d_stored, 16)
                sp.wait_ge(d_stored, 16 * d.no + 16 * (TILES + 2))
                sp.sem_inc(passed_sp, 1)

            messages_stored(sp)
            dense2(first_tile_2)
            flagged(sp, lambda t: dense2(tile_2(t)),
                    [(e_a_in, 16 * DENSE_BLOCKS), (e_m_in, 16 * DENSE_BLOCKS), (d_stored, 16, 16 * (TILES + 1)),
                     (turn, len(FINISH_2), len(FINISH) * (TILES + 1))])

        @block.gpsimd
        def _(pool):
            done = [0]

            def const(ins):
                done[0] += 1
                ins.then_inc(s_cstep, 1)
                pool.wait_ge(s_cstep, done[0])

            const(nc.gpsimd.memset(ident[:], 0.0))
            const(nc.gpsimd.affine_select(out=ident[:], in_=ident[:], compare_op=ALU.not_equal, fill=1.0, base=0,
                                          pattern=[[-1, P]], channel_multiplier=1))
            const(nc.gpsimd.memset(before[:], 1.0))
            const(nc.gpsimd.affine_select(out=before[:], in_=before[:], compare_op=ALU.is_gt, fill=0.0, base=0,
                                          pattern=[[1, P]], channel_multiplier=-1))
            for dst, pattern, base, ch in ((edge_no[:], [[1, EDGES]], 1, 0), (row_no[:], [[1, P]], 1, 0),
                                           (slot_no[:], [[0, GROUPS], [1, SLOTS]], 0, 0), (edge_col[:], [[P, GROUPS]], 0, 1),
                                           (row_first[:], [[1, TILES]], P - TILES, 0),
                                           (own_col[:], [[1, TILES]], P + 1, TILES),
                                           (rowinfo[:, 0, SLOTS + 1:SLOTS + 2], [[1, 1]], 1, 1),
                                           (rowinfo[:, 1, SLOTS + 1:SLOTS + 2], [[1, 1]], 1, 1)):
                const(nc.gpsimd.iota(dst, pattern=pattern, base=base, channel_multiplier=ch, allow_small_or_imprecise_dtypes=True))
            const(nc.gpsimd.memset(ones[:], 1.0))
            nc.gpsimd.memset(epsc[:], EPS).then_inc(s_const, 1)
            pool.wait_ge(s_loaded, 16 * 7)

            def body(at):
                t = at[2]
                if t:
                    pool.wait_ge(first_copied, t.affine(1, 1))
                    if t.at_least(1):
                        pool.wait_ge(member_ready, t.affine(1, 0))
                    pool.sem_inc(passed_pool, 1)
                    nc.gpsimd.tensor_scalar(starts[:], edge_no[:], rowinfo[:, t.parity, SLOTS:SLOTS + 1], None, ALU.is_gt
                                            ).then_inc(starts_ready, 1)
                t = at[4]
                if t:
                    pool.wait_ge(s_vx[t.parity], t.of_parity(32, 32))
                    if t.at_least(1):
                        pool.wait_ge(att_ready, t.affine(1, 0))
                        pool.wait_ge(stats_ready, t.affine(1, 0))
                    pool.wait_ge(exped, t.affine(2, 2))
                    nc.gpsimd.tensor_tensor(heads(pv_d[:]), heads(v_own[:, t.parity, :]),
                                            prob_d[:, t.parity, :].unsqueeze(2).to_broadcast([P, HEADS, HD]),
                                            ALU.mult).then_inc(pool_fin, 1)
                    nc.gpsimd.tensor_tensor(resid[:], x_own[:, t.parity, :], b_out_sb[:], ALU.add).then_inc(pool_fin, 1)
                t = at[2]
                if t:
                    pool.wait_ge(idx_ready, t.affine(1, 1))
                    if t.at_least(2):
                        pool.wait_ge(weighted_ready, t.affine(1, -1))
                    pool.sem_inc(passed_pool, 1)
                    for g in range(GROUPS):
                        nc.gpsimd.indirect_dma_start(kv_edge[:, t.parity, g, :], None, kv_dram,
                                                     bass.IndirectOffsetOnAxis(ap=cols[:, t.parity, g:g + 1], axis=0)
                                                     ).then_inc(s_kv[t.parity], 16)
                    for g in range(GROUPS):
                        nc.gpsimd.indirect_dma_start(adj_edge[:, t.parity, g:g + 1], None, adj_flat,
                                                     bass.IndirectOffsetOnAxis(ap=flat[:, t.parity, g:g + 1], axis=0)
                                                     ).then_inc(s_val[t.parity], 16)
                    nc.gpsimd.tensor_copy(cols_all[:, t.index(), :], cols[:, t.parity, :]).then_inc(pool_copy, 1)
                t = at[1]
                if t:
                    pool.wait_ge(s_qk[t.parity], t.of_parity(32, 32))
                    if t.at_least(1):
                        pool.wait_ge(idx_ready, t.affine(1, 0))
                    nc.gpsimd.tensor_tensor(diag_prod[:], q_own[:, t.parity, :], k_own[:, t.parity, :],
                                            ALU.mult).then_inc(prod_d, 1)

            iterations(pool, body)

            messages_stored(pool)

            def gather2(t):
                pool.wait_ge(l2_cols, t.affine(1, 1))
                if t.at_least(2):
                    pool.wait_ge(l2_sum, t.affine(1, -1))
                pool.sem_inc(passed_pool, 1)
                for g in range(GROUPS):
                    nc.gpsimd.indirect_dma_start(msg_edge[:, t.parity, g, :], None, msg_dram,
                                                 bass.IndirectOffsetOnAxis(ap=cols2[:, t.parity, g:g + 1], axis=0)
                                                 ).then_inc(l2_in[t.parity], 16)
            for i in range(2):
                gather2(Tile(None, i))
            with pool.Fori(0, (TILES - 3) // 2) as pair:
                for u in range(2):
                    gather2(Tile(pair, 2 + u))
            gather2(Tile(None, TILES - 1))

        @block.scalar
        def _(act):
            nc.scalar.preload_act_table_set("natural_log_exp_and_others")
            for b in range(NBLK):
                act.wait_ge(s_xt, b + 1)
                if b >= 2:
                    act.wait_ge(s_qkv, b - 1)
                nc.scalar.copy(x_t[:, b % 2, :], code[b % 2][:, 0:P]).then_inc(s_xtc, 1)

            def body(at):
                def sign(q):
                    t = at[0]
                    if not t:
                        return
                    if q % 2 == 0:
                        act.wait_ge(s_adj[t.parity][q // 2], t.of_parity(16, 16))
                    if t.at_least(1):
                        act.wait_ge(folded, t.affine(QUARTERS, q + 1 - QUARTERS))
                    nc.scalar.activation(present[:, q, :], a_ring[:, t.parity, q * QW:(q + 1) * QW].bitcast(U32),
                                         ACT.Sign).then_inc(signed, 1)

                t = at[4]
                if t:
                    act.wait_ge(shift_ready, t.affine(1, 1))
                    nc.scalar.activation(weighted[:, :, D:D + HEADS], shifted[:], ACT.Exp).then_inc(exped, 1)
                    nc.scalar.activation(prob_d[:, t.parity, :], shifted_d[:], ACT.Exp).then_inc(exped, 1)
                sign(0)
                sign(1)
                sign(2)
                if t:
                    act.wait_ge(att_turned, t.affine(1, 1))
                    nc.scalar.copy(att_t[:], att_ps).then_inc(att_copied, 1)
                sign(3)
                if t:
                    rsqrt(stats_ready, t.affine(1, 1), rstd_step, t)
                    act.wait_ge(x1_turned, t.affine(1, 1))
                    nc.scalar.copy(x1_t[:], x1_ps).then_inc(x1_copied, 1)

            def rsqrt(ready, value, done, t):
                act.wait_ge(ready, value)
                nc.scalar.activation(lnv[:], mv[:, 1:2], ACT.Ln, bias=epsc[:]).then_inc(done, 1)
                act.wait_ge(done, t.affine(2, 1))
                nc.scalar.activation(r0[:], lnv[:], ACT.Exp, scale=-0.5).then_inc(done, 1)

            def weights_exp(dst, n):
                act.wait_ge(w_squared, n)
                nc.scalar.activation(dst, wtmp[:, 0:dst.shape[1]], ACT.Exp,
                                     scale=-1.0 / (2.0 * SIGMA * SIGMA)).then_inc(w_exped, 1)

            weights_exp(diag_w[:], 1)
            act.wait_ge(s_const, 1)
            iterations(act, body)

            def do(d_base, names, name, ins):
                before_step(act, d_base, names, name)
                ins().then_inc(turn, 1)

            def dense(d):
                def copy_k(b):
                    act.wait_ge(d_k_turned, d.count(b, 1, 1))
                    reached(act, d_scored, d.count(b, HEADS, 0))
                    nc.scalar.copy(d_kt, b_edge[:]).then_inc(d_k_copied, 1)

                def exps(b):
                    act.wait_ge(d_max_ready, d.count(b, 1, 1))
                    nc.scalar.activation(d_fell[:], d_fall[:], ACT.Exp).then_inc(d_fell_ready, 1)
                    for h in range(HEADS):
                        nc.scalar.activation(d_p[:, h, :], d_s[:, h, :], ACT.Exp, bias=d_new[:, h:h + 1],
                                             accum_out=d_part[:, h:h + 1]).then_inc(d_exped, 1)
                    reached(act, d_weighed, d.count(b, 1, 0))
                    for h in range(HEADS):
                        act.wait_ge(d_p_turned, d.count(b, HEADS, h + 1))
                        nc.scalar.copy(d_pt[:, h].rearrange("p c r -> p (c r)"), p_bank[h % 2][:]).then_inc(d_p_copied, 1)

                act.wait_ge(d_q_turned, d.no + 1)
                for h in range(HEADS):
                    nc.scalar.copy(d_qh[h * HD:(h + 1) * HD, h, :], b_fin[h * HD:(h + 1) * HD, 0:P]).then_inc(d_q_copied, 1)
                copy_k(0)
                copy_k(1)
                exps(0)
                with act.Fori(0, DENSE_BLOCKS - 2) as b:
                    copy_k(b + 2)
                    exps(b + 1)
                exps(DENSE_BLOCKS - 1)
                base = d.turns
                do(base, FINISH, "copy_att", lambda: nc.scalar.copy(att_t[:], att_ps))
                do(base, FINISH, "ln", lambda: nc.scalar.activation(lnv[:], mv[:, 1:2], ACT.Ln, bias=epsc[:]))
                do(base, FINISH, "r0", lambda: nc.scalar.activation(r0[:], lnv[:], ACT.Exp, scale=-0.5))
                do(base, FINISH, "copy_x1", lambda: nc.scalar.copy(x1_t[:], x1_ps))

            dense(first_tile)
            act.wait_ge(flags_ready, 1)
            flagged(act, lambda t: dense(tile_1(t)),
                    [(d_q_copied, HEADS), (d_k_copied, DENSE_BLOCKS), (d_fell_ready, DENSE_BLOCKS),
                     (d_exped, HEADS * DENSE_BLOCKS), (d_p_copied, HEADS * DENSE_BLOCKS)])
            weights_exp(edge_w[:].rearrange("p t g -> p (t g)"), 2)

            def tile2(t):
                if t.at_least(2):
                    act.wait_ge(l2_in[t.parity], t.of_parity(16 * GROUPS, 0))
                nc.scalar.copy(cols2[:, t.parity, :], cols_all[:, t.index(), :]).then_inc(l2_cols, 1)
                if t.at_least(1):
                    prev(Tile(t.pair, t.n - 1))

            def prev(t):
                rsqrt(l2_y, t.affine(1, 1), l2_rstd, t)
            act.wait_ge(pool_copy, TILES)
            for i in range(2):
                tile2(Tile(None, i))
            with act.Fori(0, (TILES - 3) // 2) as pair:
                for u in range(2):
                    tile2(Tile(pair, 2 + u))
            tile2(Tile(None, TILES - 1))
            prev(Tile(None, TILES - 1))

            def dense2(d):
                def block(b):
                    act.wait_ge(e_squared, d.count(b, 1, 1))
                    nc.scalar.activation(d_e, d_on, ACT.Exp, scale=-1.0 / (2.0 * SIGMA * SIGMA)).then_inc(e_exped, 1)
                    act.wait_ge(e_turned, d.count(b, 1, 1))
                    reached(act, e_weighed, d.count(b, 1, 0))
                    nc.scalar.copy(d_pt[:, 0].rearrange("p c r -> p (c r)"), b_max[:]).then_inc(e_copied, 1)

                block(0)
                with act.Fori(0, DENSE_BLOCKS - 1) as b:
                    block(b + 1)
                do(d.turns, FINISH_2, "ln", lambda: nc.scalar.activation(lnv[:], mv[:, 1:2], ACT.Ln, bias=epsc[:]))
                do(d.turns, FINISH_2, "r0", lambda: nc.scalar.activation(r0[:], lnv[:], ACT.Exp, scale=-0.5))

            dense2(first_tile_2)
            flagged(act, lambda t: dense2(tile_2(t)), [(e_exped, DENSE_BLOCKS), (e_copied, DENSE_BLOCKS)])

        @block.tensor
        def _(pe):
            pe.wait_ge(s_const, 1)
            pe.wait_ge(s_loaded, 16 * 7)
            pe.wait_ge(s_xall, 16)

            def turn_x(b):
                if b >= 2:
                    pe.wait_ge(s_xtc, b - 1)
                nc.tensor.transpose(code[b % 2][:, 0:P], z[:, b, :], ident[:]).then_inc(s_xt, 1)

            turn_x(0)
            for b in range(NBLK):
                if b + 1 < NBLK:
                    turn_x(b + 1)
                pe.wait_ge(s_xtc, b + 1)
                if b >= 2:
                    pe.wait_ge(s_qkvb, b - 1)
                nc.tensor.matmul(q_edge[b % 2][:, 0:3 * D], x_t[:, b % 2, :], w_qkv_sb[:], start=True, stop=True).then_inc(s_qkv, 1)
            pe.wait_ge(s_qkvb, NBLK)
            pe.wait_ge(s_powers, 1)

            def body(at):
                def fold_quarter(q):
                    t = at[0]
                    if not t:
                        return
                    pe.wait_ge(signed, t.affine(QUARTERS, q + 1))
                    if q == 0 and t.at_least(2):
                        pe.wait_ge(code_free, t.affine(1, -1))
                    per = BLOCKS // QUARTERS
                    for b in range(q * per, (q + 1) * per):
                        last = nc.tensor.matmul(code[t.parity][:], power[:, b, :],
                                                present[:, q, (b % per) * FOLD:(b % per + 1) * FOLD],
                                                start=(b == 0), stop=(b == BLOCKS - 1))
                    last.then_inc(folded, 1)

                t = at[2]
                if t:
                    pe.wait_ge(counted, t.affine(1, 1))
                    if t.at_least(1):
                        pe.wait_ge(idx_ready, t.affine(1, 0))
                    nc.tensor.matmul(first_ps, before[:], count[:, t.parity, :], start=True, stop=True).then_inc(first_ready, 1)
                t = at[4]
                if t:
                    pe.wait_ge(max_ready, t.affine(1, 1))
                    for g in range(GROUPS):
                        last = nc.tensor.matmul(max_ps[:, g * HEADS:(g + 1) * HEADS], member[:, t.parity, g * P:(g + 1) * P],
                                                neg_max[:], start=True, stop=True)
                    last.then_inc(max_sent, 1)
                    pe.wait_ge(weighted_ready, t.affine(1, 1))
                    if t.at_least(1):
                        pe.wait_ge(att_ready, t.affine(1, 0))
                    for g in range(GROUPS):
                        last = nc.tensor.matmul(b_sum[:, 0:D + HEADS], member_t[:, g, :], weighted[:, g, :],
                                                start=(g == 0), stop=(g == GROUPS - 1))
                    last.then_inc(summed, 1)
                t = at[2]
                if t:
                    pe.wait_ge(member_ready, t.affine(1, 1))
                    for g in range(GROUPS):
                        last = nc.tensor.matmul(info_e[:, g, :], member[:, t.parity, g * P:(g + 1) * P],
                                                rowinfo[:, t.parity, :], start=True, stop=True)
                    last.then_inc(info_sent, 1)
                    pe.wait_ge(s_qk[t.parity], t.of_parity(32, 32))
                    if t.at_least(2):
                        pe.wait_ge(q_read, t.affine(1, -1))
                    for g in range(GROUPS):
                        last = nc.tensor.matmul(q_edge[t.parity][:, g * D:(g + 1) * D], member[:, t.parity, g * P:(g + 1) * P],
                                                q_own[:, t.parity, :], start=True, stop=True)
                    last.then_inc(q_sent, 1)
                fold_quarter(0)
                t = at[4]
                if t:
                    pe.wait_ge(att_ready, t.affine(1, 1))
                    if t.at_least(1):
                        pe.wait_ge(msg_ready, t.affine(1, 0))
                    nc.tensor.transpose(att_ps, att[:], ident[:]).then_inc(att_turned, 1)
                    pe.wait_ge(att_copied, t.affine(1, 1))
                    nc.tensor.matmul(proj_ps, att_t[:], w_out_sb[:], start=True, stop=True).then_inc(projected, 1)
                fold_quarter(1)
                fold_quarter(2)
                fold_quarter(3)
                t = at[3]
                if t:
                    pe.wait_ge(by_slot_ready, t.affine(1, 1))
                    for g in range(GROUPS):
                        last = nc.tensor.matmul(slot_ps, member_t[:, g, :], by_slot[:, g].rearrange("p h s -> p (h s)"),
                                                start=(g == 0), stop=(g == GROUPS - 1))
                    last.then_inc(slots_sent, 1)
                t = at[4]
                if t:
                    pe.wait_ge(x1_ready, t.affine(1, 1))
                    nc.tensor.transpose(x1_ps, x1[:], ident[:]).then_inc(x1_turned, 1)
                    pe.wait_ge(x1_copied, t.affine(1, 1))
                    nc.tensor.matmul(msg_ps, x1_t[:], w_msg_sb[:], start=True, stop=True).then_inc(msg_made, 1)

            iterations(pe, body)

            def do(d_base, names, name, work):
                before_step(pe, d_base, names, name)
                work().then_inc(turn, 1)

            def dense(d):
                def front(b):
                    pe.wait_ge(d_k_in, d.count(b, 16, 16))
                    reached(pe, d_k_copied, d.count(b, 1, 0))
                    for c in range(CHUNKS):
                        last = nc.tensor.transpose(b_edge[:, c * P:(c + 1) * P], d_k[:, c, :], ident[:])
                    last.then_inc(d_k_turned, 1)
                    pe.wait_ge(d_k_copied, d.count(b, 1, 1))
                    pe.wait_ge(d_q_copied, d.no * HEADS + HEADS)
                    for h in range(HEADS):
                        reached(pe, d_masked, d.count(b, HEADS, h + 1 - HEADS))
                        nc.tensor.matmul(score_bank[h][:], d_qh[:, h, :], d_kt, start=True, stop=True).then_inc(d_scored, 1)

                def back(b):
                    for h in range(HEADS):
                        pe.wait_ge(d_exped, d.count(b, HEADS, h + 1))
                        if h >= 2:
                            pe.wait_ge(d_p_copied, d.count(b, HEADS, h - 1))
                        for c in range(CHUNKS):
                            last = nc.tensor.transpose(p_bank[h % 2][:, c * P:(c + 1) * P], d_p[:, h, c * P:(c + 1) * P], ident[:])
                        last.then_inc(d_p_turned, 1)
                    pe.wait_ge(d_p_copied, d.count(b, HEADS, HEADS))
                    pe.wait_ge(d_v_in, d.count(b, 16, 16))
                    reached(pe, d_added, d.count(b, 1, 0))
                    for h in range(HEADS):
                        for c in range(CHUNKS):
                            last = nc.tensor.matmul(b_sum[:, h * HD:(h + 1) * HD], d_pt[:, h, c, :], d_v[:, c, h * HD:(h + 1) * HD],
                                                    start=(c == 0), stop=(c == CHUNKS - 1))
                    last.then_inc(d_weighed, 1)

                pe.wait_ge(d_qx_in, 32 * d.no + 32)
                nc.tensor.transpose(b_fin[:, 0:P], d_q[:], ident[:]).then_inc(d_q_turned, 1)
                front(0)
                front(1)
                back(0)
                with pe.Fori(0, DENSE_BLOCKS - 2) as b:
                    front(b + 2)
                    back(b + 1)
                back(DENSE_BLOCKS - 1)
                base = d.turns
                do(base, FINISH, "turn_att", lambda: nc.tensor.transpose(att_ps, att[:], ident[:]))
                do(base, FINISH, "project", lambda: nc.tensor.matmul(proj_ps, att_t[:], w_out_sb[:], start=True, stop=True))
                do(base, FINISH, "turn_x1", lambda: nc.tensor.transpose(x1_ps, x1[:], ident[:]))
                do(base, FINISH, "message", lambda: nc.tensor.matmul(msg_ps, x1_t[:], w_msg_sb[:], start=True, stop=True))

            pe.wait_ge(msg_ready, TILES)
            dense(first_tile)
            pe.wait_ge(flags_summed, 1)
            nc.tensor.matmul(b_edge[:, 0:TILES], ones[:], row_flags[:], start=True, stop=True).then_inc(flags_summed, 1)
            pe.wait_ge(flags_ready, 1)
            flagged(pe, lambda t: dense(tile_1(t)),
                    [(d_q_turned, 1), (d_k_turned, DENSE_BLOCKS), (d_scored, HEADS * DENSE_BLOCKS),
                     (d_p_turned, HEADS * DENSE_BLOCKS), (d_weighed, DENSE_BLOCKS)])

            def sum2(t):
                pe.wait_ge(l2_in[t.parity], t.of_parity(16 * GROUPS, 16 * GROUPS))
                pe.wait_ge(l2_memw, t.affine(1, 1))
                if t.at_least(2):
                    pe.wait_ge(l2_y, t.affine(1, -1))
                for g in range(GROUPS):
                    last = nc.tensor.matmul(code[t.parity][:, 0:D], memw[:, t.parity, g, :], msg_edge[:, t.parity, g, :],
                                            start=(g == 0), stop=(g == GROUPS - 1))
                last.then_inc(l2_sum, 1)
            for i in range(2):
                sum2(Tile(None, i))
            with pe.Fori(0, (TILES - 3) // 2) as pair:
                for u in range(2):
                    sum2(Tile(pair, 2 + u))
            sum2(Tile(None, TILES - 1))

            def dense2(d):
                def block(b):
                    pe.wait_ge(e_weight, d.count(b, 1, 1))
                    for c in range(CHUNKS):
                        last = nc.tensor.transpose(b_max[:, c * P:(c + 1) * P], d_w[:, c * P:(c + 1) * P], ident[:])
                    last.then_inc(e_turned, 1)
                    pe.wait_ge(e_copied, d.count(b, 1, 1))
                    pe.wait_ge(e_m_in, d.count(b, 16, 16))
                    reached(pe, e_added, d.count(b, 1, 0))
                    for c in range(CHUNKS):
                        last = nc.tensor.matmul(b_sum[:, 0:D], d_pt[:, 0, c, :], d_v[:, c, :], start=(c == 0), stop=(c == CHUNKS - 1))
                    last.then_inc(e_weighed, 1)

                block(0)
                with pe.Fori(0, DENSE_BLOCKS - 1) as b:
                    block(b + 1)

            dense2(first_tile_2)
            flagged(pe, lambda t: dense2(tile_2(t)), [(e_turned, DENSE_BLOCKS), (e_weighed, DENSE_BLOCKS)])

        @block.vector
        def _(dve):
            V = nc.vector
            STEPS = 50
            made = [0]
            loops = []
            STEPS2 = 9
            history = []

            def steps_done():
                return sum((reg * steps for reg, steps in loops), made[0])

            def run(ins, ready=None, value=None):
                if ready is None:
                    made[0] += 1
                    ins.then_inc(step, 1)
                    history.append((step, steps_done()))
                else:
                    ins.then_inc(ready, 1)
                    history.append((ready, value))

            @contextmanager
            def counting(reg, steps, last=None):
                begun = made[0]
                loops.append((reg, steps))
                history[:] = [last(reg) if last else (step, steps_done())] * 8
                yield
                assert made[0] == begun + steps and (last or history[-1][0] is step), (made[0] - begun, steps)
                loops.pop()
                made[0] = begun

            @contextmanager
            def counted_loop(count, steps, last=None):
                with dve.Fori(0, count) as reg:
                    with counting(reg, steps, last):
                        yield reg
                made[0] += count * steps
                history[:] = [last(count) if last else (step, steps_done())] * 8

            def unfused():
                dve.sem_inc(passed_dve, 1)

            def after(n=1):
                if len(history) >= n:
                    dve.wait_ge(*history[-n])

            dve.wait_ge(s_const, 1)
            for b in range(BLOCKS):
                run(V.tensor_scalar(power[:, b, :], ident[:], float(2 ** b), None, ALU.mult))
            run(V.memset(d_qh[:], 0.0))
            after()
            run(V.memset(rest2[:], 0.0), s_powers, 1)
            dve.wait_ge(s_loaded, 16 * 7)
            for b in range(NBLK):
                g = b // 4
                dve.wait_ge(s_qkv, b + 1)
                if g >= 2 and b % 4 == 0:
                    dve.wait_ge(s_stored[g % 2], 32 * (g // 2))
                run(V.tensor_tensor(qkv[:, g % 2, b % 4, :], q_edge[b % 2][:, 0:3 * D], b_qkv_sb[:], ALU.add), s_qkvb, b + 1)

            def weights(dst, src, n):
                w, zero = wtmp[:, 0:src.shape[1]], wtmp2[:, 0:src.shape[1]]
                after()
                run(V.tensor_scalar(zero, src, 0.0, None, ALU.is_equal))
                after()
                run(V.tensor_tensor(w, src, zero, ALU.add))
                after()
                run(V.reciprocal(w, w))
                after()
                run(V.tensor_scalar(w, w, -1.0, None, ALU.add))
                after()
                run(V.tensor_tensor(w, w, w, ALU.mult), w_squared, n)
                after()
                run(V.scalar_tensor_tensor(zero, src, 1.0, zero, ALU.is_lt, ALU.subtract))
                dve.wait_ge(w_exped, n)
                after()
                run(V.tensor_tensor(dst, dst, zero, ALU.mult))

            def newton():
                run(V.tensor_tensor(t1[:], r0[:], r0[:], ALU.mult))
                after()
                run(V.scalar_tensor_tensor(t2[:], mv[:, 1:2], EPS, t1[:], ALU.add, ALU.mult))
                after()
                run(V.tensor_scalar(t1[:], t2[:], -0.5, 1.5, ALU.mult, ALU.add))
                after()
                run(V.tensor_tensor(rstd[:], t1[:], r0[:], ALU.mult))

            dve.wait_ge(s_diag, 16)
            run(V.tensor_scalar(neg_gb_diag[:], diag_adj[:], gb[:], -1.0, ALU.mult, ALU.mult))
            weights(diag_w[:], diag_adj[:], 1)

            def scan(t, part):
                ps = code[t.parity]
                if part == 0:
                    dve.wait_ge(folded, t.affine(QUARTERS, QUARTERS))
                    unfused()
                    run(V.max(c8[:, 0:8], ps[:]))
                elif part == 1:
                    unfused()
                    run(V.max_index(m8[:, 0:8], c8[:, 0:8], ps[:]))
                elif part == 2:
                    unfused()
                    run(V.match_replace(code_left[:], c8[:, 0:8], ps[:], 0.0), code_free, t.affine(1, 1))
                elif part == 3:
                    unfused()
                    run(V.max(c8[:, 8:16], code_left[:]))
                elif part == 4:
                    unfused()
                    run(V.max_index(m8[:, 8:16], c8[:, 8:16], code_left[:]))
                elif part == 5:
                    run(V.tensor_scalar(bits[:, 0, :], c8[:].bitcast(U32), EXPONENT, None, ALU.bitwise_and))
                elif part == 6:
                    run(V.tensor_tensor(rest[:], c8[:], bits[:, 0, :].bitcast(F32), ALU.subtract))
                elif part == 7:
                    run(V.tensor_scalar(bits[:, 1, :], rest[:].bitcast(U32), EXPONENT, None, ALU.bitwise_and))
                elif part == 8:
                    run(V.tensor_scalar(expo[:], bits[:], 23 - 9, None, ALU.logical_shift_right))
                elif part == 9:
                    run(V.scalar_tensor_tensor(rest2[:], rest[:], 1.0, bits[:, 1, :].bitcast(F32), ALU.mult, ALU.subtract,
                                               accum_out=left[:, bass.ds(t.index(), 1)]))
                elif part == 10:
                    run(V.scalar_tensor_tensor(key[:], expo[:], float(1 - 127 * FOLD),
                                               m8[:].unsqueeze(1).to_broadcast([P, 2, SLOTS]), ALU.add, ALU.add))
                elif part == 11:
                    run(V.scalar_tensor_tensor(cand[:], bits[:].bitcast(F32), 0.0, key[:], ALU.is_gt, ALU.mult))
                elif part == 18:
                    run(V.scalar_tensor_tensor(cand[:], key[:], own_col[:, bass.ds(t.index(), 1)], cand[:], ALU.not_equal, ALU.mult))
                elif part == 12:
                    unfused()
                    run(V.max(rowinfo[:, t.parity, 0:8], cand[:].rearrange("p a s -> p (a s)")))
                elif part == 13:
                    run(V.tensor_scalar(taken[:], cand[:], 0.0, 0.0, ALU.is_gt, ALU.add, accum_out=found[:, bass.ds(t.index(), 1)]))
                elif part == 14:
                    unfused()
                    run(V.match_replace(cand_left[:].rearrange("p a s -> p (a s)"), rowinfo[:, t.parity, 0:8],
                                        cand[:].rearrange("p a s -> p (a s)"), 0.0))
                elif part == 15:
                    run(V.tensor_copy(last_code[:, bass.ds(t.index(), 1)], c8[:, SLOTS - 1:SLOTS]))
                elif part == 16:
                    unfused()
                    run(V.max(rowinfo[:, t.parity, 8:16], cand_left[:].rearrange("p a s -> p (a s)")))
                elif part == 17:
                    run(V.tensor_scalar(count[:, t.parity, :], found[:, bass.ds(t.index(), 1)], float(SLOTS), None, ALU.min),
                        counted, t.affine(1, 1))

            def gather_(t, part):
                info = rowinfo[:, t.parity, :]
                if part == 0:
                    dve.wait_ge(first_ready, t.affine(1, 1))
                    run(V.tensor_copy(info[:, SLOTS:SLOTS + 1], first_ps), first_copied, t.affine(1, 1))
                    run(V.tensor_tensor(ends[:, bass.ds(t.index(), 1)], first_ps, count[:, t.parity, :], ALU.add))
                elif part == 2:
                    dve.wait_ge(prod_d, t.affine(1, 1))
                    run(V.tensor_reduce(diag_sum[:], diag_prod[:].rearrange("p (h d) -> p h d", h=HEADS), AX_X, ALU.add))
                elif part == 3:
                    dve.wait_ge(starts_ready, t.affine(1, 1))
                    run(V.scalar_tensor_tensor(member[:, t.parity, :], edge_no[:], ends[:, bass.ds(t.index(), 1)], starts[:],
                                               ALU.is_le, ALU.mult), member_ready, t.affine(1, 1))
                elif part == 4:
                    run(V.tensor_scalar(neg_diag[:, t.parity, :], diag_sum[:], -SCALE, neg_gb_diag[:, bass.ds(t.index(), 1)],
                                        ALU.mult, ALU.add))
                elif part == 5:
                    run(V.tensor_scalar(empty[:, t.parity, :], info[:, 0:SLOTS], 0.0, MASKED, ALU.is_equal, ALU.mult))
                elif part == 6:
                    run(V.tensor_tensor(slot[:], edge_col[:], info_e[:, :, SLOTS], ALU.subtract))
                elif part == 7:
                    dve.wait_ge(info_sent, t.affine(1, 1))
                    run(V.tensor_copy(row_of[:, t.index(), :], info_e[:, :, SLOTS + 1]))
                elif part == 8:
                    run(V.tensor_tensor(is_slot[:, t.parity], slot_no[:], slot[:].unsqueeze(2).to_broadcast([P, GROUPS, SLOTS]),
                                        ALU.is_equal))
                elif part == 9:
                    run(V.tensor_scalar(row_u[:], row_of[:, t.index(), :], float(TILES), row_first[:, bass.ds(t.index(), 1)],
                                        ALU.mult, ALU.add))
                elif part == 10:
                    run(V.tensor_tensor(picked[:], is_slot[:, t.parity], info_e[:, :, 0:SLOTS], ALU.mult))
                elif part == 11:
                    run(V.tensor_scalar(row_sh[:], row_u[:], 13, None, ALU.logical_shift_left))
                elif part == 12:
                    run(V.tensor_reduce(keys[:], picked[:], AX_X, ALU.add))
                elif part == 13:
                    if t.at_least(2):
                        dve.wait_ge(pool_copy, t.affine(1, -1))
                    run(V.tensor_scalar(cols[:, t.parity, :], keys[:], -1.0, 0.0, ALU.add, ALU.max))
                elif part == 14:
                    run(V.tensor_tensor(flat[:, t.parity, :], row_sh[:], cols[:, t.parity, :], ALU.bitwise_or),
                        idx_ready, t.affine(1, 1))

            def attend_(t, part):
                if part == 0:
                    dve.wait_ge(s_kv[t.parity], t.of_parity(16 * GROUPS, 16 * GROUPS))
                    dve.wait_ge(q_sent, t.affine(1, 1))
                    run(V.tensor_tensor(prod[:], kv_edge[:, t.parity, :, 0:D],
                                        q_edge[t.parity][:, 0:GROUPS * D].rearrange("p (g d) -> p g d", g=GROUPS), ALU.mult),
                        q_read, t.affine(1, 1))
                elif part == 1:
                    run(V.tensor_scalar(pen[:], adj_edge[:, t.parity, :], 0.0, MASKED, ALU.is_equal, ALU.mult))
                elif part == 2:
                    run(V.tensor_reduce(psum_[:].rearrange("p g h -> p (g h)"),
                                        prod[:].rearrange("p g (h d) -> p (g h) d", h=HEADS), AX_X, ALU.add))
                elif part == 3:
                    run(V.scalar_tensor_tensor(bias[:], adj_edge[:, t.parity, :], gb[:], pen[:], ALU.mult, ALU.add))
                elif part == 4:
                    dve.wait_ge(s_val[t.parity], t.of_parity(16 * GROUPS, 16 * GROUPS))
                    run(V.tensor_copy(edge_adj[:, t.index(), :], adj_edge[:, t.parity, :]))
                elif part == 5:
                    run(V.scalar_tensor_tensor(score[:], psum_[:], SCALE, bias[:].unsqueeze(2).to_broadcast([P, GROUPS, HEADS]),
                                               ALU.mult, ALU.add))
                elif part in (6, 7, 8):
                    g = part - 6
                    run(V.tensor_scalar(member_t[:, g, :], row_no[:], row_of[:, t.index(), g:g + 1], None, ALU.is_equal))
                elif part == 9:
                    run(V.tensor_tensor(by_slot[:], is_slot[:, t.parity].unsqueeze(2).to_broadcast([P, GROUPS, HEADS, SLOTS]),
                                        score[:].unsqueeze(3).to_broadcast([P, GROUPS, HEADS, SLOTS]), ALU.mult),
                        by_slot_ready, t.affine(1, 1))
                elif part == 10:
                    dve.wait_ge(slots_sent, t.affine(1, 1))
                    run(V.tensor_tensor(slotted[:], slot_ps.rearrange("p (h s) -> p h s", h=HEADS),
                                        empty[:, t.parity, :].unsqueeze(1).to_broadcast([P, HEADS, SLOTS]), ALU.add))
                elif part == 11:
                    run(V.tensor_reduce(rowmax[:], slotted[:], AX_X, ALU.max))
                elif part == 12:
                    run(V.scalar_tensor_tensor(neg_max[:], rowmax[:], -1.0, neg_diag[:, t.parity, :], ALU.mult, ALU.min),
                        max_ready, t.affine(1, 1))
                elif part == 13:
                    run(V.tensor_tensor(shifted_d[:], neg_max[:], neg_diag[:, t.parity, :], ALU.subtract))
                elif part == 14:
                    dve.wait_ge(max_sent, t.affine(1, 1))
                    run(V.tensor_tensor(shifted[:].rearrange("p g h -> p (g h)"), score[:].rearrange("p g h -> p (g h)"), max_ps,
                                        ALU.add), shift_ready, t.affine(1, 1))
                elif part == 15:
                    dve.wait_ge(exped, t.affine(2, 1))
                    run(V.tensor_tensor(weighted[:, :, 0:D].rearrange("p g (h d) -> p g h d", h=HEADS),
                                        kv_edge[:, t.parity, :, D:2 * D].rearrange("p g (h d) -> p g h d", h=HEADS),
                                        weighted[:, :, D:D + HEADS].unsqueeze(3).to_broadcast([P, GROUPS, HEADS, HD]), ALU.mult),
                        weighted_ready, t.affine(1, 1))

            def finish_(t, part):
                if part == 0:
                    dve.wait_ge(summed, t.affine(1, 1))
                    dve.wait_ge(pool_fin, t.affine(2, 1))
                    run(V.tensor_tensor(den[:], b_sum[:, D:D + HEADS], prob_d[:, t.parity, :], ALU.add))
                elif part == 1:
                    run(V.tensor_tensor(num[:], b_sum[:, 0:D], pv_d[:], ALU.add))
                elif part == 2:
                    run(V.reciprocal(rden[:], den[:]))
                elif part == 3:
                    run(V.tensor_tensor(att[:].rearrange("p (h d) -> p h d", h=HEADS), num[:].rearrange("p (h d) -> p h d", h=HEADS),
                                        rden[:].unsqueeze(2).to_broadcast([P, HEADS, HD]), ALU.mult), att_ready, t.affine(1, 1))
                elif part == 4:
                    dve.wait_ge(projected, t.affine(1, 1))
                    dve.wait_ge(pool_fin, t.affine(2, 2))
                    run(V.tensor_tensor(y[:], proj_ps, resid[:], ALU.add))
                elif part == 5:
                    run(V.bn_stats(stats[:], y[:]))
                elif part == 6:
                    unfused()
                    run(V.bn_aggr(mv[:], stats[:]), stats_ready, t.affine(1, 1))
                elif part == 7:
                    dve.wait_ge(rstd_step, t.affine(2, 2))
                    run(V.tensor_tensor(t1[:], r0[:], r0[:], ALU.mult))
                elif part == 8:
                    run(V.scalar_tensor_tensor(t2[:], mv[:, 1:2], EPS, t1[:], ALU.add, ALU.mult))
                elif part == 9:
                    run(V.tensor_scalar(t1[:], t2[:], -0.5, 1.5, ALU.mult, ALU.add))
                elif part == 10:
                    run(V.tensor_tensor(rstd[:], t1[:], r0[:], ALU.mult))
                elif part == 11:
                    run(V.tensor_scalar(x1[:], y[:], mv[:, 0:1], rstd[:], ALU.subtract, ALU.mult), x1_ready, t.affine(1, 1))
                elif part == 12:
                    dve.wait_ge(msg_made, t.affine(1, 1))
                    if t.at_least(2):
                        dve.wait_ge(s_msg[t.parity], t.of_parity(16, 0))
                    run(V.tensor_tensor(msg[:, t.parity, :], msg_ps, b_msg_sb[:], ALU.add), msg_ready, t.affine(1, 1))
                elif part == 13:
                    run(V.scalar_tensor_tensor(z[:, t.index(), :], msg[:, t.parity, :], diag_w[:, bass.ds(t.index(), 1)], x1[:],
                                               ALU.mult, ALU.add))

            F, A, G, S = finish_, attend_, gather_, scan
            ORDER = [
                (G, 5, 2, 1), (F, 12, 5, 8), (G, 0, 2, 4), (F, 13, 5, 2), (A, 14, 4, 8), (S, 0, 1, 8), (A, 15, 4, 8), (S, 1, 1, 2),
                (G, 3, 2, 6), (G, 2, 2, 8), (F, 0, 4, 8), (G, 4, 2, 2), (F, 1, 4, 8), (F, 2, 4, 3), (G, 7, 2, 8), (G, 6, 2, 8),
                (G, 9, 2, 2), (G, 8, 2, 2), (G, 11, 2, 2), (G, 10, 2, 2), (G, 12, 2, 1), (G, 13, 2, 1), (G, 14, 2, 1), (F, 3, 4, 8),
                (S, 2, 1, 8), (S, 3, 1, 1), (S, 4, 1, 1), (S, 5, 1, 2), (A, 6, 3, 8), (A, 8, 3, 8), (A, 7, 3, 8), (F, 4, 4, 8),
                (S, 6, 1, 5), (F, 5, 4, 2), (S, 7, 1, 2), (F, 6, 4, 2), (S, 8, 1, 2), (S, 9, 1, 3), (S, 10, 1, 2), (A, 0, 3, 8),
                (A, 4, 3, 8), (A, 1, 3, 8), (F, 7, 4, 8), (A, 3, 3, 2), (A, 2, 3, 5), (F, 8, 4, 3), (A, 5, 3, 2), (F, 9, 4, 2),
                (A, 9, 3, 2), (F, 10, 4, 2), (S, 11, 1, 8), (F, 11, 4, 2), (S, 15, 1, 8), (S, 18, 1, 3), (S, 13, 1, 1), (A, 10, 3, 8),
                (A, 11, 3, 1), (S, 12, 1, 4), (A, 12, 3, 2), (S, 14, 1, 2), (A, 13, 3, 2), (S, 17, 1, 7), (S, 16, 1, 3)]

            def body(at):
                whole = all(at)
                for stage, part, k, back in ORDER:
                    if at[k]:
                        after(back if whole else 1)
                        stage(at[k], part)

            for i in range(LOOP_FROM):
                body(active(Tile(None, i)))
            with counted_loop(PAIRS, 2 * STEPS) as pair:
                for u in range(2):
                    body(active(Tile(pair, LOOP_FROM + u)))
            for i in range(LOOP_FROM + 2 * PAIRS, LAST):
                body(active(Tile(None, i)))

            def do(d_base, names, name, ins):
                before_step(dve, d_base, names, name)
                ins().then_inc(turn, 1)

            def wide(ap, n=P):
                return ap.unsqueeze(2).to_broadcast([P, HEADS, n])

            def newton_steps(base, names):
                do(base, names, "n1", lambda: V.tensor_tensor(t1[:], r0[:], r0[:], ALU.mult))
                do(base, names, "n2", lambda: V.scalar_tensor_tensor(t2[:], mv[:, 1:2], EPS, t1[:], ALU.add, ALU.mult))
                do(base, names, "n3", lambda: V.tensor_scalar(t1[:], t2[:], -0.5, 1.5, ALU.mult, ALU.add))
                do(base, names, "n4", lambda: V.tensor_tensor(rstd[:], t1[:], r0[:], ALU.mult))

            def aggregate(base, names):
                before_step(dve, base, names, "aggr")
                unfused()
                V.bn_aggr(mv[:], stats[:]).then_inc(turn, 1)

            def dense(d):
                reached(dve, turn, d.turns)
                for dst, value in ((d_old, 3e38), (d_sum, 0.0), (d_out, 0.0)):
                    run(V.memset(dst[:], value))

                def masked(b, h):
                    dve.wait_ge(d_scored, d.count(b, HEADS, h + 1))
                    reached(dve, d_exped, d.count(b, HEADS, h + 1 - HEADS))
                    run(V.scalar_tensor_tensor(d_s[:, h, :], score_bank[h][:], SCALE, d_on, ALU.mult, ALU.mult),
                        d_masked, d.count(b, HEADS, h + 1))

                def biased(h):
                    run(V.tensor_tensor(d_s[:, h, :], d_s[:, h, :], d_bias, ALU.add))

                def block_max(h):
                    run(V.tensor_reduce(d_bmax[:, h:h + 1], d_s[:, h, :], AX_X, ALU.max))

                def block_scores(b, last_block=None):
                    after()
                    dve.wait_ge(d_a_in, d.count(b, 16, 16))
                    run(V.tensor_scalar(d_on, d_adj, 0.0, None, ALU.not_equal))
                    run(V.tensor_scalar(d_pen, d_adj, 0.0, MASKED, ALU.is_equal, ALU.mult))
                    after()
                    run(V.scalar_tensor_tensor(d_bias, d_adj, gb[:], d_pen, ALU.mult, ALU.add), d_a_read, d.count(b, 1, 1))
                    for work, h in ((masked, 0), (masked, 1), (biased, 0), (masked, 2), (biased, 1), (block_max, 0),
                                    (masked, 3), (biased, 2), (block_max, 1), (biased, 3), (block_max, 2), (block_max, 3)):
                        after(2)
                        if work is masked:
                            work(b, h)
                        else:
                            work(h)
                    if last_block is not None:
                        accumulate(last_block)
                    after()
                    run(V.scalar_tensor_tensor(d_new[:], d_bmax[:], -1.0, d_old[:], ALU.mult, ALU.min))
                    after()
                    run(V.tensor_tensor(d_fall[:], d_new[:], d_old[:], ALU.subtract), d_max_ready, d.count(b, 1, 1))
                    after()
                    run(V.tensor_copy(d_old[:], d_new[:]))

                def accumulate(b):
                    dve.wait_ge(d_exped, d.count(b, HEADS, HEADS))
                    after()
                    run(V.tensor_tensor(d_sum[:], d_sum[:], d_fell[:], ALU.mult))
                    run(V.tensor_tensor(heads(d_out[:]), heads(d_out[:]), wide(d_fell[:], HD), ALU.mult))
                    after(2)
                    run(V.tensor_tensor(d_sum[:], d_sum[:], d_part[:], ALU.add))
                    after(2)
                    dve.wait_ge(d_weighed, d.count(b, 1, 1))
                    run(V.tensor_tensor(d_out[:], d_out[:], b_sum[:, 0:D], ALU.add), d_added, d.count(b, 1, 1))

                block_scores(0)
                block_scores(1, 0)
                with counted_loop(DENSE_BLOCKS - 2, BLOCK_STEPS) as b:
                    block_scores(b + 2, b + 1)
                accumulate(DENSE_BLOCKS - 1)
                after()
                base = d.turns
                do(base, FINISH, "rden", lambda: V.reciprocal(rden[:], d_sum[:]))
                do(base, FINISH, "att", lambda: V.tensor_tensor(heads(att[:]), heads(d_out[:]), wide(rden[:], HD), ALU.mult))
                do(base, FINISH, "add_x", lambda: V.tensor_tensor(y[:], proj_ps, d_x[:], ALU.add))
                do(base, FINISH, "add_b", lambda: V.tensor_tensor(y[:], y[:], b_out_sb[:], ALU.add))
                do(base, FINISH, "stats", lambda: V.bn_stats(stats[:], y[:]))
                aggregate(base, FINISH)
                newton_steps(base, FINISH)
                do(base, FINISH, "x1", lambda: V.tensor_scalar(x1[:], y[:], mv[:, 0:1], rstd[:], ALU.subtract, ALU.mult))
                do(base, FINISH, "add_bm", lambda: V.tensor_tensor(d_msg[:], msg_ps, b_msg_sb[:], ALU.add))
                do(base, FINISH, "keep", lambda: V.tensor_copy(z[:, d.z_index, :], x1[:]))

            BLOCK_STEPS = 15
            DENSE_STEPS = 3 + (BLOCK_STEPS - 3) + BLOCK_STEPS * (DENSE_BLOCKS - 1) + 3

            def flagged_counted(work, steps, own):
                def counted_work(t):
                    with counting(t, steps, lambda _: (step, steps_done())):
                        work(t)
                flagged(dve, counted_work, own + [(step, steps, made[0] - steps)])
                made[0] += TILES * steps
                history[:] = [(step, made[0])] * 8

            after()
            dense(first_tile)
            for n, (src, limit) in enumerate(((ends, EDGES), (found, SLOTS), (left, 0), (last_code, 0))):
                after()
                if n == 0:
                    run(V.tensor_scalar(row_flags[:], src[:], float(limit), None, ALU.is_gt))
                else:
                    run(V.scalar_tensor_tensor(row_flags[:], src[:], float(limit), row_flags[:], ALU.is_gt, ALU.add))
            after()
            run(V.scalar_tensor_tensor(row_flags[:], diag_adj[:], 0.0, row_flags[:], ALU.is_equal, ALU.add), flags_summed, 1)
            dve.wait_ge(flags_summed, 2)
            run(V.tensor_copy(flags[:, 0:TILES], b_edge[:, 0:TILES]))
            run(V.tensor_reduce(flag_part[:, 0:1], b_edge[:, 0:TILES], AX_X, ALU.add))
            after()
            run(V.tensor_copy(flags[:, TILES:TILES + 1], flag_part[:, 0:1]), flags_ready, 1)
            after()
            flagged_counted(lambda t: dense(tile_1(t)), DENSE_STEPS,
                            [(d_a_read, DENSE_BLOCKS), (d_masked, HEADS * DENSE_BLOCKS), (d_max_ready, DENSE_BLOCKS),
                             (d_added, DENSE_BLOCKS)])
            run(V.memset(flag_part[:], 0.0))

            weights(edge_w[:].rearrange("p t g -> p (t g)"), edge_adj[:].rearrange("p t g -> p (t g)"), 2)

            def members(t):
                if t.at_least(2):
                    dve.wait_ge(l2_sum, t.affine(1, -1))
                for g in range(GROUPS):
                    after(2)
                    ins = V.tensor_scalar(memw[:, t.parity, g, :], row_no[:], row_of[:, t.index(), g:g + 1],
                                          edge_w[:, t.index(), g:g + 1], ALU.is_equal, ALU.mult)
                    if g < GROUPS - 1:
                        run(ins)
                    else:
                        run(ins, l2_memw, t.affine(1, 1))

            def rows2(t):
                dve.wait_ge(l2_sum, t.affine(1, 1))
                if t.at_least(2):
                    dve.wait_ge(s_out[t.parity], t.of_parity(16, 0))
                after()
                run(V.tensor_tensor(y[:], code[t.parity][:, 0:D], z[:, t.index(), :], ALU.add))
                after()
                run(V.bn_stats(stats[:], y[:]))
                after()
                unfused()
                run(V.bn_aggr(mv[:], stats[:]), l2_y, t.affine(1, 1))

            def norm2(t):
                dve.wait_ge(l2_rstd, t.affine(2, 2))
                newton()
                after()
                run(V.tensor_scalar(y2[:, t.parity, :], y[:], mv[:, 0:1], rstd[:], ALU.subtract, ALU.mult), l2_out, t.affine(1, 1))

            def tile2(t):
                rows2(t)
                if t.pair is not None or t.n + 1 < TILES:
                    members(Tile(t.pair, t.n + 1))
                norm2(t)

            after()
            members(Tile(None, 0))
            tile2(Tile(None, 0))
            after()
            run(V.tensor_copy(t1[:], r0[:]))
            with counted_loop((TILES - 1) // 2 - 1, 2 * STEPS2) as pair:
                for u in range(2):
                    tile2(Tile(pair, 1 + u))
                    after()
                    run(V.tensor_copy(t1[:], r0[:]))
            for i in range(TILES - 2, TILES):
                tile2(Tile(None, i))

            def dense2(d):
                reached(dve, turn, d.turns)
                run(V.tensor_copy(y[:], z[:, d.z_index, :]))

                def block_weights(b, last_block=None):
                    after()
                    dve.wait_ge(e_a_in, d.count(b, 16, 16))
                    run(V.tensor_scalar(d_pen, d_adj, 0.0, None, ALU.is_equal))
                    after()
                    run(V.tensor_tensor(d_on, d_adj, d_pen, ALU.add))
                    after()
                    run(V.reciprocal(d_on, d_on))
                    after()
                    run(V.tensor_scalar(d_on, d_on, -1.0, None, ALU.add))
                    after()
                    run(V.tensor_tensor(d_on, d_on, d_on, ALU.mult), e_squared, d.count(b, 1, 1))
                    run(V.scalar_tensor_tensor(d_pen, d_adj, 1.0, d_pen, ALU.is_lt, ALU.subtract), e_a_read, d.count(b, 1, 1))
                    if last_block is not None:
                        add(last_block)
                    dve.wait_ge(e_exped, d.count(b, 1, 1))
                    after()
                    run(V.tensor_tensor(d_w, d_e, d_pen, ALU.mult), e_weight, d.count(b, 1, 1))

                def add(b):
                    dve.wait_ge(e_weighed, d.count(b, 1, 1))
                    after()
                    run(V.tensor_tensor(y[:], y[:], b_sum[:, 0:D], ALU.add), e_added, d.count(b, 1, 1))

                block_weights(0)
                block_weights(1, 0)
                with counted_loop(DENSE_BLOCKS - 2, 4, last=lambda b: (e_weight, d.count(b, 1, 2))) as b:
                    block_weights(b + 2, b + 1)
                add(DENSE_BLOCKS - 1)
                after()
                base = d.turns
                do(base, FINISH_2, "stats", lambda: V.bn_stats(stats[:], y[:]))
                aggregate(base, FINISH_2)
                newton_steps(base, FINISH_2)
                do(base, FINISH_2, "out", lambda: V.tensor_scalar(d_msg[:], y[:], mv[:, 0:1], rstd[:], ALU.subtract, ALU.mult))

            after()
            dense2(first_tile_2)
            flagged_counted(lambda t: dense2(tile_2(t)), 1 + 4 * DENSE_BLOCKS,
                            [(e_squared, DENSE_BLOCKS), (e_a_read, DENSE_BLOCKS), (e_weight, DENSE_BLOCKS), (e_added, DENSE_BLOCKS)])

        return


_INS = ["x", "adj", "L0_gnn_Wqkv", "L0_gnn_bqkv", "L0_gnn_Wout", "L0_gnn_bout", "L0_gnn_graph_bias", "L1_gnn_W", "L1_gnn_B"]
_OUTS = [((N, D), "float32")]


def kernel(**inputs):
    import numpy as _np
    import concourse.bacc as _bacc
    from concourse import mybir as _mybir
    from concourse.bass_utils import run_bass_kernel_spmd as _run

    nc = _bacc.Bacc("TRN2", target_bir_lowering=False, num_devices=1)
    arrays, args = {}, []
    for name in _INS:
        a = _np.ascontiguousarray(inputs[name])
        arrays[f"in_{name}_dram"] = a
        args.append(nc.dram_tensor(f"in_{name}_dram", a.shape, _mybir.dt.from_np(a.dtype), kind="ExternalInput").ap())
    for i, (shape, dtype) in enumerate(_OUTS):
        dt = _mybir.dt.from_np(_np.dtype(dtype))
        args.append(nc.dram_tensor(f"out_{i}_dram", shape, dt, kind="ExternalOutput").ap())
    build(nc, *args)
    r = _run(nc, [arrays], core_ids=[0])
    return r.results[0]["out_0_dram"]
```

```python
from contextlib import ExitStack, contextmanager

import concourse.bass as bass
from concourse import mybir

ALU = mybir.AluOpType
ACT = mybir.ActivationFunctionType
BF16 = mybir.dt.bfloat16
F32 = mybir.dt.float32
U32 = mybir.dt.uint32
AX_X = mybir.AxisListType.X

P = 128
N = 8192
D = 128
HEADS = 4
HD = D // HEADS
SCALE = float(HD) ** -0.5
EPS = 1e-5
MASKED = -1e9
SIGMA = 0.5

TILES = (N - P) // P
BLOCKS = 16
FOLD = N // BLOCKS
QUARTERS = 4
QW = N // QUARTERS
SLOTS = 16
GROUPS = 3
EDGES = GROUPS * P
EXPONENT = 0x7F800000


CHUNKS = 4
DENSE_COLS = CHUNKS * P
DENSE_BLOCKS = N // DENSE_COLS
POOL_HEADS = 2
FINISH = ("rden", "att", "turn_att", "copy_att", "project", "add_x", "add_b", "stats", "aggr", "ln", "r0",
          "n1", "n2", "n3", "n4", "x1", "turn_x1", "copy_x1", "message", "add_bm", "keep")
FINISH_2 = ("stats", "aggr", "ln", "r0", "n1", "n2", "n3", "n4", "out")


class Dense:

    def __init__(self, no, z_index, turns, adj_, x_=None, q_=None, msg_=None, out_=None):
        self.no, self.z_index, self.turns = no, z_index, turns
        self.adj, self.x, self.q, self.msg, self.out = adj_, x_, q_, msg_, out_

    def count(self, b, per_block, plus):
        return (self.no * DENSE_BLOCKS + b) * per_block + plus


class Tile:

    def __init__(self, turn, n, per=2):
        self.turn, self.n, self.per = turn, n, per
        self.parity, self.place = n % 2, n % 4

    def affine(self, per_tile, plus):
        c = self.n * per_tile + plus
        return c if self.turn is None else self.turn * (self.per * per_tile) + c

    def index(self):
        return self.affine(1, 0)

    def of_ring(self, ring, per_tile, plus):
        c = (self.n // ring) * per_tile + plus
        return c if self.turn is None else self.turn * (self.per // ring * per_tile) + c

    def of_parity(self, per_tile, plus):
        return self.of_ring(2, per_tile, plus)

    def at_least(self, n):
        return self.turn is not None or self.n >= n

    def after(self, n):
        return None if self.turn is None and not 0 <= self.n + n < TILES else Tile(self.turn, self.n + n, self.per)


def build(nc, x, adj, w_qkv, b_qkv, w_out, b_out, graph_bias, w_msg, b_msg, out):
    q_dram = nc.dram_tensor("q_table", (N, D), F32, kind="Internal").ap()
    kv_dram = nc.dram_tensor("kv_table", (N, 2 * D), F32, kind="Internal").ap()
    msg_dram = nc.dram_tensor("msg_table", (N, D), F32, kind="Internal").ap()
    adj_flat = adj.rearrange("a (b c) -> (a b) c", c=1)

    def rows(dram):
        return dram[P:N, :].rearrange("(p t) d -> t p d", t=TILES)

    def by_partition(dram):
        return dram[P:N, :].rearrange("(p t) d -> p t d", t=TILES)

    adj_rows, x_rows, q_rows, kv_rows, msg_rows, out_rows = map(rows, (adj, x, q_dram, kv_dram, msg_dram, out))

    with ExitStack() as ctx:
        def sb(name, shape, dt=F32):
            return ctx.enter_context(nc.sbuf_tensor(name, shape, dt))

        def bank(name):
            return ctx.enter_context(nc.psum_tensor(name, [P, 512], F32))

        def sem(name):
            return ctx.enter_context(nc.semaphore(name))

        STORES = 4
        ident = sb("ident", [P, P])
        power = sb("power", [P, BLOCKS, P], BF16)
        before = sb("before", [P, P])
        edge_no = sb("edge_no", [P, EDGES])
        row_no = sb("row_no", [P, P])
        slot_no = sb("slot_no", [P, GROUPS, SLOTS])
        edge_col = sb("edge_col", [P, GROUPS])
        own_col = sb("own_col", [P, TILES])
        ones = sb("ones", [P, P])
        row_first = sb("row_first", [P, TILES])
        epsc = sb("epsc", [P, 1])
        minus_one = sb("minus_one", [P, 1])
        w_qkv_sb = sb("w_qkv_sb", [P, 3 * D])
        b_qkv_sb = sb("b_qkv_sb", [P, 3 * D])
        w_out_sb = sb("w_out_sb", [P, D])
        b_out_sb = sb("b_out_sb", [P, D])
        w_msg_sb = sb("w_msg_sb", [P, D])
        b_msg_sb = sb("b_msg_sb", [P, D])
        gb = sb("gb", [P, 1])
        diag_adj = sb("diag_adj", [P, TILES])
        neg_gb_diag = sb("neg_gb_diag", [P, TILES])
        diag_w = sb("diag_w", [P, TILES])
        wtmp = sb("wtmp", [P, TILES * GROUPS])
        wtmp2 = sb("wtmp2", [P, TILES * GROUPS])
        row_of = sb("row_of", [P, TILES, GROUPS])
        edge_adj = sb("edge_adj", [P, TILES, GROUPS])
        edge_w = sb("edge_w", [P, TILES, GROUPS])
        cols_all = sb("cols_all", [P, TILES, GROUPS], U32)
        ends = sb("ends", [P, TILES])
        found = sb("found", [P, TILES])
        nonzeros = sb("nonzeros", [P, TILES, QUARTERS])
        all_found = sb("all_found", [P, TILES])
        z = sb("z", [P, TILES + 1, D])
        a_ring = sb("a_ring", [P, 2, N])
        present = sb("present", [P, QUARTERS, QW], BF16)
        code_left = sb("code_left", [P, FOLD])
        c8 = sb("c8", [P, SLOTS])
        m8 = sb("m8", [P, SLOTS], U32)
        bits = sb("bits", [P, 2, SLOTS], U32)
        rest = sb("rest", [P, SLOTS])
        expo = sb("expo", [P, 2, SLOTS], U32)
        key = sb("key", [P, 2, SLOTS])
        cand = sb("cand", [P, 2, SLOTS])
        cand_left = sb("cand_left", [P, 2, SLOTS])
        taken = sb("taken", [P, 2, SLOTS])
        rowinfo = sb("rowinfo", [P, 2, SLOTS + 2])
        starts = sb("starts", [P, EDGES])
        member = sb("member", [P, 2, EDGES])
        slot = sb("slot", [P, GROUPS])
        is_slot = sb("is_slot", [P, 2, GROUPS, SLOTS])
        picked = sb("picked", [P, GROUPS, SLOTS])
        keys = sb("keys", [P, GROUPS])
        row_start = sb("row_start", [P, GROUPS], U32)
        cols = sb("cols", [P, 2, GROUPS], U32)
        flat = sb("flat", [P, 2, GROUPS], U32)
        empty = sb("empty", [P, 2, SLOTS])
        q_own = sb("q_own", [P, 2, D])
        v_own = sb("v_own", [P, 2, D])
        kv_edge = sb("kv_edge", [P, 2, GROUPS, 2 * D])
        adj_edge = sb("adj_edge", [P, 2, GROUPS])
        diag_prod = sb("diag_prod", [P, 2, D])
        neg_diag = sb("neg_diag", [P, TILES, HEADS])
        prod = sb("prod", [P, GROUPS, D])
        psum_ = sb("psum_", [P, GROUPS, HEADS])
        pen = sb("pen", [P, GROUPS])
        bias = sb("bias", [P, GROUPS])
        score = sb("score", [P, GROUPS, HEADS])
        by_slot = sb("by_slot", [P, GROUPS, HEADS, SLOTS])
        member_t = sb("member_t", [P, GROUPS, P])
        slotted = sb("slotted", [P, HEADS, SLOTS])
        rowmax = sb("rowmax", [P, HEADS])
        neg_max = sb("neg_max", [P, HEADS])
        shifted = sb("shifted", [P, GROUPS, HEADS])
        shifted_d = sb("shifted_d", [P, HEADS])
        weighted = sb("weighted", [P, GROUPS, D + HEADS])
        prob_d = sb("prob_d", [P, 2, HEADS])
        pv_d = sb("pv_d", [P, D])
        resid = sb("resid", [P, D])
        num = sb("num", [P, D])
        den = sb("den", [P, HEADS])
        rden = sb("rden", [P, HEADS])
        att = sb("att", [P, D])
        att_t = sb("att_t", [P, D])
        y = sb("y", [P, D])
        stats = sb("stats", [P, 6])
        mv = sb("mv", [P, 2])
        lnv = sb("lnv", [P, 1])
        r0 = sb("r0", [P, 1])
        t1 = sb("t1", [P, 1])
        t2 = sb("t2", [P, 1])
        rstd = sb("rstd", [P, 1])
        x1 = sb("x1", [P, D])
        x1_t = sb("x1_t", [P, D])
        msg = sb("msg", [P, 2, D])
        qkv = sb("qkv", [P, STORES, 4, 3 * D])
        x_t = sb("x_t", [P, 2, P])
        cols2 = sb("cols2", [P, 4, GROUPS], U32)
        y_round = sb("y_round", [P, 4, D])
        y2 = sb("y2", [P, 4, D])
        stats_round = sb("stats_round", [P, 4, 6])
        mv_round = sb("mv_round", [P, 4, 2])
        lnv_round, r0_round, t1_round, t2_round, rstd_round = (sb(n + "_round", [P, 4]) for n in ("lnv", "r0", "t1", "t2", "rstd"))
        shift_round = sb("shift_round", [P, 4])

        room = a_ring[:].rearrange("p a n -> p (a n)")
        carved = [0]

        def carve(columns):
            carved[0] += columns
            return room[:, carved[0] - columns:carved[0]]

        d_s = carve(HEADS * DENSE_COLS).rearrange("p (h n) -> p h n", h=HEADS)
        d_p = carve(HEADS * DENSE_COLS).rearrange("p (h n) -> p h n", h=HEADS)
        d_pt = carve(HEADS * DENSE_COLS).rearrange("p (h c r) -> p h c r", h=HEADS, c=CHUNKS)
        d_adj = carve(DENSE_COLS)
        d_on = carve(DENSE_COLS)
        d_pen = carve(DENSE_COLS)
        d_bias = carve(DENSE_COLS)
        d_kt = carve(DENSE_COLS)
        d_k = carve(CHUNKS * D).rearrange("p (c d) -> p c d", c=CHUNKS)
        d_v = carve(CHUNKS * D).rearrange("p (c d) -> p c d", c=CHUNKS)
        d_e = carve(DENSE_COLS)
        d_w = carve(DENSE_COLS)
        msg_edge = carve(4 * GROUPS * D).rearrange("p (t g d) -> p t g d", t=4, g=GROUPS)
        memw = carve(4 * GROUPS * P).rearrange("p (t g r) -> p t g r", t=4, g=GROUPS)
        d_q = sb("d_q", [P, D])
        d_x = sb("d_x", [P, D])
        d_qh = sb("d_qh", [P, HEADS, P])
        d_bmax = sb("d_bmax", [P, HEADS])
        d_new = sb("d_new", [P, HEADS])
        d_old = sb("d_old", [P, HEADS])
        d_fall = sb("d_fall", [P, HEADS])
        d_fell = sb("d_fell", [P, HEADS])
        d_sum = sb("d_sum", [P, HEADS])
        d_part = sb("d_part", [P, HEADS])
        d_out = sb("d_out", [P, D])
        d_msg = sb("d_msg", [P, D])
        row_flags = sb("row_flags", [P, TILES])
        flag_part = sb("flag_part", [P, TILES])
        flags = sb("flags", [P, TILES + 1], U32)

        code = [bank("code0"), bank("code1")]
        b_edge = bank("b_edge")
        q_edge = [bank("q_edge0"), bank("q_edge1")]
        b_max = bank("b_max")
        b_sum = bank("b_sum")
        b_fin = bank("b_fin")
        score_bank = code + q_edge
        p_bank = [b_max, b_fin]
        sum_bank = code + q_edge
        info_e = b_edge[:, 16:16 + GROUPS * (SLOTS + 2)].rearrange("p (g s) -> p g s", g=GROUPS)
        first_ps = b_edge[:, 0:1]
        slot_ps = b_max[:, 0:HEADS * SLOTS]
        max_ps = b_max[:, 64:64 + GROUPS * HEADS]
        member_ps = b_max[:, P:P + GROUPS * P]
        att_ps, proj_ps, x1_ps, msg_ps = (b_fin[:, n * P:(n + 1) * P] for n in range(4))

        s_const = sem("s_const")
        s_cstep = sem("s_cstep")
        s_loaded = sem("s_loaded")
        s_xall = [sem(f"s_xall{c}") for c in range(4)]
        s_powers = sem("s_powers")
        s_diag = sem("s_diag")
        s_diag2 = sem("s_diag2")
        s_xt = sem("s_xt")
        s_xtc = sem("s_xtc")
        s_qkv = sem("s_qkv")
        s_qkvb = sem("s_qkvb")
        s_stored = [sem(f"s_stored{n}") for n in range(STORES)]
        s_adj = [[sem(f"s_adj{i}{h}") for h in range(2)] for i in range(2)]
        s_q = [sem("s_q0"), sem("s_q1")]
        s_v = [sem("s_v0"), sem("s_v1")]
        signed = sem("signed")
        folded = sem("folded")
        step = sem("step")
        code_free = sem("code_free")
        member_turned = sem("member_turned")
        member_copied = sem("member_copied")
        adj_kept = sem("adj_kept")
        passed_dve = sem("passed_dve")
        passed_pool = sem("passed_pool")
        passed_sp = sem("passed_sp")
        counted = sem("counted")
        first_ready = sem("first_ready")
        first_copied = sem("first_copied")
        starts_ready = sem("starts_ready")
        member_ready = sem("member_ready")
        info_sent = sem("info_sent")
        q_sent = sem("q_sent")
        idx_ready = sem("idx_ready")
        s_kv = [sem("s_kv0"), sem("s_kv1")]
        s_val = [sem("s_val0"), sem("s_val1")]
        diag_ready = sem("diag_ready")
        diag_summed = sem("diag_summed")
        q_read = sem("q_read")
        by_slot_ready = sem("by_slot_ready")
        slots_sent = sem("slots_sent")
        max_ready = sem("max_ready")
        max_sent = sem("max_sent")
        shift_ready = sem("shift_ready")
        exped = sem("exped")
        weighted_ready = sem("weighted_ready")
        summed = sem("summed")
        pool_fin = sem("pool_fin")
        pool_copy = sem("pool_copy")
        att_ready = sem("att_ready")
        att_turned = sem("att_turned")
        att_copied = sem("att_copied")
        projected = sem("projected")
        stats_ready = sem("stats_ready")
        rstd_step = sem("rstd_step")
        x1_ready = sem("x1_ready")
        x1_turned = sem("x1_turned")
        x1_copied = sem("x1_copied")
        msg_made = sem("msg_made")
        msg_ready = sem("msg_ready")
        s_msg = [sem("s_msg0"), sem("s_msg1")]
        w_squared = sem("w_squared")
        w_exped = sem("w_exped")
        l2_cols = sem("l2_cols")
        l2_in = [sem(f"l2_in{n}") for n in range(4)]
        l2_memw = sem("l2_memw")
        l2_sum = sem("l2_sum")
        l2_y = sem("l2_y")
        l2_shift = sem("l2_shift")
        l2_rstd = sem("l2_rstd")
        l2_out = sem("l2_out")
        s_out = sem("s_out")
        turn = sem("turn")
        d_qx_in = sem("d_qx_in")
        d_a_in = sem("d_a_in")
        d_k_in = sem("d_k_in")
        d_v_in = sem("d_v_in")
        d_q_turned = sem("d_q_turned")
        d_q_copied = sem("d_q_copied")
        d_k_turned = sem("d_k_turned")
        d_k_copied = sem("d_k_copied")
        d_scored = sem("d_scored")
        d_a_read = sem("d_a_read")
        d_masked = sem("d_masked")
        d_biased = sem("d_biased")
        d_max_ready = sem("d_max_ready")
        d_fell_ready = sem("d_fell_ready")
        d_exped = sem("d_exped")
        d_p_turned = sem("d_p_turned")
        d_p_copied = sem("d_p_copied")
        d_weighed = sem("d_weighed")
        d_added = sem("d_added")
        e_a_in = sem("e_a_in")
        e_m_in = sem("e_m_in")
        e_inverted = sem("e_inverted")
        e_squared = sem("e_squared")
        e_a_read = sem("e_a_read")
        e_exped = sem("e_exped")
        e_weight = sem("e_weight")
        e_turned = sem("e_turned")
        e_copied = sem("e_copied")
        e_weighed = sem("e_weighed")
        e_added = sem("e_added")
        d_stored = sem("d_stored")
        flags_summed = sem("flags_summed")
        flags_ready = sem("flags_ready")

        HELD = 6
        LOOP_FROM, PAIRS = HELD, (TILES - HELD) // 2 - 1
        LAST = TILES + HELD - 1

        def active(it):
            return [Tile(it.turn, it.n - k) if it.turn is not None or 0 <= it.n - k < TILES else None
                    for k in range(HELD)]

        def iterations(eng, body):
            for i in range(LOOP_FROM):
                body(active(Tile(None, i)))
            with eng.Fori(0, PAIRS) as pair:
                for u in range(2):
                    body(active(Tile(pair, LOOP_FROM + u)))
            for i in range(LOOP_FROM + 2 * PAIRS, LAST):
                body(active(Tile(None, i)))

        def before_step(eng, base, names, name):
            at = base + names.index(name)
            if not isinstance(at, int) or at > 0:
                eng.wait_ge(turn, at)

        def reached(eng, s, at_least):
            if not isinstance(at_least, int) or at_least > 0:
                eng.wait_ge(s, at_least)

        def heads(ap):
            return ap.rearrange("p (h d) -> p h d", h=HEADS)

        first_tile = Dense(0, TILES, 0, adj[0:P, :], x[0:P, :], q_dram[0:P, :], msg_dram[0:P, :])
        first_tile_2 = Dense(0, TILES, len(FINISH) * (TILES + 1), adj[0:P, :], out_=out[0:P, :])

        def tile_1(t):
            return Dense(t + 1, t, len(FINISH) * t + len(FINISH), adj_rows[t], x_rows[t], q_rows[t], msg_rows[t])

        def tile_2(t):
            return Dense(t + 1, t, len(FINISH_2) * t + (len(FINISH) * (TILES + 1) + len(FINISH_2)), adj_rows[t], out_=out_rows[t])

        def tables_stored(eng):
            for n, stored in enumerate(s_stored):
                eng.wait_ge(stored, 2 * 16 * (N // P // 4 // STORES + (n == STORES - 1)))

        def messages_stored(eng):
            eng.wait_ge(s_msg[0], 16 * ((TILES + 1) // 2))
            eng.wait_ge(s_msg[1], 16 * (TILES // 2))
            eng.wait_ge(d_stored, 16)
            eng.wait_ge(flags_ready, 1)
            eng.wait_ge(d_stored, 16 * (TILES + 1))

        def flagged(eng, work, own, first=True):
            def skip(done, tiles):
                for s, amount, *begun in own:
                    eng.wait_ge(s, amount * done + sum(begun))
                    eng.sem_inc(s, amount * tiles)

            with eng.If(eng.value_load(flags[0:1, TILES:TILES + 1], min_val=0, max_val=N) > 0):
                with eng.Fori(0, TILES) as t:
                    with eng.If(eng.value_load(flags[0:1, bass.ds(t, 1)], min_val=0, max_val=N) > 0):
                        work(t)
                    with eng.Else():
                        skip(t + 1, 1)
            with eng.Else():
                skip(1, TILES)

        RING2 = 4
        PER_ROUND = 4

        def rounds(body, looped):
            body(0, [Tile(None, u) for u in range(PER_ROUND)])
            with looped(DENSE_BLOCKS - 3) as r:
                body(r + 1, [Tile(r, PER_ROUND + u, PER_ROUND) for u in range(PER_ROUND)])
            for j in (DENSE_BLOCKS - 2, DENSE_BLOCKS - 1):
                body(j, [Tile(None, n) for n in range(PER_ROUND * j, min(PER_ROUND * j + PER_ROUND, TILES))])

        def ahead(t):
            first = [t.after(n) for n in range(RING2 - 1)] if t.turn is None and t.n == 0 else []
            return [a for a in first + [t.after(RING2 - 1)] if a]

        block = ctx.enter_context(nc.Block())
        NBLK = N // P
        X_CHUNKS = 4

        @block.sync
        def _(sp):
            def load_constants():
                for dst, src in ((w_qkv_sb, w_qkv), (w_out_sb, w_out), (w_msg_sb, w_msg)):
                    sp.dma_start(dst[:], src).then_inc(s_loaded, 16)
                for dst, src in ((b_qkv_sb, b_qkv), (b_out_sb, b_out), (b_msg_sb, b_msg)):
                    sp.dma_start(dst[:], src.rearrange("(a n) -> a n", a=1).to_broadcast([P, src.shape[0]])).then_inc(s_loaded, 16)
                sp.dma_start(gb[:], graph_bias.rearrange("a b c -> (a b) c").to_broadcast([P, 1])).then_inc(s_loaded, 16)

            for c in range(X_CHUNKS):
                cut = slice(c * NBLK // X_CHUNKS, min((c + 1) * NBLK // X_CHUNKS, TILES))
                sp.dma_start(z[:, cut, :], by_partition(x)[:, cut, :]).then_inc(s_xall[c], 16)
                if c == 0:
                    load_constants()
            sp.dma_start(z[:, TILES, :], x[0:P, :]).then_inc(s_xall[-1], 16)

            def load_adj(t, h):
                sp.dma_start(a_ring[:, t.parity, h * (N // 2):(h + 1) * (N // 2)],
                             adj_rows[t.index()][:, h * (N // 2):(h + 1) * (N // 2)]).then_inc(s_adj[t.parity][h], 16)

            for g in range(NBLK // 4):
                sp.wait_ge(s_qkvb, 4 * g + 4)
                n = min(4, TILES - 4 * g)
                for dram, first, last in ((q_dram, 0, D), (kv_dram, D, 3 * D)):
                    sp.dma_start(by_partition(dram)[:, 4 * g:4 * g + n, :], qkv[:, g % STORES, 0:n, first:last]
                                 ).then_inc(s_stored[g % STORES], 16)
                    if n < 4:
                        sp.dma_start(dram[0:P, :], qkv[:, g % STORES, n, first:last]).then_inc(s_stored[g % STORES], 16)
                if g == 0:
                    diagonal = bass.AP(tensor=adj.tensor, offset=P * (N + 1), ap=[[TILES * (N + 1), P], [N + 1, TILES]])
                    with nc.allow_non_contiguous_dma(reason="one number of every row"):
                        sp.dma_start(diag_adj[:], diagonal).then_inc(s_diag, 16)
                if g in (2, 5, 8, 11):
                    load_adj(Tile(None, (g // 3) // 2), (g // 3) % 2)
            tables_stored(sp)

            def body(at):
                t = at[0]
                if t:
                    load_ahead(t, 0)
                t = at[3]
                if t:
                    if t.at_least(2):
                        sp.wait_ge(pool_fin, t.affine(2, -2))
                    sp.dma_start(v_own[:, t.parity, :], kv_rows[t.index()][:, D:2 * D]).then_inc(s_v[t.parity], 16)
                if at[5]:
                    store_msg(at[5])
                if at[0]:
                    load_ahead(at[0], 1)
                t = at[0]
                if t:
                    if t.at_least(2):
                        sp.wait_ge(q_sent, t.affine(1, -1))
                    sp.dma_start(q_own[:, t.parity, :], q_rows[t.index()]).then_inc(s_q[t.parity], 16)

            def load_ahead(t, h):
                if not (t.turn is None and t.n + 2 >= TILES):
                    sp.wait_ge(signed, t.affine(QUARTERS, 2 * h + 2))
                    load_adj(Tile(t.turn, t.n + 2), h)

            def store_msg(t):
                sp.wait_ge(msg_ready, t.affine(1, 1))
                sp.dma_start(msg_rows[t.index()], msg[:, t.parity, :]).then_inc(s_msg[t.parity], 16)

            iterations(sp, body)

            def dense(d):
                def load_a_k(b):
                    reached(sp, d_a_read, d.count(b, 1, 0))
                    sp.dma_start(d_adj, d.adj[:, bass.ds(b * DENSE_COLS, DENSE_COLS)]).then_inc(d_a_in, 16)
                    reached(sp, d_k_turned, d.count(b, 1, 0))
                    sp.dma_start(d_k, kv_dram[bass.ds(b * DENSE_COLS, DENSE_COLS), 0:D].rearrange("(c p) d -> p c d", p=P)
                                 ).then_inc(d_k_in, 16)

                def load_v(b):
                    reached(sp, d_weighed, d.count(b, 1, 0))
                    sp.dma_start(d_v, kv_dram[bass.ds(b * DENSE_COLS, DENSE_COLS), D:2 * D].rearrange("(c p) d -> p c d", p=P)
                                 ).then_inc(d_v_in, 16)

                sp.dma_start(d_q[:], d.q).then_inc(d_qx_in, 16)
                sp.dma_start(d_x[:], d.x).then_inc(d_qx_in, 16)
                for b in range(3):
                    load_a_k(b)
                load_v(0)
                with sp.Fori(0, DENSE_BLOCKS - 3) as b:
                    load_a_k(b + 3)
                    load_v(b + 1)
                for b in (DENSE_BLOCKS - 2, DENSE_BLOCKS - 1):
                    load_v(b)
                sp.wait_ge(turn, d.turns + len(FINISH))
                sp.dma_start(d.msg, d_msg[:]).then_inc(d_stored, 16)
                sp.wait_ge(d_stored, 16 * d.no + 16)
                sp.sem_inc(passed_sp, 1)

            sp.wait_ge(signed, TILES * QUARTERS)
            dense(first_tile)
            sp.wait_ge(flags_ready, 1)
            sp.wait_ge(s_msg[0], 16 * ((TILES + 1) // 2))
            sp.wait_ge(s_msg[1], 16 * (TILES // 2))
            flagged(sp, lambda t: dense(tile_1(t)),
                    [(d_qx_in, 32), (d_a_in, 16 * DENSE_BLOCKS), (d_k_in, 16 * DENSE_BLOCKS), (d_v_in, 16 * DENSE_BLOCKS),
                     (d_stored, 16), (turn, len(FINISH))])

            def store_out(j, tiles):
                n = len(tiles)
                sp.wait_ge(l2_out, tiles[-1].affine(1, 1))
                sp.dma_start(out_rows[bass.ds(tiles[0].index(), n)].rearrange("t p d -> p t d"), y2[:, 0:n, :]).then_inc(s_out, 16)

            def load_a(d, b):
                reached(sp, e_a_read, d.count(b, 1, 0))
                sp.dma_start(d_adj, d.adj[:, bass.ds(b * DENSE_COLS, DENSE_COLS)]).then_inc(e_a_in, 16)

            def load_m(d, b):
                reached(sp, e_weighed, d.count(b, 1, 0))
                sp.dma_start(d_v, msg_dram[bass.ds(b * DENSE_COLS, DENSE_COLS), :].rearrange("(c p) d -> p c d", p=P)
                             ).then_inc(e_m_in, 16)

            def body2(j, tiles):
                load_m(first_tile_2, j)
                if tiles[0].n < PER_ROUND * (DENSE_BLOCKS - 1):
                    load_a(first_tile_2, j + 1)
                store_out(j, tiles)

            messages_stored(sp)
            load_a(first_tile_2, 0)
            rounds(body2, lambda count: sp.Fori(0, count))
            sp.wait_ge(s_out, 16 * DENSE_BLOCKS)

            def store_dense(d):
                sp.wait_ge(turn, d.turns + len(FINISH_2))
                sp.dma_start(d.out, d_msg[:]).then_inc(d_stored, 16)
                sp.wait_ge(d_stored, 16 * d.no + 16 * (TILES + 2))
                sp.sem_inc(passed_sp, 1)

            def dense2(d):
                load_a(d, 0)
                load_a(d, 1)
                load_m(d, 0)
                with sp.Fori(0, DENSE_BLOCKS - 2) as b:
                    load_a(d, b + 2)
                    load_m(d, b + 1)
                load_m(d, DENSE_BLOCKS - 1)
                store_dense(d)

            store_dense(first_tile_2)
            flagged(sp, lambda t: dense2(tile_2(t)),
                    [(e_a_in, 16 * DENSE_BLOCKS), (e_m_in, 16 * DENSE_BLOCKS), (d_stored, 16, 16 * (TILES + 1)),
                     (turn, len(FINISH_2), len(FINISH) * (TILES + 1))])

        @block.gpsimd
        def _(pool):
            done = [0]

            def const(ins):
                done[0] += 1
                ins.then_inc(s_cstep, 1)
                pool.wait_ge(s_cstep, done[0])

            const(nc.gpsimd.memset(ident[:], 0.0))
            const(nc.gpsimd.affine_select(out=ident[:], in_=ident[:], compare_op=ALU.not_equal, fill=1.0, base=0,
                                          pattern=[[-1, P]], channel_multiplier=1))
            const(nc.gpsimd.memset(before[:], 1.0))
            const(nc.gpsimd.affine_select(out=before[:], in_=before[:], compare_op=ALU.is_gt, fill=0.0, base=0,
                                          pattern=[[1, P]], channel_multiplier=-1))
            for dst, pattern, base, ch in ((edge_no[:], [[1, EDGES]], 1, 0), (row_no[:], [[1, P]], 1, 0),
                                           (slot_no[:], [[0, GROUPS], [1, SLOTS]], 0, 0), (edge_col[:], [[P, GROUPS]], 0, 1),
                                           (row_first[:], [[N, TILES]], (P - TILES) * N, 0),
                                           (own_col[:], [[1, TILES]], P + 1, TILES),
                                           (rowinfo[:, 0, SLOTS + 1:SLOTS + 2], [[1, 1]], 1, 1),
                                           (rowinfo[:, 1, SLOTS + 1:SLOTS + 2], [[1, 1]], 1, 1)):
                const(nc.gpsimd.iota(dst, pattern=pattern, base=base, channel_multiplier=ch, allow_small_or_imprecise_dtypes=True))
            const(nc.gpsimd.memset(ones[:], 1.0))
            const(nc.gpsimd.memset(minus_one[:], -1.0))
            nc.gpsimd.memset(epsc[:], EPS).then_inc(s_const, 1)
            pool.wait_ge(s_loaded, 16 * 7)

            for b in range(TILES):
                pool.wait_ge(s_qkvb, b + 1)
                if b >= 2:
                    pool.wait_ge(diag_summed, b - 1)
                own = qkv[:, b // 4 % STORES, b % 4, :]
                nc.gpsimd.tensor_tensor(diag_prod[:, b % 2, :], own[:, 0:D], own[:, D:2 * D], ALU.mult).then_inc(diag_ready, 1)
            tables_stored(pool)

            def body(at):
                t = at[2]
                if t:
                    pool.wait_ge(first_copied, t.affine(1, 1))
                    if t.at_least(1):
                        pool.wait_ge(member_ready, t.affine(1, 0))
                    pool.sem_inc(passed_pool, 1)
                    nc.gpsimd.tensor_scalar(starts[:], edge_no[:], rowinfo[:, t.parity, SLOTS:SLOTS + 1], None, ALU.is_gt
                                            ).then_inc(starts_ready, 1)
                t = at[4]
                if t:
                    pool.wait_ge(s_v[t.parity], t.of_parity(16, 16))
                    if t.at_least(1):
                        pool.wait_ge(att_ready, t.affine(1, 0))
                        pool.wait_ge(stats_ready, t.affine(1, 0))
                    pool.wait_ge(exped, t.affine(2, 2))
                    nc.gpsimd.tensor_tensor(heads(pv_d[:]), heads(v_own[:, t.parity, :]),
                                            prob_d[:, t.parity, :].unsqueeze(2).to_broadcast([P, HEADS, HD]),
                                            ALU.mult).then_inc(pool_fin, 1)
                    nc.gpsimd.tensor_tensor(resid[:], z[:, t.index(), :], b_out_sb[:], ALU.add).then_inc(pool_fin, 1)
                if t:
                    pool.wait_ge(s_val[t.parity], t.of_parity(16 * GROUPS, 16 * GROUPS))
                    nc.gpsimd.tensor_copy(edge_adj[:, t.index(), :], adj_edge[:, t.parity, :]).then_inc(adj_kept, 1)
                t = at[2]
                if t:
                    pool.wait_ge(idx_ready, t.affine(1, 1))
                    if t.at_least(2):
                        pool.wait_ge(weighted_ready, t.affine(1, -1))
                        pool.wait_ge(adj_kept, t.affine(1, -1))
                    pool.sem_inc(passed_pool, 1)
                    for g in range(GROUPS):
                        nc.gpsimd.indirect_dma_start(kv_edge[:, t.parity, g, :], None, kv_dram,
                                                     bass.IndirectOffsetOnAxis(ap=cols[:, t.parity, g:g + 1], axis=0)
                                                     ).then_inc(s_kv[t.parity], 16)
                    for g in range(GROUPS):
                        nc.gpsimd.indirect_dma_start(adj_edge[:, t.parity, g:g + 1], None, adj_flat,
                                                     bass.IndirectOffsetOnAxis(ap=flat[:, t.parity, g:g + 1], axis=0)
                                                     ).then_inc(s_val[t.parity], 16)
                    nc.gpsimd.tensor_copy(cols_all[:, t.index(), :], cols[:, t.parity, :]).then_inc(pool_copy, 1)
            iterations(pool, body)

            def dense(d):
                def block(b):
                    for h in range(POOL_HEADS):
                        pool.wait_ge(d_masked, d.count(b, HEADS, h + 1))
                        if h == 0:
                            pool.wait_ge(d_a_read, d.count(b, 1, 1))
                        nc.gpsimd.tensor_tensor(d_s[:, h, :], d_s[:, h, :], d_bias, ALU.add).then_inc(d_biased, 1)

                with pool.Fori(0, DENSE_BLOCKS) as b:
                    block(b)

            dense(first_tile)
            pool.wait_ge(flags_ready, 1)
            flagged(pool, lambda t: dense(tile_1(t)), [(d_biased, POOL_HEADS * DENSE_BLOCKS)])

            messages_stored(pool)

            def gather2(t):
                pool.wait_ge(l2_cols, t.affine(1, 1))
                if t.at_least(RING2):
                    pool.wait_ge(l2_sum, t.affine(1, 1 - RING2))
                pool.sem_inc(passed_pool, 1)
                for g in range(GROUPS):
                    nc.gpsimd.indirect_dma_start(msg_edge[:, t.place, g, :], None, msg_dram,
                                                 bass.IndirectOffsetOnAxis(ap=cols2[:, t.place, g:g + 1], axis=0)
                                                 ).then_inc(l2_in[t.place], 16)
            rounds(lambda j, tiles: [gather2(t) for t in tiles], lambda count: pool.Fori(0, count))

        @block.scalar
        def _(act):
            nc.scalar.preload_act_table_set("natural_log_exp_and_others")
            for b in range(NBLK):
                act.wait_ge(s_xt, b + 1)
                if b >= 2:
                    act.wait_ge(s_qkv, b - 1)
                nc.scalar.copy(x_t[:, b % 2, :], code[b % 2][:, 0:P]).then_inc(s_xtc, 1)

            def body(at):
                def sign(q):
                    t = at[0]
                    if not t:
                        return
                    if q % 2 == 0:
                        act.wait_ge(s_adj[t.parity][q // 2], t.of_parity(16, 16))
                    if t.at_least(1):
                        act.wait_ge(folded, t.affine(QUARTERS, q + 1 - QUARTERS))
                    nc.scalar.activation(present[:, q, :], a_ring[:, t.parity, q * QW:(q + 1) * QW].bitcast(U32),
                                         ACT.Sign, accum_out=nonzeros[:, t.index(), q:q + 1]).then_inc(signed, 1)

                t = at[5]
                if t:
                    act.wait_ge(x1_turned, t.affine(1, 1))
                    nc.scalar.copy(x1_t[:], x1_ps).then_inc(x1_copied, 1)
                t = at[4]
                if t:
                    act.wait_ge(shift_ready, t.affine(1, 1))
                    nc.scalar.activation(weighted[:, :, D:D + HEADS], shifted[:], ACT.Exp).then_inc(exped, 1)
                    nc.scalar.activation(prob_d[:, t.parity, :], shifted_d[:], ACT.Exp).then_inc(exped, 1)
                sign(0)
                t = at[5]
                if t:
                    act.wait_ge(msg_made, t.affine(1, 1))
                    if t.at_least(2):
                        act.wait_ge(s_msg[t.parity], t.of_parity(16, 0))
                    nc.scalar.copy(msg[:, t.parity, :], msg_ps).then_inc(msg_ready, 1)
                sign(1)
                if at[4]:
                    act.wait_ge(att_turned, at[4].affine(1, 1))
                    nc.scalar.copy(att_t[:], att_ps).then_inc(att_copied, 1)
                if at[3]:
                    act.wait_ge(member_turned, at[3].affine(1, 1))
                    nc.scalar.copy(member_t[:].rearrange("p g r -> p (g r)"), member_ps).then_inc(member_copied, 1)
                sign(2)
                t = at[4]
                if t:
                    rsqrt(stats_ready, t.affine(1, 1), rstd_step, t)
                sign(3)

            def rsqrt(ready, value, done, t):
                act.wait_ge(ready, value)
                nc.scalar.activation(lnv[:], mv[:, 1:2], ACT.Ln, bias=epsc[:]).then_inc(done, 1)
                act.wait_ge(done, t.affine(2, 1))
                nc.scalar.activation(r0[:], lnv[:], ACT.Exp, scale=-0.5).then_inc(done, 1)

            def weights_exp(dst, n):
                act.wait_ge(w_squared, n)
                nc.scalar.activation(dst, wtmp[:, 0:dst.shape[1]], ACT.Exp,
                                     scale=-1.0 / (2.0 * SIGMA * SIGMA)).then_inc(w_exped, 1)

            weights_exp(diag_w[:], 1)
            act.wait_ge(s_const, 1)
            iterations(act, body)

            def do(d_base, names, name, ins):
                before_step(act, d_base, names, name)
                ins().then_inc(turn, 1)

            def dense(d):
                def copy_k(b):
                    act.wait_ge(d_k_turned, d.count(b, 1, 1))
                    reached(act, d_scored, d.count(b, HEADS, 0))
                    nc.scalar.copy(d_kt, b_edge[:]).then_inc(d_k_copied, 1)

                def exps(b):
                    act.wait_ge(d_max_ready, d.count(b, 1, 1))
                    nc.scalar.activation(d_fell[:], d_fall[:], ACT.Exp).then_inc(d_fell_ready, 1)
                    for h in range(HEADS):
                        nc.scalar.activation(d_p[:, h, :], d_s[:, h, :], ACT.Exp, bias=d_new[:, h:h + 1],
                                             accum_out=d_part[:, h:h + 1]).then_inc(d_exped, 1)
                    reached(act, d_weighed, d.count(b, 1, 0))
                    for h in range(HEADS):
                        act.wait_ge(d_p_turned, d.count(b, HEADS, h + 1))
                        nc.scalar.copy(d_pt[:, h].rearrange("p c r -> p (c r)"), p_bank[h % 2][:]).then_inc(d_p_copied, 1)

                act.wait_ge(d_q_turned, d.no + 1)
                for h in range(HEADS):
                    nc.scalar.copy(d_qh[h * HD:(h + 1) * HD, h, :], b_fin[h * HD:(h + 1) * HD, 0:P]).then_inc(d_q_copied, 1)
                copy_k(0)
                copy_k(1)
                exps(0)
                copy_k(2)
                with act.Fori(0, DENSE_BLOCKS - 3) as b:
                    exps(b + 1)
                    copy_k(b + 3)
                exps(DENSE_BLOCKS - 2)
                exps(DENSE_BLOCKS - 1)
                base = d.turns
                do(base, FINISH, "copy_att", lambda: nc.scalar.copy(att_t[:], att_ps))
                do(base, FINISH, "ln", lambda: nc.scalar.activation(lnv[:], mv[:, 1:2], ACT.Ln, bias=epsc[:]))
                do(base, FINISH, "r0", lambda: nc.scalar.activation(r0[:], lnv[:], ACT.Exp, scale=-0.5))
                do(base, FINISH, "copy_x1", lambda: nc.scalar.copy(x1_t[:], x1_ps))

            dense(first_tile)
            act.wait_ge(flags_ready, 1)
            flagged(act, lambda t: dense(tile_1(t)),
                    [(d_q_copied, HEADS), (d_k_copied, DENSE_BLOCKS), (d_fell_ready, DENSE_BLOCKS),
                     (d_exped, HEADS * DENSE_BLOCKS), (d_p_copied, HEADS * DENSE_BLOCKS)])
            weights_exp(edge_w[:].rearrange("p t g -> p (t g)"), 2)

            def tile2(t):
                for a in ahead(t):
                    if a.at_least(RING2):
                        act.wait_ge(l2_in[a.place], a.of_ring(RING2, 16 * GROUPS, 0))
                    nc.scalar.copy(cols2[:, a.place, :], cols_all[:, a.index(), :]).then_inc(l2_cols, 1)
            def rsqrt_round(j, tiles):
                n = len(tiles)
                act.wait_ge(l2_y, tiles[-1].affine(1, 1))
                nc.scalar.activation(lnv_round[:, 0:n], mv_round[:, 0:n, 1], ACT.Ln, bias=epsc[:]).then_inc(l2_rstd, 1)
                act.wait_ge(l2_rstd, 2 * j + 1)
                nc.scalar.activation(r0_round[:, 0:n], lnv_round[:, 0:n], ACT.Exp, scale=-0.5).then_inc(l2_rstd, 1)

            act.wait_ge(pool_copy, TILES)

            def weights_block(d, b):
                act.wait_ge(e_inverted, d.count(b, 1, 1))
                nc.scalar.activation(d_e, d_pen, ACT.Square, bias=minus_one[:]).then_inc(e_squared, 1)
                act.wait_ge(e_squared, d.count(b, 1, 1))
                nc.scalar.activation(d_e, d_e, ACT.Exp, scale=-1.0 / (2.0 * SIGMA * SIGMA)).then_inc(e_exped, 1)

            def copy_weights(d, b):
                act.wait_ge(e_turned, d.count(b, 1, 1))
                reached(act, e_weighed, d.count(b, 1, 0))
                nc.scalar.copy(d_pt[:, 0].rearrange("p c r -> p (c r)"), b_max[:]).then_inc(e_copied, 1)

            def body2(j, tiles):
                for u, t in enumerate(tiles):
                    tile2(t)
                    if u == 1:
                        weights_block(first_tile_2, j)
                rsqrt_round(j, tiles)
                copy_weights(first_tile_2, j)
                if tiles[0].at_least(1):
                    act.wait_ge(s_out, 16 * j)
                act.wait_ge(l2_shift, j + 1)
                for u, t in enumerate(tiles):
                    nc.scalar.activation(y2[:, u, :], y_round[:, u, :], ACT.Identity, scale=rstd_round[:, u:u + 1],
                                         bias=shift_round[:, u:u + 1]).then_inc(l2_out, 1)

            rounds(body2, lambda count: act.Fori(0, count))

            def finish_block(d):
                do(d.turns, FINISH_2, "ln", lambda: nc.scalar.activation(lnv[:], mv[:, 1:2], ACT.Ln, bias=epsc[:]))
                do(d.turns, FINISH_2, "r0", lambda: nc.scalar.activation(r0[:], lnv[:], ACT.Exp, scale=-0.5))

            def dense2(d):
                weights_block(d, 0)
                copy_weights(d, 0)
                with act.Fori(0, DENSE_BLOCKS - 1) as b:
                    weights_block(d, b + 1)
                    copy_weights(d, b + 1)
                finish_block(d)

            finish_block(first_tile_2)
            flagged(act, lambda t: dense2(tile_2(t)), [(e_squared, DENSE_BLOCKS), (e_exped, DENSE_BLOCKS), (e_copied, DENSE_BLOCKS)])

        @block.tensor
        def _(pe):
            pe.wait_ge(s_const, 1)
            pe.wait_ge(s_loaded, 16 * 7)

            def turn_x(b):
                if b % (NBLK // X_CHUNKS) == 0:
                    pe.wait_ge(s_xall[b * X_CHUNKS // NBLK], 16)
                if b >= 2:
                    pe.wait_ge(s_xtc, b - 1)
                nc.tensor.transpose(code[b % 2][:, 0:P], z[:, b, :], ident[:]).then_inc(s_xt, 1)

            turn_x(0)
            for b in range(NBLK):
                if b + 1 < NBLK:
                    turn_x(b + 1)
                pe.wait_ge(s_xtc, b + 1)
                if b >= 2:
                    pe.wait_ge(s_qkvb, b - 1)
                nc.tensor.matmul(q_edge[b % 2][:, 0:3 * D], x_t[:, b % 2, :], w_qkv_sb[:], start=True, stop=True).then_inc(s_qkv, 1)
            pe.wait_ge(s_qkvb, NBLK)
            pe.wait_ge(s_powers, 1)

            def body(at):
                def fold_quarter(q):
                    t = at[0]
                    if not t:
                        return
                    pe.wait_ge(signed, t.affine(QUARTERS, q + 1))
                    if q == 0 and t.at_least(2):
                        pe.wait_ge(code_free, t.affine(1, -1))
                    per = BLOCKS // QUARTERS
                    for b in range(q * per, (q + 1) * per):
                        last = nc.tensor.matmul(code[t.parity][:], power[:, b, :],
                                                present[:, q, (b % per) * FOLD:(b % per + 1) * FOLD],
                                                start=(b == 0), stop=(b == BLOCKS - 1))
                    last.then_inc(folded, 1)

                t = at[5]
                if t:
                    pe.wait_ge(x1_ready, t.affine(1, 1))
                    nc.tensor.transpose(x1_ps, x1[:], ident[:]).then_inc(x1_turned, 1)
                t = at[4]
                if t:
                    pe.wait_ge(max_ready, t.affine(1, 1))
                    for g in range(GROUPS):
                        last = nc.tensor.matmul(max_ps[:, g * HEADS:(g + 1) * HEADS], member[:, t.parity, g * P:(g + 1) * P],
                                                neg_max[:], start=True, stop=True)
                    last.then_inc(max_sent, 1)
                t = at[5]
                if t:
                    pe.wait_ge(x1_copied, t.affine(1, 1))
                    nc.tensor.matmul(msg_ps, x1_t[:], w_msg_sb[:], start=True, stop=False)
                    nc.tensor.matmul(msg_ps, ones[0:1, :], b_msg_sb[0:1, :], start=False, stop=True).then_inc(msg_made, 1)
                t = at[4]
                if t:
                    pe.wait_ge(weighted_ready, t.affine(1, 1))
                    if t.at_least(1):
                        pe.wait_ge(att_ready, t.affine(1, 0))
                    for g in range(GROUPS):
                        last = nc.tensor.matmul(b_sum[:, 0:D + HEADS], member_t[:, g, :], weighted[:, g, :],
                                                start=(g == 0), stop=(g == GROUPS - 1))
                    last.then_inc(summed, 1)
                t = at[3]
                if t:
                    for g in range(GROUPS):
                        last = nc.tensor.transpose(member_ps[:, g * P:(g + 1) * P], member[:, t.parity, g * P:(g + 1) * P], ident[:])
                    last.then_inc(member_turned, 1)
                t = at[2]
                if t:
                    pe.wait_ge(member_ready, t.affine(1, 1))
                    for g in range(GROUPS):
                        last = nc.tensor.matmul(info_e[:, g, :], member[:, t.parity, g * P:(g + 1) * P],
                                                rowinfo[:, t.parity, :], start=True, stop=True)
                    last.then_inc(info_sent, 1)
                t = at[4]
                if t:
                    pe.wait_ge(att_ready, t.affine(1, 1))
                    if t.at_least(1):
                        pe.wait_ge(msg_ready, t.affine(1, 0))
                    nc.tensor.transpose(att_ps, att[:], ident[:]).then_inc(att_turned, 1)
                t = at[2]
                if t:
                    pe.wait_ge(s_q[t.parity], t.of_parity(16, 16))
                    if t.at_least(2):
                        pe.wait_ge(q_read, t.affine(1, -1))
                    for g in range(GROUPS):
                        last = nc.tensor.matmul(q_edge[t.parity][:, g * D:(g + 1) * D], member[:, t.parity, g * P:(g + 1) * P],
                                                q_own[:, t.parity, :], start=True, stop=True)
                    last.then_inc(q_sent, 1)
                if at[4]:
                    pe.wait_ge(att_copied, at[4].affine(1, 1))
                    nc.tensor.matmul(proj_ps, att_t[:], w_out_sb[:], start=True, stop=True).then_inc(projected, 1)
                fold_quarter(0)
                fold_quarter(1)
                fold_quarter(2)
                t = at[3]
                if t:
                    pe.wait_ge(by_slot_ready, t.affine(1, 1))
                    pe.wait_ge(member_copied, t.affine(1, 1))
                    for g in range(GROUPS):
                        last = nc.tensor.matmul(slot_ps, member_t[:, g, :], by_slot[:, g].rearrange("p h s -> p (h s)"),
                                                start=(g == 0), stop=(g == GROUPS - 1))
                    last.then_inc(slots_sent, 1)
                fold_quarter(3)
                t = at[1]
                if t:
                    pe.wait_ge(counted, t.affine(1, 1))
                    if t.at_least(1):
                        pe.wait_ge(idx_ready, t.affine(1, 0))
                    nc.tensor.matmul(first_ps, before[:], found[:, bass.ds(t.index(), 1)], start=True, stop=True).then_inc(first_ready, 1)
            iterations(pe, body)

            def do(d_base, names, name, work):
                before_step(pe, d_base, names, name)
                work().then_inc(turn, 1)

            def dense(d):
                def turn_keys(b):
                    pe.wait_ge(d_k_in, d.count(b, 16, 16))
                    reached(pe, d_k_copied, d.count(b, 1, 0))
                    for c in range(CHUNKS):
                        last = nc.tensor.transpose(b_edge[:, c * P:(c + 1) * P], d_k[:, c, :], ident[:])
                    last.then_inc(d_k_turned, 1)

                def scores(b):
                    pe.wait_ge(d_k_copied, d.count(b, 1, 1))
                    pe.wait_ge(d_q_copied, d.no * HEADS + HEADS)
                    for h in range(HEADS):
                        reached(pe, d_masked, d.count(b, HEADS, h + 1 - HEADS))
                        nc.tensor.matmul(score_bank[h][:], d_qh[:, h, :], d_kt, start=True, stop=True).then_inc(d_scored, 1)

                def turn_probs(b):
                    for h in range(HEADS):
                        pe.wait_ge(d_exped, d.count(b, HEADS, h + 1))
                        if h >= 2:
                            pe.wait_ge(d_p_copied, d.count(b, HEADS, h - 1))
                        for c in range(CHUNKS):
                            last = nc.tensor.transpose(p_bank[h % 2][:, c * P:(c + 1) * P], d_p[:, h, c * P:(c + 1) * P], ident[:])
                        last.then_inc(d_p_turned, 1)

                def weigh(b):
                    pe.wait_ge(d_p_copied, d.count(b, HEADS, HEADS))
                    pe.wait_ge(d_v_in, d.count(b, 16, 16))
                    reached(pe, d_added, d.count(b, 1, 0))
                    for h in range(HEADS):
                        for c in range(CHUNKS):
                            last = nc.tensor.matmul(b_sum[:, h * HD:(h + 1) * HD], d_pt[:, h, c, :], d_v[:, c, h * HD:(h + 1) * HD],
                                                    start=(c == 0), stop=(c == CHUNKS - 1))
                    last.then_inc(d_weighed, 1)

                pe.wait_ge(d_qx_in, 32 * d.no + 32)
                nc.tensor.transpose(b_fin[:, 0:P], d_q[:], ident[:]).then_inc(d_q_turned, 1)
                turn_keys(0)
                scores(0)
                turn_keys(1)
                scores(1)
                turn_probs(0)
                turn_keys(2)
                weigh(0)
                with pe.Fori(0, DENSE_BLOCKS - 3) as b:
                    scores(b + 2)
                    turn_probs(b + 1)
                    turn_keys(b + 3)
                    weigh(b + 1)
                scores(DENSE_BLOCKS - 1)
                for b in (DENSE_BLOCKS - 2, DENSE_BLOCKS - 1):
                    turn_probs(b)
                    weigh(b)
                base = d.turns
                do(base, FINISH, "turn_att", lambda: nc.tensor.transpose(att_ps, att[:], ident[:]))
                do(base, FINISH, "project", lambda: nc.tensor.matmul(proj_ps, att_t[:], w_out_sb[:], start=True, stop=True))
                do(base, FINISH, "turn_x1", lambda: nc.tensor.transpose(x1_ps, x1[:], ident[:]))
                do(base, FINISH, "message", lambda: nc.tensor.matmul(msg_ps, x1_t[:], w_msg_sb[:], start=True, stop=True))

            pe.wait_ge(msg_ready, TILES)
            dense(first_tile)
            pe.wait_ge(flags_summed, 1)
            nc.tensor.matmul(b_edge[:, 0:TILES], ones[:], row_flags[:], start=True, stop=True).then_inc(flags_summed, 1)
            pe.wait_ge(flags_ready, 1)
            flagged(pe, lambda t: dense(tile_1(t)),
                    [(d_q_turned, 1), (d_k_turned, DENSE_BLOCKS), (d_scored, HEADS * DENSE_BLOCKS),
                     (d_p_turned, HEADS * DENSE_BLOCKS), (d_weighed, DENSE_BLOCKS)])

            def sum2(t):
                pe.wait_ge(l2_in[t.place], t.of_ring(RING2, 16 * GROUPS, 16 * GROUPS))
                pe.wait_ge(l2_memw, t.affine(1, 1))
                if t.at_least(RING2):
                    pe.wait_ge(l2_y, t.affine(1, 1 - RING2))
                for g in range(GROUPS):
                    last = nc.tensor.matmul(sum_bank[t.place][:, 0:D], memw[:, t.place, g, :], msg_edge[:, t.place, g, :],
                                            start=(g == 0), stop=(g == GROUPS - 1))
                last.then_inc(l2_sum, 1)

            def turn_weights(d, b):
                pe.wait_ge(e_weight, d.count(b, 1, 1))
                for c in range(CHUNKS):
                    last = nc.tensor.transpose(b_max[:, c * P:(c + 1) * P], d_w[:, c * P:(c + 1) * P], ident[:])
                last.then_inc(e_turned, 1)

            def weigh_block(d, b):
                pe.wait_ge(e_copied, d.count(b, 1, 1))
                pe.wait_ge(e_m_in, d.count(b, 16, 16))
                reached(pe, e_added, d.count(b, 1, 0))
                for c in range(CHUNKS):
                    last = nc.tensor.matmul(b_sum[:, 0:D], d_pt[:, 0, c, :], d_v[:, c, :], start=(c == 0), stop=(c == CHUNKS - 1))
                last.then_inc(e_weighed, 1)

            def body2(j, tiles):
                for t in tiles:
                    sum2(t)
                turn_weights(first_tile_2, j)
                weigh_block(first_tile_2, j)

            rounds(body2, lambda count: pe.Fori(0, count))

            def dense2(d):
                turn_weights(d, 0)
                weigh_block(d, 0)
                with pe.Fori(0, DENSE_BLOCKS - 1) as b:
                    turn_weights(d, b + 1)
                    weigh_block(d, b + 1)

            flagged(pe, lambda t: dense2(tile_2(t)), [(e_turned, DENSE_BLOCKS), (e_weighed, DENSE_BLOCKS)])

        @block.vector
        def _(dve):
            V = nc.vector
            STEPS = 39
            made = [0]
            loops = []
            history = []

            def steps_done():
                return sum((reg * steps for reg, steps in loops if steps), made[0])

            def run(ins, ready=None, value=None):
                if ready is None:
                    made[0] += 1
                    ins.then_inc(step, 1)
                    history.append((step, steps_done()))
                else:
                    ins.then_inc(ready, 1)
                    history.append((ready, value))

            @contextmanager
            def counting(reg, steps, last=None):
                begun = made[0]
                loops.append((reg, steps))
                history[:] = [last(reg) if last else (step, steps_done())] * 8
                yield
                assert made[0] == begun + steps and (last or history[-1][0] is step), (made[0] - begun, steps)
                loops.pop()
                made[0] = begun

            @contextmanager
            def counted_loop(count, steps, last=None):
                with dve.Fori(0, count) as reg:
                    with counting(reg, steps, last):
                        yield reg
                made[0] += count * steps
                history[:] = [last(count) if last else (step, steps_done())] * 8

            def unfused():
                dve.sem_inc(passed_dve, 1)

            def after(n=1):
                if len(history) >= n:
                    dve.wait_ge(*history[-n])

            dve.wait_ge(s_const, 1)
            for b in range(BLOCKS):
                run(V.tensor_scalar(power[:, b, :], ident[:], float(2 ** b), None, ALU.mult))
            after()
            run(V.memset(d_qh[:], 0.0), s_powers, 1)
            dve.wait_ge(s_loaded, 16 * 7)
            def sum_diagonal(t):
                dve.wait_ge(diag_ready, t + 1)
                run(V.tensor_reduce(neg_diag[:, t, :], heads(diag_prod[:, t % 2, :]), AX_X, ALU.add), diag_summed, t + 1)

            for b in range(NBLK):
                g = b // 4
                dve.wait_ge(s_qkv, b + 1)
                if g >= STORES and b % 4 == 0:
                    dve.wait_ge(s_stored[g % STORES], 32 * (g // STORES))
                    dve.wait_ge(diag_ready, 4 * (g - STORES) + 4)
                run(V.tensor_tensor(qkv[:, g % STORES, b % 4, :], q_edge[b % 2][:, 0:3 * D], b_qkv_sb[:], ALU.add), s_qkvb, b + 1)
                if b >= 1:
                    sum_diagonal(b - 1)

            def weights(dst, src, n):
                w, zero = wtmp[:, 0:src.shape[1]], wtmp2[:, 0:src.shape[1]]
                after()
                run(V.tensor_scalar(zero, src, 0.0, None, ALU.is_equal))
                after()
                run(V.tensor_tensor(w, src, zero, ALU.add))
                after()
                run(V.reciprocal(w, w))
                after()
                run(V.tensor_scalar(w, w, -1.0, None, ALU.add))
                after()
                run(V.tensor_tensor(w, w, w, ALU.mult), w_squared, n)
                after()
                run(V.scalar_tensor_tensor(zero, src, 1.0, zero, ALU.is_lt, ALU.subtract))
                dve.wait_ge(w_exped, n)
                after()
                run(V.tensor_tensor(dst, dst, zero, ALU.mult))

            dve.wait_ge(s_diag, 16)
            run(V.tensor_scalar(neg_gb_diag[:], diag_adj[:], gb[:], -1.0, ALU.mult, ALU.mult))
            after()
            run(V.scalar_tensor_tensor(neg_diag[:], neg_diag[:], -SCALE, neg_gb_diag[:].unsqueeze(2).to_broadcast([P, TILES, HEADS]),
                                       ALU.mult, ALU.add))
            weights(diag_w[:], diag_adj[:], 1)

            def scan(t, part):
                ps = code[t.parity]
                if part == 0:
                    dve.wait_ge(folded, t.affine(QUARTERS, QUARTERS))
                    unfused()
                    run(V.max(c8[:, 0:8], ps[:]))
                elif part == 1:
                    unfused()
                    run(V.max_index(m8[:, 0:8], c8[:, 0:8], ps[:]))
                elif part == 2:
                    unfused()
                    run(V.match_replace(code_left[:], c8[:, 0:8], ps[:], 0.0), code_free, t.affine(1, 1))
                elif part == 3:
                    unfused()
                    run(V.max(c8[:, 8:16], code_left[:]))
                elif part == 4:
                    unfused()
                    run(V.max_index(m8[:, 8:16], c8[:, 8:16], code_left[:]))
                elif part == 5:
                    run(V.tensor_scalar(bits[:, 0, :], c8[:].bitcast(U32), EXPONENT, None, ALU.bitwise_and))
                elif part == 6:
                    run(V.tensor_tensor(rest[:], c8[:], bits[:, 0, :].bitcast(F32), ALU.subtract))
                elif part == 7:
                    run(V.tensor_scalar(bits[:, 1, :], rest[:].bitcast(U32), EXPONENT, None, ALU.bitwise_and))
                elif part == 8:
                    run(V.tensor_scalar(expo[:], bits[:], 23 - 9, None, ALU.logical_shift_right))
                elif part == 10:
                    run(V.scalar_tensor_tensor(key[:], expo[:], float(1 - 127 * FOLD),
                                               m8[:].unsqueeze(1).to_broadcast([P, 2, SLOTS]), ALU.add, ALU.add))
                elif part == 11:
                    run(V.scalar_tensor_tensor(cand[:], bits[:].bitcast(F32), 0.0, key[:], ALU.is_gt, ALU.mult))
                elif part == 18:
                    run(V.scalar_tensor_tensor(cand[:], key[:], own_col[:, bass.ds(t.index(), 1)], cand[:], ALU.not_equal, ALU.mult))
                elif part == 12:
                    unfused()
                    run(V.max(rowinfo[:, t.parity, 0:8], cand[:].rearrange("p a s -> p (a s)")))
                elif part == 13:
                    run(V.tensor_scalar(taken[:], cand[:], 0.0, 0.0, ALU.is_gt, ALU.add, accum_out=found[:, bass.ds(t.index(), 1)]),
                        counted, t.affine(1, 1))
                elif part == 14:
                    unfused()
                    run(V.match_replace(cand_left[:].rearrange("p a s -> p (a s)"), rowinfo[:, t.parity, 0:8],
                                        cand[:].rearrange("p a s -> p (a s)"), 0.0))
                elif part == 16:
                    unfused()
                    run(V.max(rowinfo[:, t.parity, 8:16], cand_left[:].rearrange("p a s -> p (a s)")))

            def gather_(t, part):
                info = rowinfo[:, t.parity, :]
                if part == 0:
                    dve.wait_ge(first_ready, t.affine(1, 1))
                    run(V.tensor_copy(info[:, SLOTS:SLOTS + 1], first_ps), first_copied, t.affine(1, 1))
                    run(V.tensor_tensor(ends[:, bass.ds(t.index(), 1)], first_ps, found[:, bass.ds(t.index(), 1)], ALU.add))
                elif part == 3:
                    dve.wait_ge(starts_ready, t.affine(1, 1))
                    run(V.scalar_tensor_tensor(member[:, t.parity, :], edge_no[:], ends[:, bass.ds(t.index(), 1)], starts[:],
                                               ALU.is_le, ALU.mult), member_ready, t.affine(1, 1))
                elif part == 5:
                    run(V.tensor_scalar(empty[:, t.parity, :], info[:, 0:SLOTS], 0.0, MASKED, ALU.is_equal, ALU.mult))
                elif part == 6:
                    run(V.tensor_tensor(slot[:], edge_col[:], info_e[:, :, SLOTS], ALU.subtract))
                elif part == 7:
                    dve.wait_ge(info_sent, t.affine(1, 1))
                    run(V.tensor_copy(row_of[:, t.index(), :], info_e[:, :, SLOTS + 1]))
                elif part == 8:
                    run(V.tensor_tensor(is_slot[:, t.parity], slot_no[:], slot[:].unsqueeze(2).to_broadcast([P, GROUPS, SLOTS]),
                                        ALU.is_equal))
                elif part == 9:
                    run(V.tensor_scalar(row_start[:], row_of[:, t.index(), :], float(TILES * N), row_first[:, bass.ds(t.index(), 1)],
                                        ALU.mult, ALU.add))
                elif part == 10:
                    run(V.tensor_tensor(picked[:], is_slot[:, t.parity], info_e[:, :, 0:SLOTS], ALU.mult))
                elif part == 12:
                    run(V.tensor_reduce(keys[:], picked[:], AX_X, ALU.add))
                elif part == 13:
                    if t.at_least(2):
                        dve.wait_ge(pool_copy, t.affine(1, -1))
                    run(V.tensor_scalar(cols[:, t.parity, :], keys[:], -1.0, 0.0, ALU.add, ALU.max))
                elif part == 14:
                    run(V.tensor_tensor(flat[:, t.parity, :], row_start[:], cols[:, t.parity, :], ALU.bitwise_or),
                        idx_ready, t.affine(1, 1))

            def attend_(t, part):
                if part == 0:
                    dve.wait_ge(s_kv[t.parity], t.of_parity(16 * GROUPS, 16 * GROUPS))
                    dve.wait_ge(q_sent, t.affine(1, 1))
                    run(V.tensor_tensor(prod[:], kv_edge[:, t.parity, :, 0:D],
                                        q_edge[t.parity][:, 0:GROUPS * D].rearrange("p (g d) -> p g d", g=GROUPS), ALU.mult),
                        q_read, t.affine(1, 1))
                elif part == 1:
                    dve.wait_ge(s_val[t.parity], t.of_parity(16 * GROUPS, 16 * GROUPS))
                    run(V.tensor_scalar(pen[:], adj_edge[:, t.parity, :], 0.0, MASKED, ALU.is_equal, ALU.mult))
                elif part == 2:
                    run(V.tensor_reduce(psum_[:].rearrange("p g h -> p (g h)"),
                                        prod[:].rearrange("p g (h d) -> p (g h) d", h=HEADS), AX_X, ALU.add))
                elif part == 3:
                    run(V.scalar_tensor_tensor(bias[:], adj_edge[:, t.parity, :], gb[:], pen[:], ALU.mult, ALU.add))
                elif part == 5:
                    run(V.scalar_tensor_tensor(score[:], psum_[:], SCALE, bias[:].unsqueeze(2).to_broadcast([P, GROUPS, HEADS]),
                                               ALU.mult, ALU.add))
                elif part == 9:
                    run(V.tensor_tensor(by_slot[:], is_slot[:, t.parity].unsqueeze(2).to_broadcast([P, GROUPS, HEADS, SLOTS]),
                                        score[:].unsqueeze(3).to_broadcast([P, GROUPS, HEADS, SLOTS]), ALU.mult),
                        by_slot_ready, t.affine(1, 1))
                elif part == 10:
                    dve.wait_ge(slots_sent, t.affine(1, 1))
                    run(V.tensor_tensor(slotted[:], slot_ps.rearrange("p (h s) -> p h s", h=HEADS),
                                        empty[:, t.parity, :].unsqueeze(1).to_broadcast([P, HEADS, SLOTS]), ALU.add))
                elif part == 11:
                    run(V.tensor_reduce(rowmax[:], slotted[:], AX_X, ALU.max))
                elif part == 12:
                    run(V.scalar_tensor_tensor(neg_max[:], rowmax[:], -1.0, neg_diag[:, t.index(), :], ALU.mult, ALU.min),
                        max_ready, t.affine(1, 1))
                elif part == 13:
                    run(V.tensor_tensor(shifted_d[:], neg_max[:], neg_diag[:, t.index(), :], ALU.subtract))
                elif part == 14:
                    dve.wait_ge(max_sent, t.affine(1, 1))
                    run(V.tensor_tensor(shifted[:].rearrange("p g h -> p (g h)"), score[:].rearrange("p g h -> p (g h)"), max_ps,
                                        ALU.add), shift_ready, t.affine(1, 1))
                elif part == 15:
                    dve.wait_ge(exped, t.affine(2, 1))
                    run(V.tensor_tensor(weighted[:, :, 0:D].rearrange("p g (h d) -> p g h d", h=HEADS),
                                        kv_edge[:, t.parity, :, D:2 * D].rearrange("p g (h d) -> p g h d", h=HEADS),
                                        weighted[:, :, D:D + HEADS].unsqueeze(3).to_broadcast([P, GROUPS, HEADS, HD]), ALU.mult),
                        weighted_ready, t.affine(1, 1))

            def finish_(t, part):
                if part == 0:
                    dve.wait_ge(summed, t.affine(1, 1))
                    dve.wait_ge(pool_fin, t.affine(2, 1))
                    run(V.tensor_tensor(den[:], b_sum[:, D:D + HEADS], prob_d[:, t.parity, :], ALU.add))
                elif part == 1:
                    run(V.tensor_tensor(num[:], b_sum[:, 0:D], pv_d[:], ALU.add))
                elif part == 2:
                    run(V.reciprocal(rden[:], den[:]))
                elif part == 3:
                    run(V.tensor_tensor(att[:].rearrange("p (h d) -> p h d", h=HEADS), num[:].rearrange("p (h d) -> p h d", h=HEADS),
                                        rden[:].unsqueeze(2).to_broadcast([P, HEADS, HD]), ALU.mult), att_ready, t.affine(1, 1))
                elif part == 4:
                    dve.wait_ge(projected, t.affine(1, 1))
                    dve.wait_ge(pool_fin, t.affine(2, 2))
                    run(V.tensor_tensor(y[:], proj_ps, resid[:], ALU.add))
                elif part == 5:
                    run(V.bn_stats(stats[:], y[:]))
                elif part == 6:
                    unfused()
                    run(V.bn_aggr(mv[:], stats[:]), stats_ready, t.affine(1, 1))
                elif part == 7:
                    dve.wait_ge(rstd_step, t.affine(2, 2))
                    run(V.tensor_scalar(t1[:], mv[:, 1:2], EPS, r0[:], ALU.add, ALU.mult))
                elif part == 8:
                    run(V.tensor_scalar(t2[:], t1[:], r0[:], -0.5, ALU.mult, ALU.mult))
                elif part == 10:
                    run(V.scalar_tensor_tensor(rstd[:], t2[:], 1.5, r0[:], ALU.add, ALU.mult))
                elif part == 11:
                    run(V.tensor_scalar(x1[:], y[:], mv[:, 0:1], rstd[:], ALU.subtract, ALU.mult), x1_ready, t.affine(1, 1))
                elif part == 13:
                    dve.wait_ge(msg_ready, t.affine(1, 1))
                    run(V.scalar_tensor_tensor(z[:, t.index(), :], msg[:, t.parity, :], diag_w[:, bass.ds(t.index(), 1)], x1[:],
                                               ALU.mult, ALU.add))

            F, A, G, S = finish_, attend_, gather_, scan
            ORDER = [
                (G, 5, 2, 6), (G, 0, 2, 8), (A, 14, 4, 8), (S, 0, 1, 8), (A, 15, 4, 8), (S, 1, 1, 2), (G, 3, 2, 5), (S, 2, 1, 4),
                (F, 0, 4, 8), (F, 1, 4, 8), (F, 2, 4, 2), (S, 3, 1, 4), (F, 3, 4, 2), (S, 4, 1, 2), (G, 7, 2, 8), (G, 6, 2, 8),
                (S, 5, 1, 5), (G, 9, 2, 3), (G, 8, 2, 3), (S, 6, 1, 3), (G, 10, 2, 2), (S, 7, 1, 2), (G, 12, 2, 2), (S, 8, 1, 2),
                (G, 13, 2, 2), (A, 1, 3, 8), (G, 14, 2, 2), (A, 0, 3, 8), (S, 10, 1, 5), (F, 4, 4, 8), (A, 3, 3, 5), (A, 2, 3, 4),
                (F, 5, 4, 3), (S, 11, 1, 5), (F, 6, 4, 2), (A, 5, 3, 4), (S, 18, 1, 3), (A, 9, 3, 2), (S, 13, 1, 2), (F, 13, 5, 8),
                (S, 12, 1, 4), (F, 7, 4, 7), (S, 14, 1, 2), (F, 8, 4, 2), (S, 16, 1, 2), (A, 10, 3, 8), (F, 10, 4, 3), (A, 11, 3, 2),
                (F, 11, 4, 2), (A, 12, 3, 2), (A, 13, 3, 1)]

            def body(at):
                whole = all(at)
                for stage, part, k, back in ORDER:
                    if at[k]:
                        after(back if whole else 1)
                        stage(at[k], part)

            for i in range(LOOP_FROM):
                body(active(Tile(None, i)))
            with counted_loop(PAIRS, 2 * STEPS) as pair:
                for u in range(2):
                    body(active(Tile(pair, LOOP_FROM + u)))
            for i in range(LOOP_FROM + 2 * PAIRS, LAST):
                body(active(Tile(None, i)))

            def do(d_base, names, name, ins):
                before_step(dve, d_base, names, name)
                ins().then_inc(turn, 1)

            def wide(ap, n=P):
                return ap.unsqueeze(2).to_broadcast([P, HEADS, n])

            def newton_steps(base, names):
                do(base, names, "n1", lambda: V.tensor_tensor(t1[:], r0[:], r0[:], ALU.mult))
                do(base, names, "n2", lambda: V.scalar_tensor_tensor(t2[:], mv[:, 1:2], EPS, t1[:], ALU.add, ALU.mult))
                do(base, names, "n3", lambda: V.tensor_scalar(t1[:], t2[:], -0.5, 1.5, ALU.mult, ALU.add))
                do(base, names, "n4", lambda: V.tensor_tensor(rstd[:], t1[:], r0[:], ALU.mult))

            def aggregate(base, names):
                before_step(dve, base, names, "aggr")
                unfused()
                V.bn_aggr(mv[:], stats[:]).then_inc(turn, 1)

            def dense(d):
                reached(dve, turn, d.turns)
                for dst, value in ((d_old, 3e38), (d_sum, 0.0), (d_out, 0.0)):
                    run(V.memset(dst[:], value))

                def masked(b, h):
                    dve.wait_ge(d_scored, d.count(b, HEADS, h + 1))
                    reached(dve, d_exped, d.count(b, HEADS, h + 1 - HEADS))
                    run(V.scalar_tensor_tensor(d_s[:, h, :], score_bank[h][:], SCALE, d_on, ALU.mult, ALU.mult),
                        d_masked, d.count(b, HEADS, h + 1))

                def biased(h):
                    run(V.tensor_tensor(d_s[:, h, :], d_s[:, h, :], d_bias, ALU.add))

                def block_max(b, h):
                    if h < POOL_HEADS:
                        dve.wait_ge(d_biased, d.count(b, POOL_HEADS, h + 1))
                    run(V.tensor_reduce(d_bmax[:, h:h + 1], d_s[:, h, :], AX_X, ALU.max))

                def block_scores(b, last_block=None, add=None):
                    after()
                    dve.wait_ge(d_a_in, d.count(b, 16, 16))
                    run(V.tensor_scalar(d_on, d_adj, 0.0, None, ALU.not_equal))
                    run(V.tensor_scalar(d_pen, d_adj, 0.0, MASKED, ALU.is_equal, ALU.mult))
                    if add is not None:
                        add_weighed(add)
                    after()
                    run(V.scalar_tensor_tensor(d_bias, d_adj, gb[:], d_pen, ALU.mult, ALU.add), d_a_read, d.count(b, 1, 1))
                    for work, h in ((masked, 0), (masked, 1), (masked, 2), (masked, 3), (biased, 2),
                                    (biased, 3), (block_max, 0), (block_max, 2), (block_max, 1), (block_max, 3)):
                        after(2)
                        if work is biased:
                            work(h)
                        else:
                            work(b, h)
                    if last_block is not None:
                        fall_sums(last_block)
                    after()
                    run(V.scalar_tensor_tensor(d_new[:], d_bmax[:], -1.0, d_old[:], ALU.mult, ALU.min))
                    after()
                    run(V.tensor_tensor(d_fall[:], d_new[:], d_old[:], ALU.subtract), d_max_ready, d.count(b, 1, 1))
                    after()
                    run(V.tensor_copy(d_old[:], d_new[:]))

                def fall_sums(b):
                    dve.wait_ge(d_exped, d.count(b, HEADS, HEADS))
                    after()
                    run(V.tensor_tensor(d_sum[:], d_sum[:], d_fell[:], ALU.mult))
                    run(V.tensor_tensor(heads(d_out[:]), heads(d_out[:]), wide(d_fell[:], HD), ALU.mult))
                    after(2)
                    run(V.tensor_tensor(d_sum[:], d_sum[:], d_part[:], ALU.add))

                def add_weighed(b):
                    after()
                    dve.wait_ge(d_weighed, d.count(b, 1, 1))
                    run(V.tensor_tensor(d_out[:], d_out[:], b_sum[:, 0:D], ALU.add), d_added, d.count(b, 1, 1))

                block_scores(0)
                block_scores(1, 0)
                with counted_loop(DENSE_BLOCKS - 2, BLOCK_STEPS) as b:
                    block_scores(b + 2, b + 1, b)
                add_weighed(DENSE_BLOCKS - 2)
                after()
                fall_sums(DENSE_BLOCKS - 1)
                add_weighed(DENSE_BLOCKS - 1)
                after()
                base = d.turns
                do(base, FINISH, "rden", lambda: V.reciprocal(rden[:], d_sum[:]))
                do(base, FINISH, "att", lambda: V.tensor_tensor(heads(att[:]), heads(d_out[:]), wide(rden[:], HD), ALU.mult))
                do(base, FINISH, "add_x", lambda: V.tensor_tensor(y[:], proj_ps, d_x[:], ALU.add))
                do(base, FINISH, "add_b", lambda: V.tensor_tensor(y[:], y[:], b_out_sb[:], ALU.add))
                do(base, FINISH, "stats", lambda: V.bn_stats(stats[:], y[:]))
                aggregate(base, FINISH)
                newton_steps(base, FINISH)
                do(base, FINISH, "x1", lambda: V.tensor_scalar(x1[:], y[:], mv[:, 0:1], rstd[:], ALU.subtract, ALU.mult))
                do(base, FINISH, "add_bm", lambda: V.tensor_tensor(d_msg[:], msg_ps, b_msg_sb[:], ALU.add))
                do(base, FINISH, "keep", lambda: V.tensor_copy(z[:, d.z_index, :], x1[:]))

            BLOCK_STEPS = 15 - POOL_HEADS
            DENSE_STEPS = 3 + (BLOCK_STEPS - 3) + BLOCK_STEPS * (DENSE_BLOCKS - 1) + 3

            def flagged_counted(work, steps, own):
                def counted_work(t):
                    with counting(t, steps, lambda _: (step, steps_done())):
                        work(t)
                flagged(dve, counted_work, own + [(step, steps, made[0] - steps)])
                made[0] += TILES * steps
                history[:] = [(step, made[0])] * 8

            after()
            dense(first_tile)
            after()
            run(V.tensor_reduce(all_found[:], nonzeros[:], AX_X, ALU.add))
            after()
            run(V.scalar_tensor_tensor(all_found[:], all_found[:], -1.0, found[:], ALU.add, ALU.not_equal))
            run(V.tensor_scalar(row_flags[:], ends[:], float(EDGES), None, ALU.is_gt))
            after()
            run(V.scalar_tensor_tensor(row_flags[:], found[:], float(SLOTS), row_flags[:], ALU.is_gt, ALU.add))
            after()
            run(V.tensor_tensor(row_flags[:], row_flags[:], all_found[:], ALU.add))
            after()
            run(V.scalar_tensor_tensor(row_flags[:], diag_adj[:], 0.0, row_flags[:], ALU.is_equal, ALU.add), flags_summed, 1)
            dve.wait_ge(flags_summed, 2)
            run(V.tensor_copy(flags[:, 0:TILES], b_edge[:, 0:TILES]))
            run(V.tensor_reduce(flag_part[:, 0:1], b_edge[:, 0:TILES], AX_X, ALU.add))
            after()
            run(V.tensor_copy(flags[:, TILES:TILES + 1], flag_part[:, 0:1]), flags_ready, 1)
            after()
            flagged_counted(lambda t: dense(tile_1(t)), DENSE_STEPS,
                            [(d_a_read, DENSE_BLOCKS), (d_masked, HEADS * DENSE_BLOCKS), (d_max_ready, DENSE_BLOCKS),
                             (d_added, DENSE_BLOCKS)])
            run(V.memset(flag_part[:], 0.0))

            dve.wait_ge(adj_kept, TILES)
            weights(edge_w[:].rearrange("p t g -> p (t g)"), edge_adj[:].rearrange("p t g -> p (t g)"), 2)

            def members(t):
                if t.at_least(RING2):
                    dve.wait_ge(l2_sum, t.affine(1, 1 - RING2))
                for g in range(GROUPS):
                    after(4)
                    ins = V.tensor_scalar(memw[:, t.place, g, :], row_no[:], row_of[:, t.index(), g:g + 1],
                                          edge_w[:, t.index(), g:g + 1], ALU.is_equal, ALU.mult)
                    if g < GROUPS - 1:
                        run(ins)
                    else:
                        run(ins, l2_memw, t.affine(1, 1))

            def add2(t):
                dve.wait_ge(l2_sum, t.affine(1, 1))
                if t.at_least(PER_ROUND):
                    dve.wait_ge(l2_out, t.affine(1, 1 - PER_ROUND))
                run(V.tensor_tensor(y_round[:, t.place, :], sum_bank[t.place][:, 0:D], z[:, t.index(), :], ALU.add))

            def stats2(t):
                run(V.bn_stats(stats_round[:, t.place, :], y_round[:, t.place, :]))

            def aggregate2(t):
                unfused()
                run(V.bn_aggr(mv_round[:, t.place, :], stats_round[:, t.place, :]), l2_y, t.affine(1, 1))

            def norm_round(j, tiles):
                n = len(tiles)
                t1_, t2_, r0_ = t1_round[:, 0:n], t2_round[:, 0:n], r0_round[:, 0:n]
                dve.wait_ge(l2_rstd, 2 * j + 2)
                after()
                run(V.tensor_tensor(t1_, r0_, r0_, ALU.mult))
                after()
                run(V.scalar_tensor_tensor(t2_, mv_round[:, 0:n, 1], EPS, t1_, ALU.add, ALU.mult))
                after()
                run(V.tensor_scalar(t1_, t2_, -0.5, 1.5, ALU.mult, ALU.add))
                after()
                run(V.tensor_tensor(rstd_round[:, 0:n], t1_, r0_, ALU.mult))
                after()
                run(V.scalar_tensor_tensor(shift_round[:, 0:n], mv_round[:, 0:n, 0], -1.0, rstd_round[:, 0:n], ALU.mult, ALU.mult),
                    l2_shift, j + 1)

            def fill_block(d, b):
                dve.wait_ge(e_a_in, d.count(b, 16, 16))
                run(V.scalar_tensor_tensor(d_on, d_adj, 0.0, d_adj, ALU.is_equal, ALU.add), e_a_read, d.count(b, 1, 1))

            def recip_block(d, b):
                run(V.reciprocal(d_pen, d_on), e_inverted, d.count(b, 1, 1))

            def weight_block(d, b):
                dve.wait_ge(e_exped, d.count(b, 1, 1))
                reached(dve, e_turned, d.count(b, 1, 0))
                after()
                run(V.scalar_tensor_tensor(d_w, d_on, 1.0, d_e, ALU.is_lt, ALU.mult), e_weight, d.count(b, 1, 1))

            def add_block(d, b):
                dve.wait_ge(e_weighed, d.count(b, 1, 1))
                after()
                run(V.tensor_tensor(d_out[:], d_out[:], b_sum[:, 0:D], ALU.add), e_added, d.count(b, 1, 1))

            def finish_block(d):
                after()
                base = d.turns
                do(base, FINISH_2, "stats", lambda: V.bn_stats(stats[:], d_out[:]))
                aggregate(base, FINISH_2)
                newton_steps(base, FINISH_2)
                do(base, FINISH_2, "out", lambda: V.tensor_scalar(d_msg[:], d_out[:], mv[:, 0:1], rstd[:], ALU.subtract, ALU.mult))

            def body2(j, tiles):
                def seq(*steps):
                    for step_, of in steps:
                        after(2)
                        step_(first_tile_2, j) if of is None else step_(of)

                a, b, c = tiles[0:3]
                seq((add2, a), (fill_block, None), (stats2, a))
                after()
                aggregate2(a)
                recip_block(first_tile_2, j)
                seq((add2, b), (add2, c), (stats2, b), (stats2, c), (aggregate2, b))
                if len(tiles) > 3:
                    seq((add2, tiles[3]), (aggregate2, c))
                    after()
                    stats2(tiles[3])
                    after()
                    aggregate2(tiles[3])
                else:
                    after()
                    aggregate2(c)
                weight_block(first_tile_2, j)
                norm_round(j, tiles)
                for t in tiles:
                    if t.after(PER_ROUND):
                        members(t.after(PER_ROUND))
                add_block(first_tile_2, j)

            run(V.tensor_copy(d_out[:], z[:, TILES, :]))
            after()
            for n in range(PER_ROUND):
                members(Tile(None, n))
            rounds(body2, lambda count: counted_loop(count, 4 * PER_ROUND + 4,
                                                     last=lambda r: (e_added, first_tile_2.count(r, 1, 1))))
            finish_block(first_tile_2)

            def dense2(d):
                reached(dve, turn, d.turns)
                run(V.tensor_copy(d_out[:], z[:, d.z_index, :]))

                def block(b):
                    after()
                    fill_block(d, b)
                    after()
                    recip_block(d, b)
                    weight_block(d, b)
                    add_block(d, b)

                block(0)
                with counted_loop(DENSE_BLOCKS - 1, 0, last=lambda b: (e_added, d.count(b, 1, 1))) as b:
                    block(b + 1)
                finish_block(d)

            flagged_counted(lambda t: dense2(tile_2(t)), 1,
                            [(e_inverted, DENSE_BLOCKS), (e_a_read, DENSE_BLOCKS), (e_weight, DENSE_BLOCKS), (e_added, DENSE_BLOCKS)])

        return


_INS = ["x", "adj", "L0_gnn_Wqkv", "L0_gnn_bqkv", "L0_gnn_Wout", "L0_gnn_bout", "L0_gnn_graph_bias", "L1_gnn_W", "L1_gnn_B"]
_OUTS = [((N, D), "float32")]


def kernel(**inputs):
    import numpy as _np
    import concourse.bacc as _bacc
    from concourse import mybir as _mybir
    from concourse.bass_utils import run_bass_kernel_spmd as _run

    nc = _bacc.Bacc("TRN2", target_bir_lowering=False, num_devices=1)
    arrays, args = {}, []
    for name in _INS:
        a = _np.ascontiguousarray(inputs[name])
        arrays[f"in_{name}_dram"] = a
        args.append(nc.dram_tensor(f"in_{name}_dram", a.shape, _mybir.dt.from_np(a.dtype), kind="ExternalInput").ap())
    for i, (shape, dtype) in enumerate(_OUTS):
        dt = _mybir.dt.from_np(_np.dtype(dtype))
        args.append(nc.dram_tensor(f"out_{i}_dram", shape, dt, kind="ExternalOutput").ap())
    build(nc, *args)
    r = _run(nc, [arrays], core_ids=[0])
    return r.results[0]["out_0_dram"]
```
